# Optimizing a Trainium2 kernel written in Bass

```python
import numpy as np
import jax
import jax.numpy as jnp

def _softmax(x, axis=-1):
    return jax.nn.softmax(x, axis=axis)

def _gelu(x):
    return jax.nn.gelu(x, approximate=True)

def _silu(x):
    return jax.nn.silu(x)

def _sigmoid(x):
    return jax.nn.sigmoid(x)

def _layernorm(x, axis=-1, eps=1e-05):
    m = jnp.mean(x, axis=axis, keepdims=True)
    v = jnp.var(x, axis=axis, keepdims=True)
    return (x - m) / jnp.sqrt(v + eps)

def _scatter_add(tgt, idx, src, axis=0):
    return tgt.at[idx].add(src)

def _segment_sum(src, seg, n):
    return jax.ops.segment_sum(src, seg, n)
kernel_name = 'mk_gnn_preln_d2_gnn_r8_7b1fc5'

def setup_inputs(seed: int=0):
    np.random.seed(seed)
    _w = jnp.asarray

    def _rec_inputs():
        import jax
        import jax.numpy as jnp
        _gk = jax.random.key(seed)
        x = -0.0001006 + 1 * jax.random.normal(jax.random.fold_in(_gk, 1), (6250, 96), jnp.float32)
        _s = jax.random.randint(jax.random.fold_in(_gk, 2), (100000,), 0, 6250, jnp.int32)
        _d = jax.random.randint(jax.random.fold_in(_gk, 3), (100000,), 0, 6250, jnp.int32)
        _loop = jnp.arange(6250, dtype=jnp.int32)
        src = jnp.concatenate([_s, _d, _loop])
        dst = jnp.concatenate([_d, _s, _loop])
        _o = jnp.argsort(dst, stable=True)
        src = src[_o]
        dst = dst[_o]
        edge_attr_96 = -4.21973e-05 + 0.999841 * jax.random.normal(jax.random.fold_in(_gk, 12), (206250, 96), jnp.float32)
        return (x, src, dst, edge_attr_96)
    x, src, dst, edge_attr_96 = _rec_inputs()

    def _L0_gnn_setup():
        import jax, jax.numpy as jnp
        import numpy as np
        N_NODES = 6250
        N_EDGES = 100000
        EMB = 96
        HID = 2 * EMB
        key = jax.random.key(seed)
        ks = jax.random.split(key, 8)
        h = jax.random.normal(ks[0], (N_NODES, EMB), dtype=jnp.float32)
        edge_attr = jax.random.normal(ks[1], (N_EDGES, EMB), dtype=jnp.float32)
        src = jax.random.randint(ks[2], (N_EDGES,), 0, N_NODES, dtype=jnp.int32)
        dst = jax.random.randint(ks[3], (N_EDGES,), 0, N_NODES, dtype=jnp.int32)
        W1 = jax.random.normal(ks[4], (EMB, HID), dtype=jnp.float32) * (1.0 / np.sqrt(EMB))
        b1 = jnp.zeros((HID,), dtype=jnp.float32)
        W2 = jax.random.normal(ks[5], (HID, EMB), dtype=jnp.float32) * (1.0 / np.sqrt(HID))
        b2 = jnp.zeros((EMB,), dtype=jnp.float32)
        eps = jnp.zeros((1,), dtype=jnp.float32)
        return {'h': h, 'edge_attr': edge_attr, 'src': src, 'dst': dst, 'W1': W1, 'b1': b1, 'W2': W2, 'b2': b2, 'eps': eps}
    _L0_gnn_all = _L0_gnn_setup()
    _L0_gnn_in = {k: v for k, v in _L0_gnn_all.items() if k in ('W1', 'b1', 'W2', 'b2', 'eps')}
    del _L0_gnn_all

    def _L1_gnn_setup():
        import jax, jax.numpy as jnp
        import numpy as np
        N_NODES = 6250
        N_EDGES = 100000
        D_MODEL = 96
        HEADS = 4
        key = jax.random.key(seed)
        ks = jax.random.split(key, 6)
        scale = 1.0 / np.sqrt(D_MODEL)
        return {'embeds': jax.random.normal(ks[0], (N_NODES, D_MODEL), dtype=jnp.float32), 'qW': jax.random.normal(ks[1], (D_MODEL, D_MODEL), dtype=jnp.float32) * scale, 'kW': jax.random.normal(ks[2], (D_MODEL, D_MODEL), dtype=jnp.float32) * scale, 'vW': jax.random.normal(ks[3], (D_MODEL, D_MODEL), dtype=jnp.float32) * scale, 'rows': jax.random.randint(ks[4], (N_EDGES,), 0, N_NODES, dtype=jnp.int32), 'cols': jax.random.randint(ks[5], (N_EDGES,), 0, N_NODES, dtype=jnp.int32)}
    _L1_gnn_all = _L1_gnn_setup()
    _L1_gnn_in = {k: v for k, v in _L1_gnn_all.items() if k in ('qW', 'kW', 'vW')}
    del _L1_gnn_all
    return {'x': x, 'src': src, 'dst': dst, 'edge_attr_96': edge_attr_96, 'L0_gnn_W1': _L0_gnn_in['W1'], 'L0_gnn_b1': _L0_gnn_in['b1'], 'L0_gnn_W2': _L0_gnn_in['W2'], 'L0_gnn_b2': _L0_gnn_in['b2'], 'L0_gnn_eps': _L0_gnn_in['eps'], 'L1_gnn_qW': _L1_gnn_in['qW'], 'L1_gnn_kW': _L1_gnn_in['kW'], 'L1_gnn_vW': _L1_gnn_in['vW']}

def reference(x, src, dst, edge_attr_96, L0_gnn_W1, L0_gnn_b1, L0_gnn_W2, L0_gnn_b2, L0_gnn_eps, L1_gnn_qW, L1_gnn_kW, L1_gnn_vW):
    import jax
    import jax.numpy as jnp

    def _L0_gnn_ref(h, edge_attr, src, dst, W1, b1, W2, b2, eps):
        import jax, jax.numpy as jnp
        import numpy as np
        N_NODES = 6250
        N_EDGES = 100000
        EMB = 96
        HID = 2 * EMB
        m = h[src] + edge_attr
        aggr = jax.ops.segment_sum(m, dst, num_segments=N_NODES)
        hidden = jax.nn.relu(aggr @ W1 + b1)
        mlp_out = hidden @ W2 + b2
        out = (1.0 + eps[0]) * h + mlp_out
        return out

    def _L1_gnn_ref(embeds, qW, kW, vW, rows, cols):
        import jax, jax.numpy as jnp
        import numpy as np
        N_NODES = 6250
        N_EDGES = 100000
        D_MODEL = 96
        HEADS = 4
        nvar, d = embeds.shape
        dh = d // HEADS
        e = rows.shape[0]
        q = (embeds[rows] @ qW).reshape(e, HEADS, dh)
        k = (embeds[cols] @ kW).reshape(e, HEADS, dh)
        v = (embeds[cols] @ vW).reshape(e, HEADS, dh)
        scores = jnp.clip(jnp.einsum('ehd,ehd->eh', q, k), -10.0, 10.0)
        exp_s = jnp.exp(scores)
        norms = jax.ops.segment_sum(exp_s, rows, num_segments=nvar)[rows]
        w = exp_s / (norms + 1e-08)
        res = jax.ops.segment_sum(w[:, :, None] * v, rows, num_segments=nvar).reshape(nvar, d)
        return embeds + res
    h = jnp.maximum(_layernorm(x, axis=-1), 0.0)
    x = x + _L0_gnn_ref(h, edge_attr_96, src, dst, L0_gnn_W1, L0_gnn_b1, L0_gnn_W2, L0_gnn_b2, L0_gnn_eps)
    h = jnp.maximum(_layernorm(x, axis=-1), 0.0)
    x = x + _L1_gnn_ref(h, L1_gnn_qW, L1_gnn_kW, L1_gnn_vW, src, dst)
    return x

_drawn_inputs = setup_inputs


def setup_inputs(seed=0):
    import zlib

    import numpy as np

    out = dict(_drawn_inputs(seed))
    spreads = {'L0_gnn_b1': (0.0, 0.8), 'L0_gnn_b2': (0.0, 0.8)}
    factors = {'L1_gnn_qW': 8.0, 'L1_gnn_kW': 8.0}
    for name, (base, spread) in spreads.items():
        noise = np.random.default_rng([zlib.crc32(name.encode()), seed]).standard_normal(out[name].shape)
        drawn = base * np.exp(spread * noise) if base else spread * noise
        out[name] = jnp.asarray(drawn.astype(out[name].dtype))
    for name, factor in factors.items():
        out[name] = (out[name] * factor).astype(out[name].dtype)
    return out
```

```python
from contextlib import ExitStack

import numpy as np
import concourse.bass as bass
from concourse import mybir
from concourse.alu_op_type import AluOpType as ALU

F32 = mybir.dt.float32
F16 = mybir.dt.float16
BF16 = mybir.dt.bfloat16
I32 = mybir.dt.int32
ACT = mybir.ActivationFunctionType
AX = mybir.AxisListType

P = 128
N = 6250
D = 96
HID = 192
HEADS, DH = 4, 24
E = 206250
NT = -(-N // P)
NP = NT * P
TAIL = N - (NT - 1) * P
EP, EC = 110, 1875
G = 16
NG = NP // G
GPB = P // G
K = 5
WIN = K * P
CODE = G * NT
GP = 98
GQ = NG // GP
SC = 7
NS = NT // SC
CW = 448
NC_ = NP // CW
CT = CW // 4
KR = 3 * DH
LN_EPS = 1e-5
CLIP = 10.0
EXP_HI = float(np.exp(10.0))
EXP_LO = float(np.exp(-10.0))
GTILES = E // P
GREST = E - GTILES * P
K_PART = [[0, 0, 1], [1, 0, 2]]
Q_PART = [[0, 1, 0], [1, 2, 0]]


def build(nc, x, src, dst, attr, W1, b1, W2, b2, eps, qW, kW, vW, out):
    ctx = ExitStack()
    with ctx:
        def dram(name, shape, dt):
            return nc.dram_tensor(name, shape, dt).ap()

        count_d = dram("count_d", [(NP + 1) * NP, 1], F32)
        h_d = dram("h_d", [NP, D], F32)
        xp_d = dram("xp_d", [NP, D], F32)
        aggr_d = dram("aggr_d", [NP + P, D], F32)
        aggrT_d = dram("aggrT_d", [D, NP], F32)
        start_d = dram("start_d", [1, NG + 1], F32)
        rec_d = dram("rec_d", [E, 4], F32)
        xh_d = dram("xh_d", [NP, D], F32)
        kp_d = dram("kp_d", [NT, KR, HEADS, 2, P], BF16)
        qp_d = dram("qp_d", [NC_, KR, HEADS, 2, CW], BF16)
        v_d = dram("v_d", [NT, P, P], F32)

        flag_i = ctx.enter_context(nc.sbuf_tensor("flag_i", [1, 1], I32))
        start_i = ctx.enter_context(nc.sbuf_tensor("start_i", [1, NG], I32))
        ident = ctx.enter_context(nc.sbuf_tensor("ident", [P, P], F32))
        ones = ctx.enter_context(nc.sbuf_tensor("ones", [P, P], F32))

        ids_and_norm(nc, x, src, dst, xp_d, h_d, start_d, rec_d, aggr_d, flag_i, start_i, ident, ones)
        edges(nc, src, dst, attr, h_d, aggr_d, aggrT_d, rec_d, count_d, flag_i, start_i, ident, ones)
        nodes(nc, xp_d, W1, b1, W2, b2, eps, qW, kW, vW, h_d, aggrT_d, xh_d, kp_d, qp_d, v_d, ident, ones)
        attention(nc, count_d, xh_d, kp_d, qp_d, v_d, ident, out)


def tools(nc, ctx):
    def sb(name, shape, dt):
        return ctx.enter_context(nc.sbuf_tensor(name, shape, dt))

    def ps(name, shape, dt=F32):
        return ctx.enter_context(nc.psum_tensor(name, shape, dt))

    def sem(name):
        return ctx.enter_context(nc.semaphore(name))

    return sb, ps, sem


def linker(eng, done):
    n = [0]

    def link(ins):
        n[0] += 1
        ins.then_inc(done, 1)
        eng.wait_ge(done, n[0])

    return link


def ids_and_norm(nc, x, src, dst, xp_d, h_d, start_d, rec_d, aggr_d, flag_i, start_i, ident, ones):
    ctx = ExitStack()
    with ctx:
        sb, ps, sem = tools(nc, ctx)
        xn = sb("xn", [P, NT, D], F32)
        sq = sb("sq", [P, NT, D], F32)
        mean = sb("mean", [P, NT], F32)
        rstd = sb("rstd", [P, NT], F32)
        srct = sb("srct", [EP, EC], I32)
        dstt = sb("dstt", [EP, EC], I32)
        part = sb("part", [EP, EC], I32)
        rec = sb("rec", [EP, EC, 4], F32)
        nexti = sb("nexti", [EP, 1], I32)
        nextf = sb("nextf", [EP, 1], F32)
        lasti = sb("lasti", [1, EP], I32)
        lastf = sb("lastf", [1, EP], F32)
        bad = sb("bad", [EP, 2], F32)
        lastb = sb("lastb", [GP, EP], F32)
        less = sb("less", [GP, EC], F32)
        row = sb("row", [GP, GQ, EC], I32)
        thr_i = sb("thr_i", [GP, GQ], I32)
        thr = sb("thr", [GP, GQ], F32)
        cnt = sb("cnt", [GP, GQ], F32)
        at = sb("at", [GP, GQ], F32)
        at_i = sb("at_i", [GP, GQ], I32)
        start = sb("start", [GP, GQ], F32)
        srow = sb("srow", [1, NG + 1], F32)
        diff = sb("diff", [1, NG], F32)
        fl = sb("fl", [1, 4], F32)
        lastp = ps("lastp", [GP, EP])
        badp = ps("badp", [1, 2])
        x_out = sem("x_out")
        x_in, ids_in, small_in, bnd_in = sem("x_in"), sem("ids_in"), sem("small_in"), sem("bnd_in")
        memset_done, consts, pool_done = sem("memset_done"), sem("consts"), sem("pool_done")
        dve_done, sqrt_in, sqrt_out = sem("dve_done"), sem("sqrt_in"), sem("sqrt_out")
        lastf_ready, lastp_ready = sem("lastf_ready"), sem("lastp_ready")
        bad_ready, badp_ready = sem("bad_ready"), sem("badp_ready")
        at_ready, rows_in = sem("at_ready"), sem("rows_in")
        start_ready, start_out, srow_in = sem("start_ready"), sem("start_out"), sem("srow_in")
        h_ready, rec_ready, h_out, rec_out = sem("h_ready"), sem("rec_ready"), sem("h_out"), sem("rec_out")
        block = ctx.enter_context(nc.Block())

        @block.sync
        def _(sp):
            sp.dma_start(dstt[:], dst.rearrange("(p c) -> p c", c=EC)).then_inc(ids_in, 16)
            sp.dma_start(srct[:], src.rearrange("(p c) -> p c", c=EC)).then_inc(ids_in, 16)
            d2 = dst.rearrange("(p c) -> p c", c=EC)
            with nc.allow_non_contiguous_dma(reason="110 ids"):
                sp.dma_start(nexti[0:EP - 1, :], d2[1:EP, 0:1]).then_inc(small_in, 16)
            with nc.allow_non_contiguous_dma(reason="110 ids"):
                sp.dma_start(lasti[:, :], d2[:, EC - 1:EC].rearrange("p c -> c p")).then_inc(bnd_in, 16)
            sp.wait_ge(start_ready, 1)
            for q in range(GQ):
                with nc.allow_non_contiguous_dma(reason="98 numbers"):
                    sp.dma_start(start_d[0:1, q * GP:(q + 1) * GP].rearrange("a p -> p a"),
                                 start[:, q:q + 1]).then_inc(start_out, 16)
            sp.wait_ge(start_out, 16 * GQ)
            sp.dma_start(srow[:, 0:NG], start_d[:, 0:NG]).then_inc(srow_in, 16)
            sp.wait_ge(rec_ready, 1)
            sp.dma_start(rec_d.rearrange("(p c) k -> p c k", c=EC), rec[:, :, :]).then_inc(rec_out, 16)
            sp.wait_ge(rec_out, 16)

        @block.scalar
        def _(act):
            act.wait_ge(memset_done, 1)
            act.dma_start(xn[:, 0:NT - 1, :],
                          x[0:(NT - 1) * P, :].rearrange("(t p) f -> p t f", p=P)).then_inc(x_in, 16)
            act.dma_start(xn[0:TAIL, NT - 1, :], x[(NT - 1) * P:N, :]).then_inc(x_in, 16)
            act.wait_ge(x_in, 32)
            act.dma_start(xp_d.rearrange("(t p) f -> p t f", p=P), xn[:, :, :]).then_inc(x_out, 16)
            act.wait_ge(sqrt_in, 1)
            act.activation(rstd[:, :], rstd[:, :], ACT.Sqrt).then_inc(sqrt_out, 1)
            act.wait_ge(h_ready, 1)
            act.dma_start(h_d.rearrange("(t p) f -> p t f", p=P), xn[:, :, :]).then_inc(h_out, 16)
            act.wait_ge(h_out, 16)

        @block.gpsimd
        def _(pool):
            pool.memset(ident[:], 0.0).then_inc(pool_done, 1)
            pool.memset(ones[:], 1.0).then_inc(consts, 1)
            pool.iota(thr_i[:], pattern=[[GP * G, GQ]], base=0, channel_multiplier=G).then_inc(consts, 1)
            pool.wait_ge(pool_done, 1)
            pool.affine_select(out=ident[:], in_=ident[:], compare_op=ALU.not_equal, fill=1.0, base=0,
                               pattern=[[-1, P]], channel_multiplier=1).then_inc(consts, 1)
            pool.wait_ge(at_ready, 1)
            for q in range(GQ):
                pool.indirect_dma_start(
                    out=row[:, q, :], out_offset=None, in_=dst.rearrange("(p c) -> p c", c=EC),
                    in_offset=bass.IndirectOffsetOnAxis(ap=at_i[:, q:q + 1], axis=0),
                ).then_inc(rows_in, 16)
            pool.wait_ge(rows_in, 16 * GQ)

        @block.tensor
        def _(pe):
            pe.wait_ge(consts, 3)
            pe.wait_ge(lastf_ready, 1)
            pe.matmul(lastp[:, :], ones[0:1, 0:GP], lastf[:, :], start=True, stop=True).then_inc(lastp_ready, 1)
            pe.wait_ge(bad_ready, 1)
            pe.matmul(badp[:, 0:1], ones[0:EP, 0:1], bad[:, 0:1], start=True, stop=True).then_inc(badp_ready, 1)

        @block.vector
        def _(dve):
            link = linker(dve, dve_done)
            dve.memset(xn[:, NT - 1, :], 0.0).then_inc(memset_done, 1)
            dve.memset(nextf[:, :], float(NP))
            link(dve.memset(srow[:, NG:NG + 1], float(E)))
            dve.wait_ge(consts, 3)
            link(dve.tensor_copy(thr[:, :], thr_i[:, :]))
            dve.wait_ge(bnd_in, 16)
            dve.tensor_copy(lastf[:, :], lasti[:, :]).then_inc(lastf_ready, 1)
            dve.wait_ge(lastp_ready, 1)
            link(dve.tensor_copy(lastb[:, :], lastp[:, :]))
            for q in range(GQ):
                link(dve.tensor_scalar(less[:, 0:EP], lastb[:, :], thr[:, q:q + 1], None, ALU.is_lt))
                link(dve.tensor_reduce(at[:, q:q + 1], less[:, 0:EP], axis=AX.X, op=ALU.add))
            link(dve.tensor_scalar(at[:, :], at[:, :], float(EP - 1), None, ALU.min))
            dve.tensor_copy(at_i[:, :], at[:, :]).then_inc(at_ready, 1)
            dve.wait_ge(ids_in, 32)
            link(dve.tensor_copy(rec[:, :, 1], dstt[:, :]))
            link(dve.tensor_scalar(part[:, :], srct[:, :], 7, None, ALU.logical_shift_right))
            link(dve.scalar_tensor_tensor(out=rec[:, :, 0], in0=rec[:, :, 1], scalar=float(NT), in1=part[:, :],
                                          op0=ALU.mult, op1=ALU.add))
            link(dve.tensor_scalar(part[:, :], srct[:, :], P - 1, None, ALU.bitwise_and))
            link(dve.tensor_copy(rec[:, :, 3], part[:, :]))
            link(dve.tensor_copy(rec[:, :, 2], srct[:, :]))
            dve.tensor_copy(bad[:, 1:2], rec[:, 0, 3:4]).then_inc(rec_ready, 1)
            dve.wait_ge(small_in, 16)
            link(dve.tensor_copy(nextf[0:EP - 1, :], nexti[0:EP - 1, :]))
            lt = sq[0:EP, :, :].rearrange("p a b -> p (a b)")[:, 0:EC]
            link(dve.tensor_tensor(lt[:, 0:EC - 1], rec[:, 0:EC - 1, 1], rec[:, 1:EC, 1], ALU.is_gt))
            link(dve.tensor_tensor(lt[:, EC - 1:EC], rec[:, EC - 1, 1:2], nextf[:, :], ALU.is_gt))
            dve.tensor_reduce(bad[:, 0:1], lt, axis=AX.X, op=ALU.add).then_inc(bad_ready, 1)
            dve.wait_ge(rows_in, 16 * GQ)
            for q in range(GQ):
                link(dve.tensor_scalar(less[:, :], row[:, q, :], thr[:, q:q + 1], None, ALU.is_lt))
                link(dve.tensor_reduce(cnt[:, q:q + 1], less[:, :], axis=AX.X, op=ALU.add))
            dve.scalar_tensor_tensor(out=start[:, :], in0=at[:, :], scalar=float(EC), in1=cnt[:, :],
                                     op0=ALU.mult, op1=ALU.add).then_inc(start_ready, 1)
            dve.wait_ge(srow_in, 16)
            link(dve.tensor_tensor(diff[:, :], srow[:, 1:NG + 1], srow[:, 0:NG], ALU.subtract))
            link(dve.tensor_reduce(fl[:, 0:1], diff[:, :], axis=AX.X, op=ALU.max))
            link(dve.tensor_scalar(fl[:, 1:2], fl[:, 0:1], float(WIN), None, ALU.is_le))
            dve.wait_ge(badp_ready, 1)
            link(dve.tensor_scalar(fl[:, 2:3], badp[:, 0:1], 0.0, None, ALU.is_equal))
            link(dve.tensor_tensor(fl[:, 3:4], fl[:, 1:2], fl[:, 2:3], ALU.mult))
            link(dve.tensor_copy(flag_i[:, :], fl[:, 3:4]))
            link(dve.tensor_scalar(srow[:, :], srow[:, :], float(E - WIN), None, ALU.min))
            link(dve.tensor_copy(start_i[:, :], srow[:, 0:NG]))
            dve.wait_ge(x_in, 32)
            link(dve.tensor_reduce(mean[:, :], xn[:, :, :], axis=AX.X, op=ALU.add))
            dve.wait_ge(x_out, 16)
            link(dve.tensor_scalar(mean[:, :], mean[:, :], 1.0 / D, None, ALU.mult))
            link(dve.tensor_tensor(xn[:, :, :], xn[:, :, :], mean[:, :].unsqueeze(2).to_broadcast([P, NT, D]),
                                   ALU.subtract))
            link(dve.tensor_tensor(sq[:, :, :], xn[:, :, :], xn[:, :, :], ALU.mult))
            link(dve.tensor_reduce(rstd[:, :], sq[:, :, :], axis=AX.X, op=ALU.add))
            dve.tensor_scalar(rstd[:, :], rstd[:, :], 1.0 / D, LN_EPS, ALU.mult, ALU.add).then_inc(sqrt_in, 1)
            dve.wait_ge(sqrt_out, 1)
            link(dve.reciprocal(rstd[:, :], rstd[:, :]))
            link(dve.tensor_tensor(xn[:, :, :], xn[:, :, :], rstd[:, :].unsqueeze(2).to_broadcast([P, NT, D]),
                                   ALU.mult))
            dve.tensor_scalar(xn[:, :, :], xn[:, :, :], 0.0, None, ALU.max).then_inc(h_ready, 1)


def edges(nc, src, dst, attr, h_d, aggr_d, aggrT_d, rec_d, count_d, flag_i, start_i, ident, ones):
    count_rows = count_d[0:NP * NP, :].rearrange("(r c) o -> r (c o)", c=NP)
    ctx = ExitStack()
    with ctx:
        sb, ps, sem = tools(nc, ctx)
        hf = sb("hf", [P, NT, D], F32)
        hpart = sb("hpart", [P, 3, NT, D], F16)
        slab = sb("slab", [P, 2, NT, P], F16)
        rowsT = sb("rowsT", [P, 2, NP], F32)
        aggrT = sb("aggrT", [D, 2, P], F32)
        attr_w = sb("attr_w", [P, 4, K, D], F32)
        rec_w = sb("rec_w", [P, 4, K, 4], F32)
        rel = sb("rel", [P, 4, K, 2], F32)
        base_i = sb("base_i", [P, NG, 2], I32)
        base = sb("base", [P, NG, 2], F32)
        iota_i = sb("iota_i", [P, CODE], I32)
        iota = sb("iota", [P, CODE], F16)
        iota_g = sb("iota_g", [P, G], F32)
        code_oh = sb("code_oh", [P, 2, K, CODE], F16)
        lane_oh = sb("lane_oh", [P, 2, K, P], F16)
        dst_oh = sb("dst_oh", [P, 2, K, G], F32)
        ident16 = sb("ident16", [P, P], F16)
        lane_i = sb("lane_i", [P, 1], I32)
        lane = sb("lane", [P, 1], F32)
        g_rec = sb("g_rec", [P, 4], F32)
        g_src = sb("g_src", [P, 1], I32)
        g_attr = sb("g_attr", [P, D], F32)
        g_h = sb("g_h", [P, D], F32)
        g_rest = sb("g_rest", [P, 2], F32)
        g_keys = sb("g_keys", [P, 2, P], F32)
        g_eq = sb("g_eq", [P, 3, P], F32)
        g_low = sb("g_low", [P, P], F32)
        g_first = sb("g_first", [P, 2, P], F32)
        g_dup = sb("g_dup", [P, 2], F32)
        g_cnt = sb("g_cnt", [P, 1], F32)
        g_tmp = sb("g_tmp", [P, 4], F32)
        g_idx = sb("g_idx", [P, 4], I32)
        g_sum = sb("g_sum", [P, D], F32)
        carrier = sb("carrier", [P, 4], F32)
        grp = ps("grp", [P, 2, 2, 512])
        acc = ps("acc", [P, 2, 512])
        tp = ps("tp", [P, 2, 512])
        h_in, base_ready, set_done, consts = sem("h_in"), sem("base_ready"), sem("set_done"), sem("consts2")
        win_in = [sem(f"win_in{s}") for s in range(4)]
        rel_ready, oh_ready, group_done, slab_part = sem("rel_ready"), sem("oh_ready"), sem("group_done"), sem("slab_part")
        tp_ready, tp_used, rows_ready = sem("tp_ready"), sem("tp_used"), sem("rows_ready")
        rows_out = [sem("rows_out0"), sem("rows_out1")]
        g_zero_out, g_in, g_dve, g_pe, g_idx_ready = sem("g_zero_out"), sem("g_in"), sem("g_dve"), sem("g_pe"), sem("g_idx_ready")
        g_h_in, g_keys_in, g_keysT, g_m_ready, g_summed = sem("g_h_in"), sem("g_keys_in"), sem("g_keysT"), sem("g_m_ready"), sem("g_summed")
        g_padded, g_out, g_zeroed, g_low_ready = sem("g_padded"), sem("g_out"), sem("g_zeroed"), sem("g_low_ready")
        g_carrier = sem("g_carrier")
        f_in, f_T, f_sb, f_out = sem("f_in"), sem("f_T"), sem("f_sb"), sem("f_out")
        block = ctx.enter_context(nc.Block())

        SLICES = [range(13 * gi // 8, 13 * (gi + 1) // 8) for gi in range(GPB)]

        def tiles_of(batch):
            return range(4 * batch, min(4 * batch + 4, NT))

        def all_blocks(eng, body, last_stage):
            body(0, 0, False)
            with eng.Fori(0, (NT - 1) // 2) as i:
                body(2 * i + 1, 1, True)
                body(2 * i + 2, 0, True)
            last_stage(NT - 1)

        @block.sync
        def _(sp):
            fast = sp.value_load(flag_i[0:1, 0:1], min_val=0, max_val=1)
            with sp.If(fast == 1):
                def windows(b, par, has_stage):
                    for gi in range(GPB):
                        g, slot = b * GPB + gi, gi % 4
                        first = sp.value_load(start_i[0:1, bass.ds(g, 1)], min_val=0, max_val=E - WIN)
                        sp.wait_ge(group_done, g + 1)
                        sp.dma_start(rec_w[:, slot, :, :].rearrange("p k c -> p (k c)"),
                                     rec_d[bass.ds(first, WIN), :].rearrange("(p k) c -> p (k c)", k=K)
                                     ).then_inc(win_in[slot], 16)
                        sp.dma_start(attr_w[:, slot, :, :].rearrange("p k c -> p (k c)"),
                                     attr[bass.ds(first, WIN), :].rearrange("(p k) c -> p (k c)", k=K)
                                     ).then_inc(win_in[slot], 16)
                all_blocks(sp, windows, lambda b: None)
            with sp.Else():
                sp.wait_ge(g_zeroed, 1)
                with sp.Fori(0, NT) as j:
                    sp.dma_start(count_rows[bass.ds(j * P, P), :], rowsT[:, 0, :]).then_inc(g_zero_out, 16)
                    sp.dma_start(aggr_d[bass.ds(j * P, P), :], rowsT[:, 0, 0:D]).then_inc(g_zero_out, 16)
                sp.dma_start(count_d[NP * NP:NP * NP + NP, :].rearrange("(p c) o -> p (c o)", c=NT),
                             rowsT[:, 0, 0:NT]).then_inc(g_zero_out, 16)
                sp.dma_start(aggr_d[NP:NP + P, :], rowsT[:, 0, 0:D]).then_inc(g_zero_out, 16)
                sp.wait_ge(g_zero_out, 16 * (2 * NT + 2))

                def load(t, rows, at):
                    sp.wait_ge(g_out, t * 32)
                    sp.dma_start(g_rec[0:rows, :], rec_d[bass.ds(at, rows), :]).then_inc(g_in, 16)
                    sp.dma_start(g_attr[0:rows, :], attr[bass.ds(at, rows), :]).then_inc(g_in, 16)
                with sp.Fori(0, GTILES) as t:
                    load(t, P, t * P)
                sp.wait_ge(g_out, GTILES * 32)
                sp.wait_ge(g_padded, 1)
                sp.dma_start(g_rec[0:GREST, :], rec_d[GTILES * P:E, :]).then_inc(g_in, 16)
                sp.dma_start(g_attr[0:GREST, :], attr[GTILES * P:E, :]).then_inc(g_in, 16)
                sp.wait_ge(g_out, (GTILES + 1) * 32)
                with sp.Fori(0, NT) as j:
                    first, stored = sp.snap(j * P), sp.snap(j * 16)
                    sp.wait_ge(f_out, stored)
                    sp.dma_start(g_attr[:, :], aggr_d[bass.ds(first, P), :]).then_inc(f_in, 16)
                sp.wait_ge(f_out, NT * 16)

        @block.gpsimd
        def _(pool):
            fast = pool.value_load(flag_i[0:1, 0:1], min_val=0, max_val=1)
            pool.iota(base_i[:, :, 0], pattern=[[CODE, NG]], base=0, channel_multiplier=0).then_inc(base_ready, 1)
            pool.iota(base_i[:, :, 1], pattern=[[G, NG]], base=0, channel_multiplier=0).then_inc(base_ready, 1)
            pool.iota(iota_i[:, :], pattern=[[1, CODE]], base=0, channel_multiplier=0).then_inc(base_ready, 1)
            pool.iota(lane_i[:, :], pattern=[[0, 1]], base=0, channel_multiplier=1).then_inc(base_ready, 1)
            with pool.If(fast == 1):
                def store(b, par):
                    pool.wait_ge(rows_ready, b + 1)
                    pool.dma_start(count_rows[bass.ds(b * P, P), :], rowsT[:, par, :]).then_inc(rows_out[par], 16)
                    pool.dma_start(aggrT_d[:, bass.ds(b * P, P)], aggrT[:, par, :]).then_inc(rows_out[par], 16)
                with pool.Fori(0, (NT - 1) // 2) as i:
                    store(2 * i, 0)
                    store(2 * i + 1, 1)
                store(NT - 1, 0)
                pool.wait_ge(rows_out[0], 32 * ((NT + 1) // 2))
                pool.wait_ge(rows_out[1], 32 * ((NT - 1) // 2))
            with pool.Else():
                pool.wait_ge(g_low_ready, 1)
                pool.affine_select(out=g_low[:, :], in_=g_low[:, :], compare_op=ALU.is_gt, fill=0.0, base=0,
                                   pattern=[[-1, P]], channel_multiplier=1).then_inc(g_low_ready, 1)

                pool.memset(carrier[:, :], 0.0).then_inc(g_carrier, 1)
                pool.wait_ge(g_carrier, 1)

                def add(t):
                    pool.wait_ge(g_idx_ready, 2 * t + 1)
                    pool.tensor_tensor(carrier[:, 1:2], carrier[:, 0:1], carrier[:, 0:1], ALU.add)
                    pool.indirect_dma_start(out=g_h[:, :], out_offset=None, in_=h_d,
                                            in_offset=bass.IndirectOffsetOnAxis(ap=g_idx[:, 0:1], axis=0),
                                            ).then_inc(g_h_in, 16)
                    pool.wait_ge(g_idx_ready, 2 * t + 2)
                    pool.tensor_tensor(carrier[:, 2:3], carrier[:, 0:1], carrier[:, 0:1], ALU.add)
                    pool.indirect_dma_start(out=aggr_d, out_offset=bass.IndirectOffsetOnAxis(ap=g_idx[:, 1:2], axis=0),
                                            in_=g_sum[:, :], in_offset=None, compute_op=ALU.add).then_inc(g_out, 16)
                    pool.indirect_dma_start(out=count_d, out_offset=bass.IndirectOffsetOnAxis(ap=g_idx[:, 2:3], axis=0),
                                            in_=g_cnt[:, :], in_offset=None, compute_op=ALU.add).then_inc(g_out, 16)
                    pool.wait_ge(g_out, (t + 1) * 32)
                with pool.Fori(0, GTILES) as t:
                    add(t)
                add(GTILES)
                with pool.Fori(0, NT) as j:
                    pool.wait_ge(f_sb, j + 1)
                    pool.dma_start(aggrT_d[:, bass.ds(j * P, P)], aggrT[:, 0, :]).then_inc(f_out, 16)
                pool.wait_ge(f_out, NT * 16)

        @block.vector
        def _(dve):
            link = linker(dve, set_done)
            fast = dve.value_load(flag_i[0:1, 0:1], min_val=0, max_val=1)
            dve.wait_ge(base_ready, 4)
            dve.tensor_copy(base[:, :, :], base_i[:, :, :])
            dve.tensor_copy(iota[:, :], iota_i[:, :])
            dve.tensor_copy(iota_g[:, :], iota_i[:, 0:G])
            dve.tensor_copy(lane[:, :], lane_i[:, :])
            link(dve.tensor_copy(ident16[:, :], ident[:, :]))
            with dve.If(fast == 1):
                dve.wait_ge(h_in, 16)
                link(dve.tensor_copy(hpart[:, 0, :, :], hf[:, :, :]))
                link(dve.tensor_tensor(hf[:, :, :], hf[:, :, :], hpart[:, 0, :, :], ALU.subtract))
                link(dve.tensor_copy(hpart[:, 1, :, :], hf[:, :, :]))
                link(dve.tensor_tensor(hf[:, :, :], hf[:, :, :], hpart[:, 1, :, :], ALU.subtract))
                dve.tensor_copy(hpart[:, 2, :, :], hf[:, :, :]).then_inc(consts, 1)

                def one_hots(b, par, has_stage):
                    for gi in range(GPB):
                        g, slot, s = b * GPB + gi, gi % 4, gi % 2
                        dve.wait_ge(win_in[slot], 32 * (2 * b + gi // 4 + 1))
                        dve.wait_ge(group_done, g + 3)
                        dve.tensor_tensor(rel[:, slot, :, :], rec_w[:, slot, :, 0:2],
                                          base[:, bass.ds(g, 1), :].to_broadcast([P, K, 2]),
                                          ALU.subtract).then_inc(rel_ready, 1)
                        dve.wait_ge(rel_ready, g + 1)
                        for k in range(K):
                            dve.tensor_scalar(code_oh[:, s, k, :], iota[:, :], rel[:, slot, k, 0:1], None, ALU.is_equal)
                            dve.tensor_scalar(lane_oh[:, s, k, :], iota[:, 0:P], rec_w[:, slot, k, 3:4], None, ALU.is_equal)
                        dve.tensor_tensor(dst_oh[:, s, :, :], iota_g[:, :].unsqueeze(1).to_broadcast([P, K, G]),
                                          rel[:, slot, :, 1:2].to_broadcast([P, K, G]),
                                          ALU.is_equal).then_inc(oh_ready, 1)
                all_blocks(dve, one_hots, lambda b: None)
            with dve.Else():
                dve.memset(g_low[:, :], 1.0).then_inc(g_low_ready, 1)
                dve.memset(g_rec[:, :], 0.0)
                dve.memset(g_attr[:, :], 0.0)
                dve.memset(rowsT[:, 0, :], 0.0).then_inc(g_zeroed, 1)
                dve.wait_ge(g_zeroed, 1)
                dve.wait_ge(g_low_ready, 2)

                def work(t):
                    steps = [0]

                    def step(ins):
                        steps[0] += 1
                        ins.then_inc(g_dve, 1)
                        dve.wait_ge(g_dve, t * 19 + steps[0])
                    dve.wait_ge(g_in, (t + 1) * 32)
                    step(dve.tensor_copy(g_keys[:, 0, :], g_rec[:, 1:2].to_broadcast([P, P])))
                    dve.tensor_copy(g_keys[:, 1, :], g_rec[:, 2:3].to_broadcast([P, P])).then_inc(g_keys_in, 1)
                    dve.tensor_copy(g_idx[:, 0:1], g_rec[:, 2:3]).then_inc(g_idx_ready, 1)
                    dve.wait_ge(g_keysT, t + 1)
                    step(dve.tensor_scalar(g_eq[:, 0, :], grp[:, 0, 0, 0:P], g_rec[:, 1:2], None, ALU.is_equal))
                    step(dve.tensor_scalar(g_eq[:, 1, :], grp[:, 0, 0, P:2 * P], g_rec[:, 2:3], None, ALU.is_equal))
                    step(dve.tensor_tensor(g_eq[:, 2, :], g_eq[:, 0, :], g_eq[:, 1, :], ALU.mult))
                    step(dve.tensor_reduce(g_cnt[:, :], g_eq[:, 2, :], axis=AX.X, op=ALU.add))
                    step(dve.tensor_tensor(g_first[:, 0, :], g_eq[:, 0, :], g_low[:, :], ALU.mult))
                    step(dve.tensor_tensor(g_first[:, 1, :], g_eq[:, 2, :], g_low[:, :], ALU.mult))
                    step(dve.tensor_reduce(g_dup[:, :], g_first[:, :, :], axis=AX.X, op=ALU.max))
                    step(dve.tensor_scalar(g_tmp[:, 0:1], lane[:, :], float(NP), g_rec[:, 1:2], ALU.add, ALU.subtract))
                    step(dve.tensor_tensor(g_tmp[:, 1:2], g_tmp[:, 0:1], g_dup[:, 0:1], ALU.mult))
                    step(dve.tensor_tensor(g_idx[:, 1:2], g_tmp[:, 1:2], g_rec[:, 1:2], ALU.add))
                    step(dve.tensor_scalar(g_tmp[:, 0:1], g_rec[:, 0:1], -1.0, float(NP * NT), ALU.mult, ALU.add))
                    step(dve.scalar_tensor_tensor(out=g_idx[:, 2:3], in0=g_tmp[:, 0:1], scalar=g_dup[:, 1:2],
                                                  in1=g_rec[:, 0:1], op0=ALU.mult, op1=ALU.add))
                    step(dve.tensor_tensor(g_tmp[:, 2:3], lane[:, :], g_rec[:, 3:4], ALU.subtract))
                    step(dve.scalar_tensor_tensor(out=g_idx[:, 3:4], in0=g_tmp[:, 2:3], scalar=g_dup[:, 1:2],
                                                  in1=g_rec[:, 3:4], op0=ALU.mult, op1=ALU.add))
                    step(dve.tensor_scalar(g_idx[:, 2:3], g_idx[:, 2:3], 7, None, ALU.logical_shift_left))
                    step(dve.tensor_tensor(g_idx[:, 2:3], g_idx[:, 2:3], g_idx[:, 3:4], ALU.bitwise_or))
                    dve.wait_ge(g_h_in, (t + 1) * 16)
                    step(dve.tensor_tensor(g_attr[:, :], g_attr[:, :], g_h[:, :], ALU.add))
                    dve.nop().then_inc(g_m_ready, 1)
                    dve.wait_ge(g_summed, t + 1)
                    step(dve.tensor_copy(g_sum[:, :], acc[:, 0, 0:D]))
                    assert steps[0] == 19
                    dve.nop().then_inc(g_idx_ready, 1)

                def padding(t):
                    dve.wait_ge(g_out, t * 32)
                    dve.memset(g_attr[:, :], 0.0)
                    dve.memset(g_rec[:, 0:1], float(NP * NT - 1))
                    dve.memset(g_rec[:, 1:3], float(NP - 1))
                    dve.memset(g_rec[:, 3:4], float(P - 1)).then_inc(g_padded, 1)

                with dve.Fori(0, GTILES) as t:
                    work(t)
                padding(GTILES)
                work(GTILES)
                with dve.Fori(0, NT) as j:
                    dve.wait_ge(f_T, j + 1)
                    dve.wait_ge(f_out, j * 16)
                    dve.tensor_copy(aggrT[:, 0, :], acc[0:D, 0, 0:P]).then_inc(f_sb, 1)
                    dve.wait_ge(f_sb, j + 1)

        @block.scalar
        def _(act):
            fast = act.value_load(flag_i[0:1, 0:1], min_val=0, max_val=1)
            with act.If(fast == 1):
                act.nop().then_inc(tp_used, 2)
                act.dma_start(hf[:, :, :], h_d.rearrange("(t p) f -> p t f", p=P)).then_inc(h_in, 16)

                def rows(st, par, batch):
                    tiles = tiles_of(batch)
                    n = st * 13 + batch
                    act.wait_ge(tp_ready, n + 1)
                    act.activation(rowsT[:, par, 4 * batch * P:(4 * batch + len(tiles)) * P],
                                   tp[:, batch % 2 if par == 0 else (batch + 1) % 2, 0:len(tiles) * P],
                                   ACT.Copy).then_inc(tp_used, 1)

                def finish(st, par):
                    act.wait_ge(tp_ready, (st + 1) * 13)
                    act.activation(aggrT[:, par, :], acc[0:D, par, 0:P], ACT.Copy).then_inc(rows_ready, 1)

                def copies(b, par, has_stage):
                    for gi in range(GPB):
                        g, s = b * GPB + gi, gi % 2
                        act.wait_ge(group_done, g + 5)
                        act.activation(slab[:, par, :, gi * G:(gi + 1) * G].rearrange("p t (a d) -> p a d t", a=2),
                                       grp[:, s, :, 0:CODE // 2].rearrange("p a (d t) -> p a d t", t=NT),
                                       ACT.Copy).then_inc(slab_part, 1)
                        if has_stage:
                            if gi == 0:
                                act.wait_ge(rows_out[1 - par], 16 * (b - 1 - (1 - par)))
                            for batch in SLICES[gi]:
                                rows(b - 1, 1 - par, batch)
                    if has_stage:
                        finish(b - 1, 1 - par)

                def last(st):
                    act.wait_ge(rows_out[0], 32 * (st // 2))
                    for batch in range(13):
                        rows(st, 0, batch)
                    finish(st, 0)
                all_blocks(act, copies, last)
            with act.Else():
                act.nop()

        @block.tensor
        def _(pe):
            fast = pe.value_load(flag_i[0:1, 0:1], min_val=0, max_val=1)
            pe.wait_ge(set_done, 1)
            with pe.If(fast == 1):
                pe.nop().then_inc(group_done, 4)
                pe.wait_ge(consts, 1)

                def turn(st, par, batch):
                    n = st * 13 + batch
                    pe.wait_ge(tp_used, n + 1)
                    tiles = tiles_of(batch)
                    bank = batch % 2 if par == 0 else (batch + 1) % 2
                    for j, t in enumerate(tiles):
                        for part in range(3):
                            pe.matmul(acc[0:D, par, 0:P], hpart[:, part, t, :], slab[:, par, t, :],
                                      start=False, stop=(t == NT - 1 and part == 2), skip_group_check=True)
                        last = pe.matmul(tp[:, bank, j * P:(j + 1) * P], slab[:, par, t, :], ident16[:, :],
                                         start=True, stop=True)
                    last.then_inc(tp_ready, 1)

                def products(b, par, has_stage):
                    for gi in range(GPB):
                        g, slot, s = b * GPB + gi, gi % 4, gi % 2
                        pe.wait_ge(oh_ready, g + 1)
                        if gi >= 2 or has_stage:
                            pe.wait_ge(slab_part, g - 1)
                        if gi == 0 and has_stage:
                            pe.wait_ge(rows_ready, b - 1)
                        for k in range(K):
                            for half in range(2):
                                pe.matmul(grp[:, s, half, 0:CODE // 2], lane_oh[:, s, k, :],
                                          code_oh[:, s, k, half * (CODE // 2):(half + 1) * (CODE // 2)],
                                          start=(k == 0), stop=(k == K - 1))
                        for k in range(K):
                            last = pe.matmul(acc[0:D, par, gi * G:(gi + 1) * G], attr_w[:, slot, k, :],
                                             dst_oh[:, s, k, :], start=(gi == 0 and k == 0), stop=(k == K - 1),
                                             skip_group_check=True)
                        last.then_inc(group_done, 1)
                        if has_stage:
                            if gi == 0:
                                pe.wait_ge(slab_part, b * GPB)
                            for batch in SLICES[gi]:
                                turn(b - 1, 1 - par, batch)

                def last_stage(st):
                    pe.wait_ge(slab_part, NG)
                    for batch in range(13):
                        turn(st, 0, batch)
                all_blocks(pe, products, last_stage)
            with pe.Else():
                def match(t):
                    pe.wait_ge(g_keys_in, t + 1)
                    for c in range(2):
                        last = pe.matmul(grp[:, 0, 0, c * P:(c + 1) * P], g_keys[:, c, :], ident[:, :],
                                         start=True, stop=True)
                    last.then_inc(g_keysT, 1)
                    pe.wait_ge(g_m_ready, t + 1)
                    pe.matmul(acc[:, 0, 0:D], g_eq[:, 0, :], g_attr[:, :], start=True, stop=True).then_inc(g_summed, 1)
                with pe.Fori(0, GTILES) as t:
                    match(t)
                match(GTILES)
                with pe.Fori(0, NT) as j:
                    pe.wait_ge(f_in, (j + 1) * 16)
                    pe.wait_ge(f_sb, j)
                    pe.transpose(acc[0:D, 0, 0:P], g_attr[:, :], ident[:, :]).then_inc(f_T, 1)


def nodes(nc, xp_d, W1, b1, W2, b2, eps, qW, kW, vW, h_d, aggrT_d, xh_d, kp_d, qp_d, v_d, ident, ones):
    ctx = ExitStack()
    W = SC * P
    with ctx:
        sb, ps, sem = tools(nc, ctx)
        w1 = sb("w1", [D, HID], F32)
        w2 = sb("w2", [D, 2, D], F32)
        b1c = sb("b1c", [D, 2], F32)
        b2r = sb("b2r", [1, D], F32)
        qkv = sb("qkv", [D, 3, D], F32)
        eps1 = sb("eps1", [P, 1], F32)
        xt = sb("xt", [P, SC, D], F32)
        ht = sb("ht", [P, SC, D], F32)
        aT = sb("aT", [D, W], F32)
        hid = sb("hid", [D, 2, W], F32)
        x1 = sb("x1", [P, SC, D], F32)
        cen = sb("cen", [P, SC, D], F32)
        sq = sb("sq2", [P, SC, D], F32)
        xh = sb("xh", [P, SC, D], F32)
        mean = sb("mean2", [P, SC], F32)
        rstd = sb("rstd2", [P, SC], F32)
        h2T = sb("h2T", [D, W], F32)
        parts = sb("parts", [D, 2, 3, W], BF16)
        left = sb("left", [D, W], F32)
        vt = sb("vt", [P, SC, HEADS, 32], F32)
        pa = ps("pa", [D, 2, 512])
        pb = ps("pb", [D, 2, 512])
        pm = ps("pm", [P, 2, 4, P])
        pt = ps("pt", [D, 2, 512])
        w_in, in_s = sem("w_in"), sem("in_s")
        hid_p, hid_s, mlp_p, var_s, std_s = sem("hid_p"), sem("hid_s"), sem("mlp_p"), sem("var_s"), sem("std_s")
        h2_s, h2T_p, h2T_s, q_p, k_p, v_p = sem("h2_s"), sem("h2T_p"), sem("h2T_s"), sem("q_p"), sem("k_p"), sem("v_p")
        v_s, parts_s, xh_s, step_s = sem("v_s"), sem("parts_s"), sem("xh_s"), sem("step_s")
        sp_out, pool_out, vt_set = sem("sp_out"), sem("pool_out"), sem("vt_set")
        NSP, NPOOL = 2 + 24, 24
        block = ctx.enter_context(nc.Block())
        halves = ((0, 4), (4, 3))

        @block.sync
        def _(sp):
            sp.dma_start(w1[:, :], W1).then_inc(w_in, 16)
            sp.dma_start(w2[:, :, :], W2.rearrange("(a p) n -> p a n", a=2)).then_inc(w_in, 16)
            with nc.allow_non_contiguous_dma(reason="192 numbers"):
                sp.dma_start(b1c[:, :], b1.rearrange("(a p) -> p a", a=2)).then_inc(w_in, 16)
            sp.dma_start(b2r[:, :], b2.rearrange("(a n) -> a n", a=1)).then_inc(w_in, 16)
            for n, w in enumerate((qW, kW, vW)):
                sp.dma_start(qkv[:, n, :], w).then_inc(w_in, 16)
            sp.dma_start(eps1[:, :], eps.rearrange("(a n) -> a n", a=1).to_broadcast([P, 1])).then_inc(w_in, 16)
            with sp.Fori(0, NS) as s:
                rows, hidden = bass.ds(sp.snap(s * W), W), sp.snap(4 * s)
                sp.wait_ge(hid_s, hidden)
                sp.wait_ge(xh_s, s)
                sp.dma_start(xt[:, :, :], xp_d[rows, :].rearrange("(t p) f -> p t f", p=P)).then_inc(in_s, 16)
                sp.dma_start(ht[:, :, :], h_d[rows, :].rearrange("(t p) f -> p t f", p=P)).then_inc(in_s, 16)
                sp.dma_start(aT[:, :], aggrT_d[:, rows]).then_inc(in_s, 16)
                sp.wait_ge(xh_s, s + 1)
                sp.dma_start(xh_d[rows, :].rearrange("(t p) f -> p t f", p=P), xh[:, :, :]).then_inc(sp_out, 16)
                sp.wait_ge(v_s, 2 * (s + 1))
                sp.dma_start(v_d[bass.ds(s * SC, SC), :, :].rearrange("t p c -> p t c"),
                             vt[:, :, :, :].rearrange("p t h c -> p t (h c)")).then_inc(sp_out, 16)
                sp.wait_ge(parts_s, 2 * (s + 1))
                for h in range(HEADS):
                    for m in range(2):
                        for slot in range(3):
                            sp.dma_start(kp_d[bass.ds(s * SC, SC), slot * DH:(slot + 1) * DH, h, m, :]
                                         .rearrange("t r n -> r t n"),
                                         parts[h * DH:(h + 1) * DH, 1, K_PART[m][slot], :]
                                         .rearrange("r (t n) -> r t n", n=P)).then_inc(sp_out, 16)
            sp.wait_ge(sp_out, 16 * NSP * NS)

        @block.gpsimd
        def _(pool):
            pool.memset(vt[:, :, :, :], 0.0).then_inc(vt_set, 1)
            pool.wait_ge(vt_set, 1)
            pool.memset(vt[:, :, :, DH:DH + 1], 1.0).then_inc(vt_set, 1)
            with pool.Fori(0, NS) as s:
                pool.wait_ge(parts_s, 2 * s + 1)
                for h in range(HEADS):
                    for m in range(2):
                        for slot in range(3):
                            pool.dma_start(qp_d[bass.ds(2 * s, 2), slot * DH:(slot + 1) * DH, h, m, :]
                                           .rearrange("c r n -> r c n"),
                                           parts[h * DH:(h + 1) * DH, 0, Q_PART[m][slot], :]
                                           .rearrange("r (c n) -> r c n", n=CW)).then_inc(pool_out, 16)
            pool.wait_ge(pool_out, 16 * NPOOL * NS)

        @block.tensor
        def _(pe):
            pe.wait_ge(w_in, 128)
            with pe.Fori(0, NS) as s:
                pe.wait_ge(in_s, 48 * (s + 1))
                pe.wait_ge(parts_s, 2 * s)
                for a, bank in enumerate((pa, pb)):
                    for c in range(2):
                        pe.matmul(bank[:, c, 0:CW], w1[:, a * D:(a + 1) * D], aT[:, c * CW:(c + 1) * CW],
                                  start=True, stop=True).then_inc(hid_p, 1)
                pe.wait_ge(hid_s, 4 * (s + 1))
                pe.wait_ge(v_s, 2 * s)
                for c, (first, n) in enumerate(halves):
                    for j in range(n):
                        o, t = pm[:, c, j, 0:D], first + j
                        pe.matmul(o, ones[0:1, :], b2r[:, :], start=True, stop=False)
                        pe.matmul(o, hid[:, 0, t * P:(t + 1) * P], w2[:, 0, :], start=False, stop=False)
                        last = pe.matmul(o, hid[:, 1, t * P:(t + 1) * P], w2[:, 1, :], start=False, stop=True)
                    last.then_inc(mlp_p, 1)
                pe.wait_ge(h2_s, s + 1)
                for c, (first, n) in enumerate(halves):
                    for j in range(n):
                        last = pe.transpose(pt[:, c, j * P:(j + 1) * P], cen[:, first + j, :], ident[:, :])
                    last.then_inc(h2T_p, 1)
                pe.wait_ge(h2T_s, 2 * (s + 1))
                for n, (bank, done) in enumerate(((pa, q_p), (pb, k_p))):
                    for c in range(2):
                        last = pe.matmul(bank[:, c, 0:CW], qkv[:, n, :], h2T[:, c * CW:(c + 1) * CW],
                                         start=True, stop=True)
                    last.then_inc(done, 1)
                for c, (first, n) in enumerate(halves):
                    for j in range(n):
                        last = pe.matmul(pm[:, c, j, 0:D], h2T[:, (first + j) * P:(first + j + 1) * P],
                                         qkv[:, 2, :], start=True, stop=True)
                    last.then_inc(v_p, 1)

        @block.scalar
        def _(act):
            act.wait_ge(w_in, 128)
            act.wait_ge(vt_set, 2)
            with act.Fori(0, NS) as s:
                for a, bank in enumerate((pa, pb)):
                    for c in range(2):
                        act.wait_ge(hid_p, 4 * s + 2 * a + c + 1)
                        act.activation(hid[:, a, c * CW:(c + 1) * CW], bank[:, c, 0:CW], ACT.Relu,
                                       bias=b1c[:, a:a + 1]).then_inc(hid_s, 1)
                act.wait_ge(var_s, s + 1)
                act.activation(rstd[:, :], rstd[:, :], ACT.Sqrt).then_inc(std_s, 1)
                for c, (first, n) in enumerate(halves):
                    act.wait_ge(h2T_p, 2 * s + c + 1)
                    act.activation(h2T[:, first * P:(first + n) * P], pt[:, c, 0:n * P], ACT.Copy).then_inc(h2T_s, 1)
                act.wait_ge(sp_out, 16 * NSP * s)
                for c, (first, n) in enumerate(halves):
                    act.wait_ge(v_p, 2 * s + c + 1)
                    act.activation(vt[:, first:first + n, :, 0:DH],
                                   pm[:, c, 0:n, 0:D].rearrange("p t (h d) -> p t h d", h=HEADS),
                                   ACT.Copy).then_inc(v_s, 1)

        @block.vector
        def _(dve):
            dve.wait_ge(w_in, 128)
            dve.tensor_scalar(eps1[:, :], eps1[:, :], 1.0, None, ALU.add).then_inc(step_s, 1)
            dve.wait_ge(step_s, 1)
            with dve.Fori(0, NS) as s:
                STEPS = 18
                n = [0]

                def step(ins):
                    n[0] += 1
                    ins.then_inc(step_s, 1)
                    dve.wait_ge(step_s, STEPS * s + n[0] + 1)
                dve.wait_ge(in_s, 48 * (s + 1))
                dve.wait_ge(mlp_p, 2 * (s + 1))
                for c, (first, m) in enumerate(halves):
                    step(dve.scalar_tensor_tensor(out=x1[:, first:first + m, :], in0=ht[:, first:first + m, :],
                                                  scalar=eps1[:, 0:1], in1=pm[:, c, 0:m, 0:D],
                                                  op0=ALU.mult, op1=ALU.add))
                step(dve.tensor_tensor(x1[:, :, :], x1[:, :, :], xt[:, :, :], ALU.add))
                step(dve.tensor_reduce(mean[:, :], x1[:, :, :], axis=AX.X, op=ALU.add))
                step(dve.tensor_scalar(mean[:, :], mean[:, :], 1.0 / D, None, ALU.mult))
                step(dve.tensor_tensor(cen[:, :, :], x1[:, :, :], mean[:, :].unsqueeze(2).to_broadcast([P, SC, D]),
                                       ALU.subtract))
                step(dve.tensor_tensor(sq[:, :, :], cen[:, :, :], cen[:, :, :], ALU.mult))
                step(dve.tensor_reduce(rstd[:, :], sq[:, :, :], axis=AX.X, op=ALU.add))
                dve.tensor_scalar(rstd[:, :], rstd[:, :], 1.0 / D, LN_EPS, ALU.mult, ALU.add).then_inc(var_s, 1)
                dve.wait_ge(std_s, s + 1)
                step(dve.reciprocal(rstd[:, :], rstd[:, :]))
                step(dve.tensor_tensor(cen[:, :, :], cen[:, :, :],
                                       rstd[:, :].unsqueeze(2).to_broadcast([P, SC, D]), ALU.mult))
                dve.tensor_scalar(cen[:, :, :], cen[:, :, :], 0.0, None, ALU.max).then_inc(h2_s, 1)
                dve.wait_ge(h2_s, s + 1)
                dve.wait_ge(sp_out, 16 * NSP * s)
                dve.wait_ge(pool_out, 16 * NPOOL * s)
                dve.tensor_tensor(xh[:, :, :], x1[:, :, :], cen[:, :, :], ALU.add).then_inc(xh_s, 1)
                for i, (bank, done) in enumerate(((pa, q_p), (pb, k_p))):
                    dve.wait_ge(done, s + 1)
                    p3 = parts[:, i, :, :].rearrange("p a (c n) -> p a c n", c=2)
                    l2 = left[:, :].rearrange("p (c n) -> p c n", c=2)
                    step(dve.tensor_copy(p3[:, 0], bank[:, :, 0:CW]))
                    step(dve.tensor_tensor(l2, bank[:, :, 0:CW], p3[:, 0], ALU.subtract))
                    step(dve.tensor_copy(parts[:, i, 1, :], left[:, :]))
                    step(dve.tensor_tensor(left[:, :], left[:, :], parts[:, i, 1, :], ALU.subtract))
                    dve.tensor_copy(parts[:, i, 2, :], left[:, :]).then_inc(parts_s, 1)
                assert n[0] == STEPS, n


def attention(nc, count_d, xh_d, kp_d, qp_d, v_d, ident, out):
    ctx = ExitStack()
    GJ = 7
    FIRST = [0] + [GJ + (GJ - 1) * k for k in range(8)]
    GROUPS = len(FIRST) - 1
    assert FIRST[-1] == NT
    R = 3
    CREDIT = R
    with ctx:
        sb, ps, sem = tools(nc, ctx)
        cnt = sb("counts", [P, 2, GJ, CW], F32)
        kb = sb("kb", [KR, 2, GJ, HEADS, 2, P], BF16)
        vb = sb("vb", [P, 2, GJ, P], F32)
        qb = sb("qb", [KR, HEADS, 2, CW], BF16)
        wa = sb("wa", [P, R + 1, 2, CW], F32)
        wb = sb("wb", [P, R + 1, 2, CW], F32)
        ten = sb("ten", [P, 1], F32)
        accs = sb("accs", [P, CW], F32)
        xh = sb("xh3", [CT, 4, D], F32)
        den = sb("den", [CT, 4, HEADS, 1], F32)
        res = sb("res", [CT, 4, HEADS, DH], F32)
        sc = ps("sc", [P, 3, 2, 512])
        acc = ps("acc3", [P, 512])
        tq = ps("tq", [CT, 4, P])
        q_in, xh_in = sem("q_in"), sem("xh_in")
        t_in = [sem("t_in0"), sem("t_in1")]
        sc_a, sc_b, clip_a, relu_b = sem("sc_a"), sem("sc_b"), sem("clip_a"), sem("relu_b")
        exp_a, exp_b, w_a, w_b, pv_done = sem("exp_a"), sem("exp_b"), sem("w_a"), sem("w_b"), sem("pv_done")
        ten_set, acc_out, tq_ready, den_s, o_ready, o_out = (sem(n) for n in (
            "ten_set", "acc_out", "tq_ready", "den_s", "o_ready", "o_out"))
        rows = count_d[0:NP * NP, :].rearrange("(r c) o -> r (c o)", c=NP)
        block = ctx.enter_context(nc.Block())

        def ring(t):
            return R if t == NT - 1 else t % R

        def place(t):
            k = max(k for k in range(GROUPS) if FIRST[k] <= t)
            return k, k % 2, t - FIRST[k]

        @block.sync
        def _(sp):
            def chunk(c):
                if not isinstance(c, int):
                    sp.wait_ge(sc_a, c * NT)
                    sp.wait_ge(sc_b, c * NT)
                sp.dma_start(qb[:, :, :, :], qp_d[bass.ds(c, 1), :, :, :, :].rearrange("c r h m n -> (c r) h m n")
                             ).then_inc(q_in, 16)
                for k in range(GROUPS):
                    first, n = FIRST[k], FIRST[k + 1] - FIRST[k]
                    if k >= 2:
                        sp.wait_ge(pv_done, c * NT + FIRST[k - 1] + CREDIT)
                    elif not isinstance(c, int):
                        sp.wait_ge(pv_done, (c - 1) * NT + FIRST[GROUPS + k - 1] + CREDIT)
                    s = k % 2
                    sp.dma_start(cnt[:, s, 0:n, :], rows[first * P:(first + n) * P, bass.ds(c * CW, CW)]
                                 .rearrange("(j p) s -> p j s", p=P)).then_inc(t_in[s], 16)
                    sp.dma_start(kb[:, s, 0:n, :, :, :].rearrange("r j h m n -> r j (h m n)"),
                                 kp_d[first:first + n, :, :, :, :].rearrange("j r h m n -> r j (h m n)")
                                 ).then_inc(t_in[s], 16)
                    sp.dma_start(vb[:, s, 0:n, :], v_d[first:first + n, :, :].rearrange("j p c -> p j c")
                                 ).then_inc(t_in[s], 16)
                    if k == 2:
                        if not isinstance(c, int):
                            store(c - 1, CT)
                        sp.dma_start(xh[:, :, :], xh_d[bass.ds(c * CW, CW), :].rearrange("(t p) f -> p t f", p=CT)
                                     ).then_inc(xh_in, 16)

            def store(c, last):
                sp.wait_ge(o_ready, c + 1)
                res3 = res[:, :, :, :].rearrange("p t h d -> p t (h d)")
                if last == CT:
                    sp.dma_start(out[bass.ds(c * CW, CW), :].rearrange("(t p) f -> p t f", p=CT),
                                 res3).then_inc(o_out, 16)
                    sp.wait_ge(o_out, 16 * (c + 1))
                else:
                    sp.dma_start(out[c * CW:c * CW + 3 * CT, :].rearrange("(t p) f -> p t f", p=CT),
                                 res3[:, 0:3, :]).then_inc(o_out, 16)
                    sp.dma_start(out[c * CW + 3 * CT:N, :], res3[0:last, 3, :]).then_inc(o_out, 16)
                    sp.wait_ge(o_out, 16 * (c + 2))
            chunk(0)
            with sp.Fori(1, NC_) as c:
                chunk(c)
            store(NC_ - 1, N - (NC_ - 1) * CW - 3 * CT)

        @block.tensor
        def _(pe):
            pe.nop().then_inc(pv_done, CREDIT)

            def scores(c, t):
                _, slot, j = place(t)
                for pair, done in ((0, sc_a), (1, sc_b)):
                    for h in range(2):
                        for m in range(2):
                            last = pe.matmul(sc[:, (2 * t + pair) % 3, h, 0:CW], kb[:, slot, j, 2 * pair + h, m, :],
                                             qb[:, 2 * pair + h, m, :], start=(m == 0), stop=(m == 1))
                    last.then_inc(done, 1)

            def weigh(c, t):
                _, slot, j = place(t)
                for pair, w, ready in ((1, wb, w_b), (0, wa, w_a)):
                    pe.wait_ge(ready, c * NT + t + 1)
                    for h in range(2):
                        q = 2 * pair + h
                        last = pe.matmul(acc[32 * q:32 * q + 32, 0:CW], vb[:, slot, j, 32 * q:32 * q + 32],
                                         w[:, ring(t), h, :], start=(t == 0), stop=(t == NT - 1))
                last.then_inc(pv_done, 1)

            with pe.Fori(0, NC_) as c:
                pe.wait_ge(q_in, 16 * (c + 1))
                for t in range(NT + 1):
                    if t < NT:
                        k, slot, j = place(t)
                        if j == 0:
                            pe.wait_ge(t_in[slot], 48 * (GROUPS // 2) * c + 48 * (k // 2 + 1))
                        if t == 0:
                            pe.wait_ge(clip_a, c * NT)
                            pe.wait_ge(relu_b, c * NT)
                        else:
                            pe.wait_ge(clip_a, c * NT + t)
                            if t >= 2:
                                pe.wait_ge(relu_b, c * NT + t - 1)
                        scores(c, t)
                    if t == 2:
                        pe.wait_ge(acc_out, c)
                    if t >= 2:
                        weigh(c, t - 2)
                weigh(c, NT - 1)
                pe.wait_ge(acc_out, c + 1)
                pe.wait_ge(o_ready, c)
                for i in range(4):
                    last = pe.transpose(tq[:, i, :], accs[:, i * CT:(i + 1) * CT], ident[:, :])
                last.then_inc(tq_ready, 1)

        @block.scalar
        def _(act):
            act.wait_ge(ten_set, 1)
            with act.Fori(0, NC_) as c:
                for t in range(NT):
                    n, r = c * NT + t, ring(t)
                    act.wait_ge(sc_b, n + 1)
                    act.wait_ge(pv_done, n - 2 + CREDIT)
                    act.activation(wb[:, r, :, :], sc[:, (2 * t + 1) % 3, :, 0:CW], ACT.Relu,
                                   bias=ten[:, 0:1], scale=-1.0).then_inc(relu_b, 1)
                    act.wait_ge(relu_b, n + 1)
                    act.activation(wb[:, r, :, :], wb[:, r, :, :], ACT.Exp,
                                   bias=ten[:, 0:1], scale=-1.0).then_inc(exp_b, 1)
                    act.wait_ge(clip_a, n + 1)
                    act.activation(wa[:, r, :, :], wa[:, r, :, :], ACT.Exp).then_inc(exp_a, 1)

        @block.gpsimd
        def _(pool):
            pool.memset(ten[:, :], CLIP).then_inc(ten_set, 1)
            with pool.Fori(0, NC_) as c:
                for t in range(NT):
                    n, r = c * NT + t, ring(t)
                    k, slot, j = place(t)
                    if j == 0:
                        pool.wait_ge(t_in[slot], 48 * (GROUPS // 2) * c + 48 * (k // 2 + 1))
                    pool.wait_ge(exp_a, n + 1)
                    pool.tensor_tensor(wa[:, r, :, :], wa[:, r, :, :],
                                       cnt[:, slot, j, :].unsqueeze(1).to_broadcast([P, 2, CW]),
                                       ALU.mult).then_inc(w_a, 1)

        @block.vector
        def _(dve):
            with dve.Fori(0, NC_) as c:
                for t in range(NT):
                    n, r = c * NT + t, ring(t)
                    k, slot, j = place(t)
                    if j == 0:
                        dve.wait_ge(t_in[slot], 48 * (GROUPS // 2) * c + 48 * (k // 2 + 1))
                    dve.wait_ge(sc_a, n + 1)
                    dve.wait_ge(pv_done, n - 2 + CREDIT)
                    dve.tensor_scalar(wa[:, r, :, :], sc[:, (2 * t) % 3, :, 0:CW], CLIP, -CLIP,
                                      ALU.min, ALU.max).then_inc(clip_a, 1)
                    dve.wait_ge(exp_b, n + 1)
                    dve.scalar_tensor_tensor(out=wb[:, r, :, :], in0=wb[:, r, :, :], scalar=EXP_LO,
                                             in1=cnt[:, slot, j, :].unsqueeze(1).to_broadcast([P, 2, CW]),
                                             op0=ALU.max, op1=ALU.mult).then_inc(w_b, 1)
                dve.wait_ge(pv_done, (c + 1) * NT + CREDIT)
                dve.wait_ge(tq_ready, c)
                dve.tensor_copy(accs[:, :], acc[:, 0:CW]).then_inc(acc_out, 1)
                dve.wait_ge(tq_ready, c + 1)
                num = tq[:, :, :].rearrange("p t (h d) -> p t h d", h=HEADS)
                dve.tensor_scalar(den[:, :, :, :], num[:, :, :, DH:DH + 1], 1e-8, None, ALU.add).then_inc(den_s, 1)
                dve.wait_ge(den_s, 3 * c + 1)
                dve.reciprocal(den[:, :, :, :], den[:, :, :, :]).then_inc(den_s, 1)
                dve.wait_ge(den_s, 3 * c + 2)
                dve.wait_ge(o_out, 16 * c)
                dve.tensor_tensor(res[:, :, :, :], num[:, :, :, 0:DH],
                                  den[:, :, :, :].to_broadcast([CT, 4, HEADS, DH]), ALU.mult).then_inc(den_s, 1)
                dve.wait_ge(den_s, 3 * c + 3)
                dve.wait_ge(xh_in, 16 * (c + 1))
                dve.tensor_tensor(res[:, :, :, :], res[:, :, :, :],
                                  xh[:, :, :].rearrange("p t (h d) -> p t h d", h=HEADS), ALU.add).then_inc(o_ready, 1)


_INS = ["x", "src", "dst", "edge_attr_96", "L0_gnn_W1", "L0_gnn_b1", "L0_gnn_W2", "L0_gnn_b2", "L0_gnn_eps",
        "L1_gnn_qW", "L1_gnn_kW", "L1_gnn_vW"]


def kernel(**inputs):
    import numpy as _np
    import concourse.bacc as _bacc
    from concourse import mybir as _mybir
    from concourse.bass_utils import run_bass_kernel_spmd as _run

    nc = _bacc.Bacc("TRN2", target_bir_lowering=False, num_devices=1)
    arrays, args = {}, []
    for name in _INS:
        a = _np.ascontiguousarray(inputs[name])
        arrays[f"in_{name}"] = a
        args.append(nc.dram_tensor(f"in_{name}", a.shape, _mybir.dt.from_np(a.dtype), kind="ExternalInput").ap())
    args.append(nc.dram_tensor("out_x", (N, D), _mybir.dt.float32, kind="ExternalOutput").ap())
    build(nc, *args)
    r = _run(nc, [arrays], core_ids=[0])
    return r.results[0]["out_x"]
```

```python
from contextlib import ExitStack

import numpy as np
import concourse.bass as bass
from concourse import mybir
from concourse.alu_op_type import AluOpType as ALU

F32 = mybir.dt.float32
F16 = mybir.dt.float16
BF16 = mybir.dt.bfloat16
I32 = mybir.dt.int32
ACT = mybir.ActivationFunctionType
AX = mybir.AxisListType

P = 128
N = 6250
D = 96
HID = 192
HEADS, DH = 4, 24
E = 206250
NT = -(-N // P)
NP = NT * P
TAIL = N - (NT - 1) * P
EP, EC = 110, 1875
G = 8
NG = NP // G
GPB = P // G
K = 3
WIN = K * P
QG = 32 // G
RING = 8
AHEAD = 4
CODE = G * NT
GP = 98
GQ = NG // GP
SC = 7
NS = NT // SC
CW = 448
NC_ = NP // CW
CT = CW // 4
LN_EPS = 1e-5
CLIP = 10.0
EXP_HI = float(np.exp(10.0))
EXP_LO = float(np.exp(-10.0))
GTILES = E // P
GREST = E - GTILES * P
PAIRS = [[(0, 0), (0, 1), (1, 0), (1, 1), (0, 2)], [(2, 0), (1, 2), (2, 1), (2, 2)]]
ROWS = [len(p) * DH for p in PAIRS]


def build(nc, x, src, dst, attr, W1, b1, W2, b2, eps, qW, kW, vW, out):
    ctx = ExitStack()
    with ctx:
        def dram(name, shape, dt):
            return nc.dram_tensor(name, shape, dt).ap()

        count_d = dram("count_d", [(NP + 1) * NP, 1], F32)
        h_d = dram("h_d", [NP, D], F32)
        xp_d = dram("xp_d", [NP, D], F32)
        aggr_d = dram("aggr_d", [NP + P, D], F32)
        start_d = dram("start_d", [1, NG + 1], F32)
        rec_d = dram("rec_d", [E, 4], F32)
        xh_d = dram("xh_d", [NP, D], F32)
        parts_d = dram("parts_d", [2, D, 3, NP], BF16)
        qp_d = [dram(f"q{m}_d", [ROWS[m], HEADS, NP], BF16) for m in range(2)]
        kp_d = [dram(f"k{m}_d", [ROWS[m], HEADS, NP], BF16) for m in range(2)]
        v_d = dram("v_d", [NT, P, P], F32)

        flag_i = ctx.enter_context(nc.sbuf_tensor("flag_i", [1, 1], I32))
        start_i = ctx.enter_context(nc.sbuf_tensor("start_i", [1, NG], I32))
        ident = ctx.enter_context(nc.sbuf_tensor("ident", [P, P], F32))
        ones = ctx.enter_context(nc.sbuf_tensor("ones", [P, P], F32))

        ids_and_norm(nc, x, src, dst, xp_d, h_d, start_d, rec_d, aggr_d, flag_i, start_i, ident, ones)
        edges(nc, src, dst, attr, h_d, aggr_d, rec_d, count_d, flag_i, start_i, ident, ones)
        nodes(nc, xp_d, W1, b1, W2, b2, eps, qW, kW, vW, h_d, aggr_d, xh_d, parts_d, kp_d, qp_d, v_d, ident, ones)
        attention(nc, count_d, xh_d, kp_d, qp_d, v_d, ident, out)


def tools(nc, ctx):
    def sb(name, shape, dt):
        return ctx.enter_context(nc.sbuf_tensor(name, shape, dt))

    def ps(name, shape, dt=F32):
        return ctx.enter_context(nc.psum_tensor(name, shape, dt))

    def sem(name):
        return ctx.enter_context(nc.semaphore(name))

    return sb, ps, sem


def linker(eng, done):
    n = [0]

    def link(ins):
        n[0] += 1
        ins.then_inc(done, 1)
        eng.wait_ge(done, n[0])

    return link


def ids_and_norm(nc, x, src, dst, xp_d, h_d, start_d, rec_d, aggr_d, flag_i, start_i, ident, ones):
    ctx = ExitStack()
    with ctx:
        sb, ps, sem = tools(nc, ctx)
        xn = sb("xn", [P, NT, D], F32)
        sq = sb("sq", [P, NT, D], F32)
        mean = sb("mean", [P, NT], F32)
        rstd = sb("rstd", [P, NT], F32)
        srct = sb("srct", [EP, EC], I32)
        dstt = sb("dstt", [EP, EC], I32)
        part = sb("part", [EP, EC], I32)
        rec = sb("rec", [EP, EC, 4], F32)
        nexti = sb("nexti", [EP, 1], I32)
        nextf = sb("nextf", [EP, 1], F32)
        lasti = sb("lasti", [1, EP], I32)
        lastf = sb("lastf", [1, EP], F32)
        bad = sb("bad", [EP, 2], F32)
        lastb = sb("lastb", [GP, EP], F32)
        less = sb("less", [GP, EC], F32)
        row = sb("row", [GP, GQ, EC], I32)
        thr_i = sb("thr_i", [GP, GQ], I32)
        thr = sb("thr", [GP, GQ], F32)
        cnt = sb("cnt", [GP, GQ], F32)
        at = sb("at", [GP, GQ], F32)
        at_i = sb("at_i", [GP, GQ], I32)
        start = sb("start", [GP, GQ], F32)
        srow = sb("srow", [1, NG + 1], F32)
        diff = sb("diff", [1, NG], F32)
        fl = sb("fl", [1, 4], F32)
        lastp = ps("lastp", [GP, EP])
        badp = ps("badp", [1, 2])
        x_out = sem("x_out")
        x_in, ids_in, small_in, bnd_in = sem("x_in"), sem("ids_in"), sem("small_in"), sem("bnd_in")
        memset_done, consts, pool_done = sem("memset_done"), sem("consts"), sem("pool_done")
        dve_done, sqrt_in, sqrt_out = sem("dve_done"), sem("sqrt_in"), sem("sqrt_out")
        lastf_ready, lastp_ready = sem("lastf_ready"), sem("lastp_ready")
        bad_ready, badp_ready = sem("bad_ready"), sem("badp_ready")
        at_ready, rows_in = sem("at_ready"), sem("rows_in")
        start_ready, start_out, srow_in = sem("start_ready"), sem("start_out"), sem("srow_in")
        h_ready, rec_ready, h_out, rec_out = sem("h_ready"), sem("rec_ready"), sem("h_out"), sem("rec_out")
        block = ctx.enter_context(nc.Block())

        @block.sync
        def _(sp):
            sp.dma_start(dstt[:], dst.rearrange("(p c) -> p c", c=EC)).then_inc(ids_in, 16)
            sp.dma_start(srct[:], src.rearrange("(p c) -> p c", c=EC)).then_inc(ids_in, 16)
            d2 = dst.rearrange("(p c) -> p c", c=EC)
            with nc.allow_non_contiguous_dma(reason="110 ids"):
                sp.dma_start(nexti[0:EP - 1, :], d2[1:EP, 0:1]).then_inc(small_in, 16)
            with nc.allow_non_contiguous_dma(reason="110 ids"):
                sp.dma_start(lasti[:, :], d2[:, EC - 1:EC].rearrange("p c -> c p")).then_inc(bnd_in, 16)
            sp.wait_ge(start_ready, 1)
            for q in range(GQ):
                with nc.allow_non_contiguous_dma(reason="98 numbers"):
                    sp.dma_start(start_d[0:1, q * GP:(q + 1) * GP].rearrange("a p -> p a"),
                                 start[:, q:q + 1]).then_inc(start_out, 16)
            sp.wait_ge(start_out, 16 * GQ)
            sp.dma_start(srow[:, 0:NG], start_d[:, 0:NG]).then_inc(srow_in, 16)
            sp.wait_ge(rec_ready, 1)
            sp.dma_start(rec_d.rearrange("(p c) k -> p c k", c=EC), rec[:, :, :]).then_inc(rec_out, 16)
            sp.wait_ge(rec_out, 16)

        @block.scalar
        def _(act):
            act.wait_ge(memset_done, 1)
            act.dma_start(xn[:, 0:NT - 1, :],
                          x[0:(NT - 1) * P, :].rearrange("(t p) f -> p t f", p=P)).then_inc(x_in, 16)
            act.dma_start(xn[0:TAIL, NT - 1, :], x[(NT - 1) * P:N, :]).then_inc(x_in, 16)
            act.wait_ge(x_in, 32)
            act.dma_start(xp_d.rearrange("(t p) f -> p t f", p=P), xn[:, :, :]).then_inc(x_out, 16)
            act.wait_ge(sqrt_in, 1)
            act.activation(rstd[:, :], rstd[:, :], ACT.Sqrt).then_inc(sqrt_out, 1)
            act.wait_ge(h_ready, 1)
            act.dma_start(h_d.rearrange("(t p) f -> p t f", p=P), xn[:, :, :]).then_inc(h_out, 16)
            act.wait_ge(h_out, 16)

        @block.gpsimd
        def _(pool):
            pool.memset(ident[:], 0.0).then_inc(pool_done, 1)
            pool.memset(ones[:], 1.0).then_inc(consts, 1)
            pool.iota(thr_i[:], pattern=[[GP * G, GQ]], base=0, channel_multiplier=G).then_inc(consts, 1)
            pool.wait_ge(pool_done, 1)
            pool.affine_select(out=ident[:], in_=ident[:], compare_op=ALU.not_equal, fill=1.0, base=0,
                               pattern=[[-1, P]], channel_multiplier=1).then_inc(consts, 1)
            pool.wait_ge(at_ready, 1)
            for q in range(GQ):
                pool.indirect_dma_start(
                    out=row[:, q, :], out_offset=None, in_=dst.rearrange("(p c) -> p c", c=EC),
                    in_offset=bass.IndirectOffsetOnAxis(ap=at_i[:, q:q + 1], axis=0),
                ).then_inc(rows_in, 16)
            pool.wait_ge(rows_in, 16 * GQ)

        @block.tensor
        def _(pe):
            pe.wait_ge(consts, 3)
            pe.wait_ge(lastf_ready, 1)
            pe.matmul(lastp[:, :], ones[0:1, 0:GP], lastf[:, :], start=True, stop=True).then_inc(lastp_ready, 1)
            pe.wait_ge(bad_ready, 1)
            pe.matmul(badp[:, 0:1], ones[0:EP, 0:1], bad[:, 0:1], start=True, stop=True).then_inc(badp_ready, 1)

        @block.vector
        def _(dve):
            link = linker(dve, dve_done)
            dve.memset(xn[:, NT - 1, :], 0.0).then_inc(memset_done, 1)
            dve.memset(nextf[:, :], float(NP))
            link(dve.memset(srow[:, NG:NG + 1], float(E)))
            dve.wait_ge(consts, 3)
            link(dve.tensor_copy(thr[:, :], thr_i[:, :]))
            dve.wait_ge(bnd_in, 16)
            dve.tensor_copy(lastf[:, :], lasti[:, :]).then_inc(lastf_ready, 1)
            dve.wait_ge(lastp_ready, 1)
            link(dve.tensor_copy(lastb[:, :], lastp[:, :]))
            for q in range(GQ):
                link(dve.tensor_scalar(less[:, 0:EP], lastb[:, :], thr[:, q:q + 1], None, ALU.is_lt))
                link(dve.tensor_reduce(at[:, q:q + 1], less[:, 0:EP], axis=AX.X, op=ALU.add))
            link(dve.tensor_scalar(at[:, :], at[:, :], float(EP - 1), None, ALU.min))
            dve.tensor_copy(at_i[:, :], at[:, :]).then_inc(at_ready, 1)
            dve.wait_ge(ids_in, 32)
            link(dve.tensor_copy(rec[:, :, 1], dstt[:, :]))
            link(dve.tensor_scalar(part[:, :], srct[:, :], 7, None, ALU.logical_shift_right))
            link(dve.scalar_tensor_tensor(out=rec[:, :, 0], in0=rec[:, :, 1], scalar=float(NT), in1=part[:, :],
                                          op0=ALU.mult, op1=ALU.add))
            link(dve.tensor_scalar(part[:, :], srct[:, :], P - 1, None, ALU.bitwise_and))
            link(dve.tensor_copy(rec[:, :, 3], part[:, :]))
            link(dve.tensor_copy(rec[:, :, 2], srct[:, :]))
            dve.tensor_copy(bad[:, 1:2], rec[:, 0, 3:4]).then_inc(rec_ready, 1)
            dve.wait_ge(small_in, 16)
            link(dve.tensor_copy(nextf[0:EP - 1, :], nexti[0:EP - 1, :]))
            lt = sq[0:EP, :, :].rearrange("p a b -> p (a b)")[:, 0:EC]
            link(dve.tensor_tensor(lt[:, 0:EC - 1], rec[:, 0:EC - 1, 1], rec[:, 1:EC, 1], ALU.is_gt))
            link(dve.tensor_tensor(lt[:, EC - 1:EC], rec[:, EC - 1, 1:2], nextf[:, :], ALU.is_gt))
            dve.tensor_reduce(bad[:, 0:1], lt, axis=AX.X, op=ALU.add).then_inc(bad_ready, 1)
            dve.wait_ge(rows_in, 16 * GQ)
            for q in range(GQ):
                link(dve.tensor_scalar(less[:, :], row[:, q, :], thr[:, q:q + 1], None, ALU.is_lt))
                link(dve.tensor_reduce(cnt[:, q:q + 1], less[:, :], axis=AX.X, op=ALU.add))
            dve.scalar_tensor_tensor(out=start[:, :], in0=at[:, :], scalar=float(EC), in1=cnt[:, :],
                                     op0=ALU.mult, op1=ALU.add).then_inc(start_ready, 1)
            dve.wait_ge(srow_in, 16)
            link(dve.tensor_tensor(diff[:, :], srow[:, 1:NG + 1], srow[:, 0:NG], ALU.subtract))
            link(dve.tensor_reduce(fl[:, 0:1], diff[:, :], axis=AX.X, op=ALU.max))
            link(dve.tensor_scalar(fl[:, 1:2], fl[:, 0:1], float(WIN), None, ALU.is_le))
            dve.wait_ge(badp_ready, 1)
            link(dve.tensor_scalar(fl[:, 2:3], badp[:, 0:1], 0.0, None, ALU.is_equal))
            link(dve.tensor_tensor(fl[:, 3:4], fl[:, 1:2], fl[:, 2:3], ALU.mult))
            link(dve.tensor_copy(flag_i[:, :], fl[:, 3:4]))
            link(dve.tensor_scalar(srow[:, :], srow[:, :], float(E - WIN), None, ALU.min))
            link(dve.tensor_copy(start_i[:, :], srow[:, 0:NG]))
            dve.wait_ge(x_in, 32)
            link(dve.tensor_reduce(mean[:, :], xn[:, :, :], axis=AX.X, op=ALU.add))
            dve.wait_ge(x_out, 16)
            link(dve.tensor_scalar(mean[:, :], mean[:, :], 1.0 / D, None, ALU.mult))
            link(dve.tensor_tensor(xn[:, :, :], xn[:, :, :], mean[:, :].unsqueeze(2).to_broadcast([P, NT, D]),
                                   ALU.subtract))
            link(dve.tensor_tensor(sq[:, :, :], xn[:, :, :], xn[:, :, :], ALU.mult))
            link(dve.tensor_reduce(rstd[:, :], sq[:, :, :], axis=AX.X, op=ALU.add))
            dve.tensor_scalar(rstd[:, :], rstd[:, :], 1.0 / D, LN_EPS, ALU.mult, ALU.add).then_inc(sqrt_in, 1)
            dve.wait_ge(sqrt_out, 1)
            link(dve.reciprocal(rstd[:, :], rstd[:, :]))
            link(dve.tensor_tensor(xn[:, :, :], xn[:, :, :], rstd[:, :].unsqueeze(2).to_broadcast([P, NT, D]),
                                   ALU.mult))
            dve.tensor_scalar(xn[:, :, :], xn[:, :, :], 0.0, None, ALU.max).then_inc(h_ready, 1)


def edges(nc, src, dst, attr, h_d, aggr_d, rec_d, count_d, flag_i, start_i, ident, ones):
    count_rows = count_d[0:NP * NP, :].rearrange("(r c) o -> r (c o)", c=NP)
    ctx = ExitStack()
    with ctx:
        sb, ps, sem = tools(nc, ctx)
        hf = sb("hf", [P, NT, D], F32)
        hpart = sb("hpart", [P, NT, 3, D], F16)
        slab = sb("slab", [P, 2, NT, P], F16)
        rowsT = sb("rowsT", [P, 2, NP], F32)
        sums = sb("sums", [P, 2, 4, D], F32)
        aggr = sb("aggr", [P, D], F32)
        attr_w = sb("attr_w", [P, RING, K, D], F32)
        rec_w = sb("rec_w", [P, RING, K, 4], F32)
        rel = sb("rel", [P, RING, K, 2], F32)
        base_i = sb("base_i", [P, NG, 2], I32)
        base = sb("base", [P, NG, 2], F32)
        iota_i = sb("iota_i", [P, CODE], I32)
        iota = sb("iota", [P, CODE], F16)
        iota_g = sb("iota_g", [P, QG, QG * G], F32)
        code_oh = sb("code_oh", [P, 2, K, CODE], F16)
        lane_oh = sb("lane_oh", [P, 2, K, P], F16)
        dst_oh = sb("dst_oh", [P, 2, K, QG * G], F32)
        ident16 = sb("ident16", [P, P], F16)
        lane_i = sb("lane_i", [P, 1], I32)
        lane = sb("lane", [P, 1], F32)
        g_rec = sb("g_rec", [P, 4], F32)
        g_src = sb("g_src", [P, 1], I32)
        g_attr = sb("g_attr", [P, D], F32)
        g_h = sb("g_h", [P, D], F32)
        g_rest = sb("g_rest", [P, 2], F32)
        g_keys = sb("g_keys", [P, 2, P], F32)
        g_eq = sb("g_eq", [P, 3, P], F32)
        g_low = sb("g_low", [P, P], F32)
        g_first = sb("g_first", [P, 2, P], F32)
        g_dup = sb("g_dup", [P, 2], F32)
        g_cnt = sb("g_cnt", [P, 1], F32)
        g_tmp = sb("g_tmp", [P, 4], F32)
        g_idx = sb("g_idx", [P, 4], I32)
        g_sum = sb("g_sum", [P, D], F32)
        carrier = sb("carrier", [P, 4], F32)
        grp = ps("grp", [P, 4, 512])
        acc = ps("acc", [P, 2, 512])
        tp = ps("tp", [P, 2, 512])
        h_in, base_ready, set_done, consts = sem("h_in"), sem("base_ready"), sem("set_done"), sem("consts2")
        rec_in = [sem(f"rec_in{s}") for s in range(RING)]
        attr_in = [sem(f"attr_in{s}") for s in range(RING)]
        summed, sum_step, aggr_out = sem("summed"), sem("sum_step"), sem("aggr_out")
        rel_ready, oh_ready, group_done, slab_part = sem("rel_ready"), sem("oh_ready"), sem("group_done"), sem("slab_part")
        grp_ready, set_iota = sem("grp_ready"), sem("set_iota")
        tp_ready, tp_used, rows_ready = sem("tp_ready"), sem("tp_used"), sem("rows_ready")
        rows_out = [sem("rows_out0"), sem("rows_out1")]
        g_zero_out, g_in, g_dve, g_pe, g_idx_ready = sem("g_zero_out"), sem("g_in"), sem("g_dve"), sem("g_pe"), sem("g_idx_ready")
        g_h_in, g_keys_in, g_keysT, g_m_ready, g_summed = sem("g_h_in"), sem("g_keys_in"), sem("g_keysT"), sem("g_m_ready"), sem("g_summed")
        g_padded, g_out, g_zeroed, g_low_ready = sem("g_padded"), sem("g_out"), sem("g_zeroed"), sem("g_low_ready")
        g_carrier = sem("g_carrier")
        block = ctx.enter_context(nc.Block())

        SLICES = [range(13 * gi // GPB, 13 * (gi + 1) // GPB) for gi in range(GPB)]

        FIRST_SLICE = next(gi for gi in range(GPB) if SLICES[gi])

        def tiles_of(batch):
            return range(4 * batch, min(4 * batch + 4, NT))

        def all_blocks(eng, body, last_stage):
            body(0, 0, False)
            with eng.Fori(0, (NT - 1) // 2) as i:
                body(2 * i + 1, 1, True)
                body(2 * i + 2, 0, True)
            last_stage(NT - 1)

        @block.sync
        def _(sp):
            fast = sp.value_load(flag_i[0:1, 0:1], min_val=0, max_val=1)
            with sp.If(fast == 1):
                def windows(b, par, has_store):
                    for gi in range(GPB):
                        g, slot = b * GPB + gi, gi % RING
                        first = sp.value_load(start_i[0:1, bass.ds(g, 1)], min_val=0, max_val=E - WIN)
                        sp.wait_ge(group_done, g + 1)
                        sp.dma_start(attr_w[:, slot, :, :].rearrange("p k c -> p (k c)"),
                                     attr[bass.ds(first, WIN), :].rearrange("(p k) c -> p (k c)", k=K)
                                     ).then_inc(attr_in[slot], 16)
                        if has_store and gi == 10:
                            store(b - 2, par)

                def store(st, par):
                    rows = bass.ds(st * P if isinstance(st, int) else sp.snap(st * P), P)
                    sp.wait_ge(rows_ready, st + 1)
                    for piece in range(4):
                        cols = slice(piece * (NP // 4), (piece + 1) * (NP // 4))
                        sp.dma_start(count_rows[rows, cols], rowsT[:, par, cols]
                                     ).then_inc(rows_out[par], 16)
                windows(0, 0, False)
                windows(1, 1, False)
                with sp.Fori(1, (NT - 1) // 2) as i:
                    windows(2 * i, 0, True)
                    windows(2 * i + 1, 1, True)
                windows(NT - 1, 0, True)
                store(NT - 2, 1)
                store(NT - 1, 0)
                sp.wait_ge(rows_out[0], 64 * ((NT + 1) // 2))
                sp.wait_ge(rows_out[1], 64 * ((NT - 1) // 2))
            with sp.Else():
                sp.wait_ge(g_zeroed, 1)
                with sp.Fori(0, NT) as j:
                    sp.dma_start(count_rows[bass.ds(j * P, P), :], rowsT[:, 0, :]).then_inc(g_zero_out, 16)
                    sp.dma_start(aggr_d[bass.ds(j * P, P), :], rowsT[:, 0, 0:D]).then_inc(g_zero_out, 16)
                sp.dma_start(count_d[NP * NP:NP * NP + NP, :].rearrange("(p c) o -> p (c o)", c=NT),
                             rowsT[:, 0, 0:NT]).then_inc(g_zero_out, 16)
                sp.dma_start(aggr_d[NP:NP + P, :], rowsT[:, 0, 0:D]).then_inc(g_zero_out, 16)
                sp.wait_ge(g_zero_out, 16 * (2 * NT + 2))

                def load(t, rows, at):
                    sp.wait_ge(g_out, t * 32)
                    sp.dma_start(g_rec[0:rows, :], rec_d[bass.ds(at, rows), :]).then_inc(g_in, 16)
                    sp.dma_start(g_attr[0:rows, :], attr[bass.ds(at, rows), :]).then_inc(g_in, 16)
                with sp.Fori(0, GTILES) as t:
                    load(t, P, t * P)
                sp.wait_ge(g_out, GTILES * 32)
                sp.wait_ge(g_padded, 1)
                sp.dma_start(g_rec[0:GREST, :], rec_d[GTILES * P:E, :]).then_inc(g_in, 16)
                sp.dma_start(g_attr[0:GREST, :], attr[GTILES * P:E, :]).then_inc(g_in, 16)

        @block.gpsimd
        def _(pool):
            fast = pool.value_load(flag_i[0:1, 0:1], min_val=0, max_val=1)
            pool.iota(base_i[:, :, 0], pattern=[[CODE, NG]], base=0, channel_multiplier=0).then_inc(base_ready, 1)
            pool.iota(base_i[:, :, 1], pattern=[[G, NG]], base=0, channel_multiplier=0).then_inc(base_ready, 1)
            pool.iota(iota_i[:, :], pattern=[[1, CODE]], base=0, channel_multiplier=0).then_inc(base_ready, 1)
            pool.iota(lane_i[:, :], pattern=[[0, 1]], base=0, channel_multiplier=1).then_inc(base_ready, 1)
            with pool.If(fast == 1):
                pool.nop().then_inc(summed, 2)

                def load(g, slot):
                    first = pool.value_load(start_i[0:1, bass.ds(g, 1)], min_val=0, max_val=E - WIN)
                    pool.wait_ge(group_done, g + 1)
                    pool.dma_start(rec_w[:, slot, :, :].rearrange("p k c -> p (k c)"),
                                   rec_d[bass.ds(first, WIN), :].rearrange("(p k) c -> p (k c)", k=K)
                                   ).then_inc(rec_in[slot], 16)

                def relative(b, par, has_store):
                    for gi in range(GPB):
                        g, slot = b * GPB + gi, gi % RING
                        if not (isinstance(b, int) and g + AHEAD >= NG):
                            load(g + AHEAD, (gi + AHEAD) % RING)
                        pool.wait_ge(rec_in[slot], 16 * (GPB // RING * b + gi // RING + 1))
                        pool.tensor_tensor(rel[:, slot, :, :], rec_w[:, slot, :, 0:2],
                                           base[:, bass.ds(g, 1), :].to_broadcast([P, K, 2]),
                                           ALU.subtract).then_inc(rel_ready, 1)
                        if has_store and gi == 6:
                            store(b - 2, par)

                def store(st, par):
                    pool.wait_ge(rows_ready, st + 1)
                    pool.wait_ge(aggr_out, 16 * st)
                    pool.tensor_tensor(aggr[:, :], sums[:, par, 0, :], sums[:, par, 1, :], ALU.add).then_inc(sum_step, 1)
                    pool.wait_ge(sum_step, 2 * st + 1)
                    pool.tensor_tensor(aggr[:, :], aggr[:, :], sums[:, par, 2, :], ALU.add).then_inc(sum_step, 1)
                    pool.wait_ge(sum_step, 2 * st + 2)
                    pool.tensor_tensor(aggr[:, :], aggr[:, :], sums[:, par, 3, :], ALU.add).then_inc(summed, 1)
                    pool.wait_ge(summed, st + 3)
                    pool.dma_start(aggr_d[bass.ds(st * P, P), :], aggr[:, :]).then_inc(aggr_out, 16)
                pool.wait_ge(set_done, 1)
                for g in range(AHEAD):
                    load(g, g)
                relative(0, 0, False)
                relative(1, 1, False)
                with pool.Fori(1, (NT - 1) // 2) as i:
                    relative(2 * i, 0, True)
                    relative(2 * i + 1, 1, True)
                relative(NT - 1, 0, True)
                store(NT - 2, 1)
                store(NT - 1, 0)
                pool.wait_ge(aggr_out, 16 * NT)
            with pool.Else():
                pool.wait_ge(g_low_ready, 1)
                pool.affine_select(out=g_low[:, :], in_=g_low[:, :], compare_op=ALU.is_gt, fill=0.0, base=0,
                                   pattern=[[-1, P]], channel_multiplier=1).then_inc(g_low_ready, 1)

                pool.memset(carrier[:, :], 0.0).then_inc(g_carrier, 1)
                pool.wait_ge(g_carrier, 1)

                def add(t):
                    pool.wait_ge(g_idx_ready, 2 * t + 1)
                    pool.tensor_tensor(carrier[:, 1:2], carrier[:, 0:1], carrier[:, 0:1], ALU.add
                                       ).then_inc(g_carrier, 1)
                    pool.indirect_dma_start(out=g_h[:, :], out_offset=None, in_=h_d,
                                            in_offset=bass.IndirectOffsetOnAxis(ap=g_idx[:, 0:1], axis=0),
                                            ).then_inc(g_h_in, 16)
                    pool.wait_ge(g_idx_ready, 2 * t + 2)
                    pool.tensor_tensor(carrier[:, 2:3], carrier[:, 0:1], carrier[:, 0:1], ALU.add
                                       ).then_inc(g_carrier, 1)
                    pool.indirect_dma_start(out=aggr_d, out_offset=bass.IndirectOffsetOnAxis(ap=g_idx[:, 1:2], axis=0),
                                            in_=g_sum[:, :], in_offset=None, compute_op=ALU.add).then_inc(g_out, 16)
                    pool.indirect_dma_start(out=count_d, out_offset=bass.IndirectOffsetOnAxis(ap=g_idx[:, 2:3], axis=0),
                                            in_=g_cnt[:, :], in_offset=None, compute_op=ALU.add).then_inc(g_out, 16)
                    pool.wait_ge(g_carrier, 2 * t + 3)
                    pool.wait_ge(g_out, (t + 1) * 32)
                with pool.Fori(0, GTILES) as t:
                    add(t)
                add(GTILES)

        @block.vector
        def _(dve):
            link = linker(dve, set_done)
            fast = dve.value_load(flag_i[0:1, 0:1], min_val=0, max_val=1)
            dve.wait_ge(base_ready, 4)
            dve.tensor_copy(base[:, :, :], base_i[:, :, :])
            dve.tensor_copy(iota[:, :], iota_i[:, :])
            dve.memset(iota_g[:, :, :], -1e6).then_inc(set_iota, 1)
            dve.wait_ge(set_iota, 1)
            for q in range(QG):
                dve.tensor_copy(iota_g[:, q, q * G:(q + 1) * G], iota_i[:, 0:G]).then_inc(set_iota, 1)
            dve.tensor_copy(lane[:, :], lane_i[:, :])
            link(dve.tensor_copy(ident16[:, :], ident[:, :]))
            dve.wait_ge(set_iota, QG + 1)
            with dve.If(fast == 1):
                dve.wait_ge(h_in, 16)
                for part in range(2):
                    link(dve.tensor_copy(hpart[:, :, part, :], hf[:, :, :]))
                    link(dve.tensor_tensor(hf[:, :, :], hf[:, :, :], hpart[:, :, part, :], ALU.subtract))
                dve.tensor_copy(hpart[:, :, 2, :], hf[:, :, :]).then_inc(consts, 1)

                def one_hots(b, par, has_stage):
                    for gi in range(GPB):
                        g, slot, s = b * GPB + gi, gi % RING, gi % 2
                        dve.wait_ge(rel_ready, g + 1)
                        dve.wait_ge(group_done, g - 1 + RING)
                        for k in range(K):
                            dve.tensor_scalar(code_oh[:, s, k, :], iota[:, :], rel[:, slot, k, 0:1], None, ALU.is_equal)
                            dve.tensor_scalar(lane_oh[:, s, k, :], iota[:, 0:P], rec_w[:, slot, k, 3:4], None, ALU.is_equal)
                        dve.tensor_tensor(dst_oh[:, s, :, :],
                                          iota_g[:, gi % QG, :].unsqueeze(1).to_broadcast([P, K, QG * G]),
                                          rel[:, slot, :, 1:2].to_broadcast([P, K, QG * G]),
                                          ALU.is_equal).then_inc(oh_ready, 1)
                all_blocks(dve, one_hots, lambda b: None)
            with dve.Else():
                dve.memset(g_low[:, :], 1.0).then_inc(g_low_ready, 1)
                dve.memset(g_rec[:, :], 0.0)
                dve.memset(g_attr[:, :], 0.0)
                dve.memset(rowsT[:, 0, :], 0.0).then_inc(g_zeroed, 1)
                dve.wait_ge(g_zeroed, 1)
                dve.wait_ge(g_low_ready, 2)

                def work(t):
                    steps = [0]

                    def step(ins):
                        steps[0] += 1
                        ins.then_inc(g_dve, 1)
                        dve.wait_ge(g_dve, t * 19 + steps[0])
                    dve.wait_ge(g_in, (t + 1) * 32)
                    step(dve.tensor_copy(g_keys[:, 0, :], g_rec[:, 1:2].to_broadcast([P, P])))
                    dve.tensor_copy(g_keys[:, 1, :], g_rec[:, 2:3].to_broadcast([P, P])).then_inc(g_keys_in, 1)
                    dve.tensor_copy(g_idx[:, 0:1], g_rec[:, 2:3]).then_inc(g_idx_ready, 1)
                    dve.wait_ge(g_keysT, t + 1)
                    step(dve.tensor_scalar(g_eq[:, 0, :], grp[:, 0, 0:P], g_rec[:, 1:2], None, ALU.is_equal))
                    step(dve.tensor_scalar(g_eq[:, 1, :], grp[:, 0, P:2 * P], g_rec[:, 2:3], None, ALU.is_equal))
                    step(dve.tensor_tensor(g_eq[:, 2, :], g_eq[:, 0, :], g_eq[:, 1, :], ALU.mult))
                    step(dve.tensor_reduce(g_cnt[:, :], g_eq[:, 2, :], axis=AX.X, op=ALU.add))
                    step(dve.tensor_tensor(g_first[:, 0, :], g_eq[:, 0, :], g_low[:, :], ALU.mult))
                    step(dve.tensor_tensor(g_first[:, 1, :], g_eq[:, 2, :], g_low[:, :], ALU.mult))
                    step(dve.tensor_reduce(g_dup[:, :], g_first[:, :, :], axis=AX.X, op=ALU.max))
                    step(dve.tensor_scalar(g_tmp[:, 0:1], lane[:, :], float(NP), g_rec[:, 1:2], ALU.add, ALU.subtract))
                    step(dve.tensor_tensor(g_tmp[:, 1:2], g_tmp[:, 0:1], g_dup[:, 0:1], ALU.mult))
                    step(dve.tensor_tensor(g_idx[:, 1:2], g_tmp[:, 1:2], g_rec[:, 1:2], ALU.add))
                    step(dve.tensor_scalar(g_tmp[:, 0:1], g_rec[:, 0:1], -1.0, float(NP * NT), ALU.mult, ALU.add))
                    step(dve.scalar_tensor_tensor(out=g_idx[:, 2:3], in0=g_tmp[:, 0:1], scalar=g_dup[:, 1:2],
                                                  in1=g_rec[:, 0:1], op0=ALU.mult, op1=ALU.add))
                    step(dve.tensor_tensor(g_tmp[:, 2:3], lane[:, :], g_rec[:, 3:4], ALU.subtract))
                    step(dve.scalar_tensor_tensor(out=g_idx[:, 3:4], in0=g_tmp[:, 2:3], scalar=g_dup[:, 1:2],
                                                  in1=g_rec[:, 3:4], op0=ALU.mult, op1=ALU.add))
                    step(dve.tensor_scalar(g_idx[:, 2:3], g_idx[:, 2:3], 7, None, ALU.logical_shift_left))
                    step(dve.tensor_tensor(g_idx[:, 2:3], g_idx[:, 2:3], g_idx[:, 3:4], ALU.bitwise_or))
                    dve.wait_ge(g_h_in, (t + 1) * 16)
                    step(dve.tensor_tensor(g_attr[:, :], g_attr[:, :], g_h[:, :], ALU.add))
                    dve.nop().then_inc(g_m_ready, 1)
                    dve.wait_ge(g_summed, t + 1)
                    step(dve.tensor_copy(g_sum[:, :], acc[:, 0, 0:D]))
                    assert steps[0] == 19
                    dve.nop().then_inc(g_idx_ready, 1)

                def padding(t):
                    dve.wait_ge(g_out, t * 32)
                    dve.memset(g_attr[:, :], 0.0)
                    dve.memset(g_rec[:, 0:1], float(NP * NT - 1))
                    dve.memset(g_rec[:, 1:3], float(NP - 1))
                    dve.memset(g_rec[:, 3:4], float(P - 1)).then_inc(g_padded, 1)

                with dve.Fori(0, GTILES) as t:
                    work(t)
                padding(GTILES)
                work(GTILES)

        @block.scalar
        def _(act):
            fast = act.value_load(flag_i[0:1, 0:1], min_val=0, max_val=1)
            with act.If(fast == 1):
                act.nop().then_inc(tp_used, 2)
                act.dma_start(hf[:, :, :], h_d.rearrange("(t p) f -> p t f", p=P)).then_inc(h_in, 16)

                def rows(st, par, batch):
                    tiles = tiles_of(batch)
                    n = st * 13 + batch
                    act.wait_ge(tp_ready, n + 1)
                    act.activation(rowsT[:, par, 4 * batch * P:(4 * batch + len(tiles)) * P],
                                   tp[:, batch % 2 if par == 0 else (batch + 1) % 2, 0:len(tiles) * P],
                                   ACT.Copy).then_inc(tp_used, 1)

                def finish(st, par):
                    act.wait_ge(tp_ready, (st + 1) * 13)
                    act.wait_ge(summed, st + 1)
                    act.activation(sums[:, par, :, :].rearrange("p a f -> p (a f)"), acc[:, par, 0:4 * D],
                                   ACT.Copy).then_inc(rows_ready, 1)

                def copies(b, par, has_stage):
                    for gi in range(GPB):
                        g = b * GPB + gi
                        act.wait_ge(grp_ready, g + 1)
                        act.activation(slab[:, par, :, gi * G:(gi + 1) * G].rearrange("p t d -> p d t"),
                                       grp[:, gi % 4, 0:CODE].rearrange("p (d t) -> p d t", t=NT),
                                       ACT.Copy).then_inc(slab_part, 1)
                        if has_stage:
                            if gi == 0:
                                act.wait_ge(rows_out[1 - par], 32 * (b - 1 - (1 - par)))
                            for batch in SLICES[gi]:
                                rows(b - 1, 1 - par, batch)
                    if has_stage:
                        finish(b - 1, 1 - par)

                def last(st):
                    act.wait_ge(rows_out[0], 64 * (st // 2))
                    for batch in range(13):
                        rows(st, 0, batch)
                    finish(st, 0)
                all_blocks(act, copies, last)
            with act.Else():
                act.nop()

        @block.tensor
        def _(pe):
            fast = pe.value_load(flag_i[0:1, 0:1], min_val=0, max_val=1)
            pe.wait_ge(set_done, 1)
            with pe.If(fast == 1):
                pe.nop().then_inc(group_done, RING)
                pe.wait_ge(consts, 1)

                def turn(st, par, batch):
                    n = st * 13 + batch
                    pe.wait_ge(tp_used, n + 1)
                    tiles = tiles_of(batch)
                    bank = batch % 2 if par == 0 else (batch + 1) % 2
                    for j, t in enumerate(tiles):
                        pe.matmul(acc[:, par, 0:3 * D], slab[:, par, t, :],
                                  hpart[:, t, :, :].rearrange("p a f -> p (a f)"),
                                  start=(t == 0), stop=(t == NT - 1), skip_group_check=True)
                        last = pe.matmul(tp[:, bank, j * P:(j + 1) * P], slab[:, par, t, :], ident16[:, :],
                                         start=True, stop=True)
                    last.then_inc(tp_ready, 1)

                def products(b, par, has_stage):
                    for gi in range(GPB):
                        g, slot, s = b * GPB + gi, gi % RING, gi % 2
                        pe.wait_ge(oh_ready, g + 1)
                        if gi >= 4 or has_stage:
                            pe.wait_ge(slab_part, g - 3)
                        for k in range(K):
                            last = pe.matmul(grp[:, gi % 4, 0:CODE], lane_oh[:, s, k, :], code_oh[:, s, k, :],
                                             start=(k == 0), stop=(k == K - 1))
                        last.then_inc(grp_ready, 1)
                        if gi == 0 and has_stage:
                            pe.wait_ge(rows_ready, b - 1)
                        pe.wait_ge(attr_in[slot], 16 * (GPB // RING * b + gi // RING + 1))
                        rows32 = slice(gi // QG * 32, gi // QG * 32 + 32)
                        for k in range(K):
                            last = pe.matmul(acc[rows32, par, 3 * D:4 * D], dst_oh[:, s, k, :], attr_w[:, slot, k, :],
                                             start=(gi % QG == 0 and k == 0), stop=(gi % QG == QG - 1 and k == K - 1),
                                             skip_group_check=True)
                        last.then_inc(group_done, 1)
                        if has_stage:
                            if gi == FIRST_SLICE:
                                pe.wait_ge(slab_part, b * GPB)
                            for batch in SLICES[gi]:
                                turn(b - 1, 1 - par, batch)

                def last_stage(st):
                    pe.wait_ge(slab_part, NG)
                    for batch in range(13):
                        turn(st, 0, batch)
                all_blocks(pe, products, last_stage)
            with pe.Else():
                def match(t):
                    pe.wait_ge(g_keys_in, t + 1)
                    for c in range(2):
                        last = pe.matmul(grp[:, 0, c * P:(c + 1) * P], g_keys[:, c, :], ident[:, :],
                                         start=True, stop=True)
                    last.then_inc(g_keysT, 1)
                    pe.wait_ge(g_m_ready, t + 1)
                    pe.matmul(acc[:, 0, 0:D], g_eq[:, 0, :], g_attr[:, :], start=True, stop=True).then_inc(g_summed, 1)
                with pe.Fori(0, GTILES) as t:
                    match(t)
                match(GTILES)


def nodes(nc, xp_d, W1, b1, W2, b2, eps, qW, kW, vW, h_d, aggr_d, xh_d, parts_d, kp_d, qp_d, v_d, ident, ones):
    ctx = ExitStack()
    W = SC * P
    with ctx:
        sb, ps, sem = tools(nc, ctx)
        w1 = sb("w1", [D, HID], F32)
        w2 = sb("w2", [D, 2, D], F32)
        b1c = sb("b1c", [D, 2], F32)
        b2r = sb("b2r", [1, D], F32)
        qkv = sb("qkv", [D, 3, D], F32)
        eps1 = sb("eps1", [P, 1], F32)
        xt = sb("xt", [P, SC, D], F32)
        ht = sb("ht", [P, SC, D], F32)
        at = sb("at2", [P, SC, D], F32)
        aT = sb("aT", [D, W], F32)
        hid = sb("hid", [D, 2, W], F32)
        x1 = sb("x1", [P, SC, D], F32)
        cen = sb("cen", [P, SC, D], F32)
        sq = sb("sq2", [P, SC, D], F32)
        xh = sb("xh", [P, SC, D], F32)
        mean = sb("mean2", [P, SC], F32)
        rstd = sb("rstd2", [P, SC], F32)
        h2T = sb("h2T", [D, W], F32)
        parts = sb("parts", [D, 2, 3, W], BF16)
        left = sb("left", [D, W], F32)
        vt = sb("vt", [P, SC, HEADS, 32], F32)
        pa = ps("pa", [D, 2, 512])
        pb = ps("pb", [D, 2, 512])
        pm = ps("pm", [P, 2, 4, P])
        pt = ps("pt", [D, 2, 512])
        w_in, in_s = sem("w_in"), sem("in_s")
        hid_p, hid_s, mlp_p, var_s, std_s = sem("hid_p"), sem("hid_s"), sem("mlp_p"), sem("var_s"), sem("std_s")
        h2_s, h2T_p, h2T_s, q_p, k_p, v_p = sem("h2_s"), sem("h2T_p"), sem("h2T_s"), sem("q_p"), sem("k_p"), sem("v_p")
        v_s, parts_s, xh_s, step_s = sem("v_s"), sem("parts_s"), sem("xh_s"), sem("step_s")
        sp_out, pool_out, vt_set = sem("sp_out"), sem("pool_out"), sem("vt_set")
        x1_s, aT_p, aT_s, packed = sem("x1_s"), sem("aT_p"), sem("aT_s"), [sem("q_packed"), sem("k_packed")]
        NSP, NPOOL = 2, 2
        block = ctx.enter_context(nc.Block())
        halves = ((0, 4), (4, 3))

        def pack(eng, s, which):
            cols = bass.ds((s - 1) * W if isinstance(s, int) else eng.snap((s - 1) * W), W)
            eng.wait_ge(pool_out, 16 * NPOOL * s)
            for m in range(2):
                for slot, pair in enumerate(PAIRS[m]):
                    part = pair[1 - which]
                    eng.dma_start((qp_d, kp_d)[which][m][slot * DH:(slot + 1) * DH, :, cols],
                                  parts_d[which, :, part, cols].rearrange("(h r) n -> r h n", h=HEADS)
                                  ).then_inc(packed[which], 16)

        @block.sync
        def _(sp):
            sp.dma_start(w1[:, :], W1).then_inc(w_in, 16)
            sp.dma_start(w2[:, :, :], W2.rearrange("(a p) n -> p a n", a=2)).then_inc(w_in, 16)
            with nc.allow_non_contiguous_dma(reason="192 numbers"):
                sp.dma_start(b1c[:, :], b1.rearrange("(a p) -> p a", a=2)).then_inc(w_in, 16)
            sp.dma_start(b2r[:, :], b2.rearrange("(a n) -> a n", a=1)).then_inc(w_in, 16)
            for n, w in enumerate((qW, kW, vW)):
                sp.dma_start(qkv[:, n, :], w).then_inc(w_in, 16)
            sp.dma_start(eps1[:, :], eps.rearrange("(a n) -> a n", a=1).to_broadcast([P, 1])).then_inc(w_in, 16)

            def load(s):
                rows = bass.ds(s * W if isinstance(s, int) else sp.snap(s * W), W)
                if not isinstance(s, int):
                    sp.wait_ge(x1_s, s)
                sp.dma_start(xt[:, :, :], xp_d[rows, :].rearrange("(t p) f -> p t f", p=P)).then_inc(in_s, 16)
                sp.dma_start(ht[:, :, :], h_d[rows, :].rearrange("(t p) f -> p t f", p=P)).then_inc(in_s, 16)
                sp.dma_start(at[:, :, :], aggr_d[rows, :].rearrange("(t p) f -> p t f", p=P)).then_inc(in_s, 16)
            load(0)
            with sp.Fori(1, NS) as s:
                load(s)
                pack(sp, s, 0)
            pack(sp, NS, 0)
            sp.wait_ge(packed[0], 16 * 9 * NS)

        @block.gpsimd
        def _(pool):
            pool.memset(vt[:, :, :, :], 0.0).then_inc(vt_set, 1)
            pool.wait_ge(vt_set, 1)
            pool.memset(vt[:, :, :, DH:DH + 1], 1.0).then_inc(vt_set, 1)

            def store(s):
                rows = bass.ds(s * W if isinstance(s, int) else pool.snap(s * W), W)
                pool.wait_ge(xh_s, s + 1)
                pool.dma_start(xh_d[rows, :].rearrange("(t p) f -> p t f", p=P), xh[:, :, :]).then_inc(sp_out, 16)
                pool.wait_ge(v_s, 2 * (s + 1))
                pool.dma_start(v_d[bass.ds(s * SC, SC), :, :].rearrange("t p c -> p t c"),
                               vt[:, :, :, :].rearrange("p t h c -> p t (h c)")).then_inc(sp_out, 16)
                for i in range(2):
                    pool.wait_ge(parts_s, 2 * s + i + 1)
                    pool.dma_start(parts_d[i, :, :, rows], parts[:, i, :, :]).then_inc(pool_out, 16)
            store(0)
            with pool.Fori(1, NS) as s:
                pack(pool, s, 1)
                store(s)
            pack(pool, NS, 1)
            pool.wait_ge(sp_out, 16 * NSP * NS)
            pool.wait_ge(packed[1], 16 * 9 * NS)

        @block.tensor
        def _(pe):
            pe.wait_ge(w_in, 128)
            with pe.Fori(0, NS) as s:
                pe.wait_ge(in_s, 48 * (s + 1))
                for c, (first, n) in enumerate(halves):
                    for j in range(n):
                        last = pe.transpose(pt[:, c, j * P:(j + 1) * P], at[:, first + j, :], ident[:, :])
                    last.then_inc(aT_p, 1)
                pe.wait_ge(parts_s, 2 * s)
                pe.wait_ge(aT_s, 2 * (s + 1))
                for a, bank in enumerate((pa, pb)):
                    for c in range(2):
                        pe.matmul(bank[:, c, 0:CW], w1[:, a * D:(a + 1) * D], aT[:, c * CW:(c + 1) * CW],
                                  start=True, stop=True).then_inc(hid_p, 1)
                pe.wait_ge(hid_s, 4 * (s + 1))
                pe.wait_ge(v_s, 2 * s)
                for c, (first, n) in enumerate(halves):
                    for j in range(n):
                        o, t = pm[:, c, j, 0:D], first + j
                        pe.matmul(o, ones[0:1, :], b2r[:, :], start=True, stop=False)
                        pe.matmul(o, hid[:, 0, t * P:(t + 1) * P], w2[:, 0, :], start=False, stop=False)
                        last = pe.matmul(o, hid[:, 1, t * P:(t + 1) * P], w2[:, 1, :], start=False, stop=True)
                    last.then_inc(mlp_p, 1)
                pe.wait_ge(h2_s, s + 1)
                for c, (first, n) in enumerate(halves):
                    for j in range(n):
                        last = pe.transpose(pt[:, c, j * P:(j + 1) * P], cen[:, first + j, :], ident[:, :])
                    last.then_inc(h2T_p, 1)
                pe.wait_ge(h2T_s, 2 * (s + 1))
                for n, (bank, done) in enumerate(((pa, q_p), (pb, k_p))):
                    for c in range(2):
                        last = pe.matmul(bank[:, c, 0:CW], qkv[:, n, :], h2T[:, c * CW:(c + 1) * CW],
                                         start=True, stop=True)
                    last.then_inc(done, 1)
                for c, (first, n) in enumerate(halves):
                    for j in range(n):
                        last = pe.matmul(pm[:, c, j, 0:D], h2T[:, (first + j) * P:(first + j + 1) * P],
                                         qkv[:, 2, :], start=True, stop=True)
                    last.then_inc(v_p, 1)

        @block.scalar
        def _(act):
            act.wait_ge(w_in, 128)
            act.wait_ge(vt_set, 2)
            with act.Fori(0, NS) as s:
                for c, (first, n) in enumerate(halves):
                    act.wait_ge(aT_p, 2 * s + c + 1)
                    act.activation(aT[:, first * P:(first + n) * P], pt[:, c, 0:n * P], ACT.Copy).then_inc(aT_s, 1)
                for a, bank in enumerate((pa, pb)):
                    for c in range(2):
                        act.wait_ge(hid_p, 4 * s + 2 * a + c + 1)
                        act.activation(hid[:, a, c * CW:(c + 1) * CW], bank[:, c, 0:CW], ACT.Relu,
                                       bias=b1c[:, a:a + 1]).then_inc(hid_s, 1)
                act.wait_ge(var_s, s + 1)
                act.activation(rstd[:, :], rstd[:, :], ACT.Sqrt).then_inc(std_s, 1)
                for c, (first, n) in enumerate(halves):
                    act.wait_ge(h2T_p, 2 * s + c + 1)
                    act.activation(h2T[:, first * P:(first + n) * P], pt[:, c, 0:n * P], ACT.Copy).then_inc(h2T_s, 1)
                act.wait_ge(sp_out, 16 * NSP * s)
                for c, (first, n) in enumerate(halves):
                    act.wait_ge(v_p, 2 * s + c + 1)
                    act.activation(vt[:, first:first + n, :, 0:DH],
                                   pm[:, c, 0:n, 0:D].rearrange("p t (h d) -> p t h d", h=HEADS),
                                   ACT.Copy).then_inc(v_s, 1)

        @block.vector
        def _(dve):
            dve.wait_ge(w_in, 128)
            dve.tensor_scalar(eps1[:, :], eps1[:, :], 1.0, None, ALU.add).then_inc(step_s, 1)
            dve.wait_ge(step_s, 1)
            with dve.Fori(0, NS) as s:
                STEPS = 17
                n = [0]

                def step(ins):
                    n[0] += 1
                    ins.then_inc(step_s, 1)
                    dve.wait_ge(step_s, STEPS * s + n[0] + 1)
                dve.wait_ge(in_s, 48 * (s + 1))
                dve.wait_ge(mlp_p, 2 * (s + 1))
                for c, (first, m) in enumerate(halves):
                    step(dve.scalar_tensor_tensor(out=x1[:, first:first + m, :], in0=ht[:, first:first + m, :],
                                                  scalar=eps1[:, 0:1], in1=pm[:, c, 0:m, 0:D],
                                                  op0=ALU.mult, op1=ALU.add))
                dve.tensor_tensor(x1[:, :, :], x1[:, :, :], xt[:, :, :], ALU.add).then_inc(x1_s, 1)
                dve.wait_ge(x1_s, s + 1)
                step(dve.tensor_reduce(mean[:, :], x1[:, :, :], axis=AX.X, op=ALU.add))
                step(dve.tensor_scalar(mean[:, :], mean[:, :], 1.0 / D, None, ALU.mult))
                step(dve.tensor_tensor(cen[:, :, :], x1[:, :, :], mean[:, :].unsqueeze(2).to_broadcast([P, SC, D]),
                                       ALU.subtract))
                step(dve.tensor_tensor(sq[:, :, :], cen[:, :, :], cen[:, :, :], ALU.mult))
                step(dve.tensor_reduce(rstd[:, :], sq[:, :, :], axis=AX.X, op=ALU.add))
                dve.tensor_scalar(rstd[:, :], rstd[:, :], 1.0 / D, LN_EPS, ALU.mult, ALU.add).then_inc(var_s, 1)
                dve.wait_ge(std_s, s + 1)
                step(dve.reciprocal(rstd[:, :], rstd[:, :]))
                step(dve.tensor_tensor(cen[:, :, :], cen[:, :, :],
                                       rstd[:, :].unsqueeze(2).to_broadcast([P, SC, D]), ALU.mult))
                dve.tensor_scalar(cen[:, :, :], cen[:, :, :], 0.0, None, ALU.max).then_inc(h2_s, 1)
                dve.wait_ge(h2_s, s + 1)
                dve.wait_ge(sp_out, 16 * NSP * s)
                dve.wait_ge(pool_out, 16 * NPOOL * s)
                dve.tensor_tensor(xh[:, :, :], x1[:, :, :], cen[:, :, :], ALU.add).then_inc(xh_s, 1)
                for i, (bank, done) in enumerate(((pa, q_p), (pb, k_p))):
                    dve.wait_ge(done, s + 1)
                    p3 = parts[:, i, :, :].rearrange("p a (c n) -> p a c n", c=2)
                    l2 = left[:, :].rearrange("p (c n) -> p c n", c=2)
                    step(dve.tensor_copy(p3[:, 0], bank[:, :, 0:CW]))
                    step(dve.tensor_tensor(l2, bank[:, :, 0:CW], p3[:, 0], ALU.subtract))
                    step(dve.tensor_copy(parts[:, i, 1, :], left[:, :]))
                    step(dve.tensor_tensor(left[:, :], left[:, :], parts[:, i, 1, :], ALU.subtract))
                    dve.tensor_copy(parts[:, i, 2, :], left[:, :]).then_inc(parts_s, 1)
                assert n[0] == STEPS, n


def attention(nc, count_d, xh_d, kp_d, qp_d, v_d, ident, out):
    ctx = ExitStack()
    GJ = 7
    FIRST = [0] + [GJ + (GJ - 1) * k for k in range(8)]
    GROUPS = len(FIRST) - 1
    assert FIRST[-1] == NT
    R = 3
    CREDIT = R
    with ctx:
        sb, ps, sem = tools(nc, ctx)
        cnt = sb("counts", [P, 2, GJ, CW], F32)
        kb = [sb(f"kb{m}", [ROWS[m], 2, HEADS, GJ * P], BF16) for m in range(2)]
        vb = sb("vb", [P, 2, GJ, P], F32)
        qb = [sb(f"qb{m}", [ROWS[m], HEADS, CW], BF16) for m in range(2)]
        wa = sb("wa", [P, R + 1, 2, CW], F32)
        wb = sb("wb", [P, R + 1, 2, CW], F32)
        ten = sb("ten", [P, 1], F32)
        accs = sb("accs", [P, CW], F32)
        xh = sb("xh3", [CT, 4, D], F32)
        den = sb("den", [CT, 4, HEADS, 1], F32)
        res = sb("res", [CT, 4, HEADS, DH], F32)
        sc = ps("sc", [P, 3, 2, 512])
        acc = ps("acc3", [P, 512])
        tq = ps("tq", [CT, 4, P])
        q_in, xh_in = sem("q_in"), sem("xh_in")
        t_in = [sem("t_in0"), sem("t_in1")]
        sc_a, sc_b, clip_a, clip_b = sem("sc_a"), sem("sc_b"), sem("clip_a"), sem("clip_b")
        exp_a, exp_b, w_a, w_b, pv_done = sem("exp_a"), sem("exp_b"), sem("w_a"), sem("w_b"), sem("pv_done")
        ten_set, acc_out, tq_ready, den_s, o_ready, o_out = (sem(n) for n in (
            "ten_set", "acc_out", "tq_ready", "den_s", "o_ready", "o_out"))
        rows = count_d[0:NP * NP, :].rearrange("(r c) o -> r (c o)", c=NP)
        block = ctx.enter_context(nc.Block())

        def ring(t):
            return R if t == NT - 1 else t % R

        def vector_clips(t):
            return t % 3 == 2

        def place(t):
            k = max(k for k in range(GROUPS) if FIRST[k] <= t)
            return k, k % 2, t - FIRST[k]

        @block.sync
        def _(sp):
            def chunk(c):
                cols = bass.ds(c * CW if isinstance(c, int) else sp.snap(c * CW), CW)
                if not isinstance(c, int):
                    sp.wait_ge(sc_a, c * NT)
                    sp.wait_ge(sc_b, c * NT)
                for m in range(2):
                    sp.dma_start(qb[m][:, :, :], qp_d[m][:, :, cols]).then_inc(q_in, 16)
                for k in range(GROUPS):
                    first, n = FIRST[k], FIRST[k + 1] - FIRST[k]
                    if k >= 2:
                        sp.wait_ge(pv_done, c * NT + FIRST[k - 1] + CREDIT)
                    elif not isinstance(c, int):
                        sp.wait_ge(pv_done, (c - 1) * NT + FIRST[GROUPS + k - 1] + CREDIT)
                    s = k % 2
                    for m in range(2):
                        sp.dma_start(kb[m][:, s, :, 0:n * P], kp_d[m][:, :, first * P:(first + n) * P]
                                     ).then_inc(t_in[s], 16)
                    sp.dma_start(cnt[:, s, 0:n, :], rows[first * P:(first + n) * P, cols]
                                 .rearrange("(j p) s -> p j s", p=P)).then_inc(t_in[s], 16)
                    sp.dma_start(vb[:, s, 0:n, :], v_d[first:first + n, :, :].rearrange("j p c -> p j c")
                                 ).then_inc(t_in[s], 16)
                    if k == 2:
                        if not isinstance(c, int):
                            store(c - 1, CT)
                        sp.dma_start(xh[:, :, :], xh_d[cols, :].rearrange("(t p) f -> p t f", p=CT)
                                     ).then_inc(xh_in, 16)

            def store(c, last):
                sp.wait_ge(o_ready, c + 1)
                res3 = res[:, :, :, :].rearrange("p t h d -> p t (h d)")
                if last == CT:
                    sp.dma_start(out[bass.ds(c * CW, CW), :].rearrange("(t p) f -> p t f", p=CT),
                                 res3).then_inc(o_out, 16)
                    sp.wait_ge(o_out, 16 * (c + 1))
                else:
                    sp.dma_start(out[c * CW:c * CW + 3 * CT, :].rearrange("(t p) f -> p t f", p=CT),
                                 res3[:, 0:3, :]).then_inc(o_out, 16)
                    sp.dma_start(out[c * CW + 3 * CT:N, :], res3[0:last, 3, :]).then_inc(o_out, 16)
                    sp.wait_ge(o_out, 16 * (c + 2))
            chunk(0)
            with sp.Fori(1, NC_) as c:
                chunk(c)
            store(NC_ - 1, N - (NC_ - 1) * CW - 3 * CT)

        @block.tensor
        def _(pe):
            pe.nop().then_inc(pv_done, CREDIT)

            def scores(c, t):
                _, slot, j = place(t)
                for pair, done in ((0, sc_a), (1, sc_b)):
                    for h in range(2):
                        for m in range(2):
                            last = pe.matmul(sc[:, (2 * t + pair) % 3, h, 0:CW], kb[m][:, slot, 2 * pair + h, j * P:(j + 1) * P],
                                             qb[m][:, 2 * pair + h, :], start=(m == 0), stop=(m == 1))
                    last.then_inc(done, 1)

            def weigh(c, t):
                _, slot, j = place(t)
                for pair, w, ready in ((1, wb, w_b), (0, wa, w_a)):
                    pe.wait_ge(ready, c * NT + t + 1)
                    for h in range(2):
                        q = 2 * pair + h
                        last = pe.matmul(acc[32 * q:32 * q + 32, 0:CW], vb[:, slot, j, 32 * q:32 * q + 32],
                                         w[:, ring(t), h, :], start=(t == 0), stop=(t == NT - 1))
                last.then_inc(pv_done, 1)

            with pe.Fori(0, NC_) as c:
                pe.wait_ge(q_in, 32 * (c + 1))
                for t in range(NT + 1):
                    if t < NT:
                        k, slot, j = place(t)
                        if j == 0:
                            pe.wait_ge(t_in[slot], 64 * (GROUPS // 2) * c + 64 * (k // 2 + 1))
                        if t == 0:
                            pe.wait_ge(clip_a, c * NT)
                            pe.wait_ge(clip_b, c * NT)
                        else:
                            pe.wait_ge(clip_a, c * NT + t)
                            if t >= 2:
                                pe.wait_ge(clip_b, c * NT + t - 1)
                        scores(c, t)
                    if t == 2:
                        pe.wait_ge(acc_out, c)
                    if t >= 2:
                        weigh(c, t - 2)
                weigh(c, NT - 1)
                pe.wait_ge(acc_out, c + 1)
                pe.wait_ge(o_ready, c)
                for i in range(4):
                    last = pe.transpose(tq[:, i, :], accs[:, i * CT:(i + 1) * CT], ident[:, :])
                last.then_inc(tq_ready, 1)

        @block.scalar
        def _(act):
            act.wait_ge(ten_set, 1)
            with act.Fori(0, NC_) as c:
                for t in range(NT):
                    n, r = c * NT + t, ring(t)
                    if not vector_clips(t):
                        act.wait_ge(sc_b, n + 1)
                        act.wait_ge(pv_done, n - 2 + CREDIT)
                        act.activation(wb[:, r, :, :], sc[:, (2 * t + 1) % 3, :, 0:CW], ACT.Relu,
                                       bias=ten[:, 0:1], scale=-1.0).then_inc(clip_b, 1)
                        act.wait_ge(clip_b, n + 1)
                        act.activation(wb[:, r, :, :], wb[:, r, :, :], ACT.Exp,
                                       bias=ten[:, 0:1], scale=-1.0).then_inc(exp_b, 1)
                    else:
                        act.wait_ge(clip_b, n + 1)
                        act.activation(wb[:, r, :, :], wb[:, r, :, :], ACT.Exp).then_inc(exp_b, 1)
                    act.wait_ge(clip_a, n + 1)
                    act.activation(wa[:, r, :, :], wa[:, r, :, :], ACT.Exp).then_inc(exp_a, 1)

        @block.gpsimd
        def _(pool):
            pool.memset(ten[:, :], CLIP).then_inc(ten_set, 1)
            with pool.Fori(0, NC_) as c:
                for t in range(NT):
                    n, r = c * NT + t, ring(t)
                    k, slot, j = place(t)
                    if j == 0:
                        pool.wait_ge(t_in[slot], 64 * (GROUPS // 2) * c + 64 * (k // 2 + 1))
                    pool.wait_ge(exp_a, n + 1)
                    pool.tensor_tensor(wa[:, r, :, :], wa[:, r, :, :],
                                       cnt[:, slot, j, :].unsqueeze(1).to_broadcast([P, 2, CW]),
                                       ALU.mult).then_inc(w_a, 1)

        @block.vector
        def _(dve):
            with dve.Fori(0, NC_) as c:
                for t in range(NT):
                    n, r = c * NT + t, ring(t)
                    k, slot, j = place(t)
                    if j == 0:
                        dve.wait_ge(t_in[slot], 64 * (GROUPS // 2) * c + 64 * (k // 2 + 1))
                    dve.wait_ge(sc_a, n + 1)
                    dve.wait_ge(pv_done, n - 2 + CREDIT)
                    dve.tensor_scalar(wa[:, r, :, :], sc[:, (2 * t) % 3, :, 0:CW], CLIP, -CLIP,
                                      ALU.min, ALU.max).then_inc(clip_a, 1)
                    if vector_clips(t):
                        dve.wait_ge(sc_b, n + 1)
                        dve.tensor_scalar(wb[:, r, :, :], sc[:, (2 * t + 1) % 3, :, 0:CW], CLIP, -CLIP,
                                          ALU.min, ALU.max).then_inc(clip_b, 1)
                    dve.wait_ge(exp_b, n + 1)
                    dve.scalar_tensor_tensor(out=wb[:, r, :, :], in0=wb[:, r, :, :], scalar=EXP_LO,
                                             in1=cnt[:, slot, j, :].unsqueeze(1).to_broadcast([P, 2, CW]),
                                             op0=ALU.max, op1=ALU.mult).then_inc(w_b, 1)
                dve.wait_ge(pv_done, (c + 1) * NT + CREDIT)
                dve.wait_ge(tq_ready, c)
                dve.tensor_copy(accs[:, :], acc[:, 0:CW]).then_inc(acc_out, 1)
                dve.wait_ge(tq_ready, c + 1)
                num = tq[:, :, :].rearrange("p t (h d) -> p t h d", h=HEADS)
                dve.tensor_scalar(den[:, :, :, :], num[:, :, :, DH:DH + 1], 1e-8, None, ALU.add).then_inc(den_s, 1)
                dve.wait_ge(den_s, 3 * c + 1)
                dve.reciprocal(den[:, :, :, :], den[:, :, :, :]).then_inc(den_s, 1)
                dve.wait_ge(den_s, 3 * c + 2)
                dve.wait_ge(o_out, 16 * c)
                dve.tensor_tensor(res[:, :, :, :], num[:, :, :, 0:DH],
                                  den[:, :, :, :].to_broadcast([CT, 4, HEADS, DH]), ALU.mult).then_inc(den_s, 1)
                dve.wait_ge(den_s, 3 * c + 3)
                dve.wait_ge(xh_in, 16 * (c + 1))
                dve.tensor_tensor(res[:, :, :, :], res[:, :, :, :],
                                  xh[:, :, :].rearrange("p t (h d) -> p t h d", h=HEADS), ALU.add).then_inc(o_ready, 1)


_INS = ["x", "src", "dst", "edge_attr_96", "L0_gnn_W1", "L0_gnn_b1", "L0_gnn_W2", "L0_gnn_b2", "L0_gnn_eps",
        "L1_gnn_qW", "L1_gnn_kW", "L1_gnn_vW"]


def kernel(**inputs):
    import numpy as _np
    import concourse.bacc as _bacc
    from concourse import mybir as _mybir
    from concourse.bass_utils import run_bass_kernel_spmd as _run

    nc = _bacc.Bacc("TRN2", target_bir_lowering=False, num_devices=1)
    arrays, args = {}, []
    for name in _INS:
        a = _np.ascontiguousarray(inputs[name])
        arrays[f"in_{name}"] = a
        args.append(nc.dram_tensor(f"in_{name}", a.shape, _mybir.dt.from_np(a.dtype), kind="ExternalInput").ap())
    args.append(nc.dram_tensor("out_x", (N, D), _mybir.dt.float32, kind="ExternalOutput").ap())
    build(nc, *args)
    r = _run(nc, [arrays], core_ids=[0])
    return r.results[0]["out_x"]
```

```python
from contextlib import ExitStack

import numpy as np
import concourse.bass as bass
from concourse import mybir
from concourse.alu_op_type import AluOpType as ALU

F32 = mybir.dt.float32
F16 = mybir.dt.float16
BF16 = mybir.dt.bfloat16
I32 = mybir.dt.int32
ACT = mybir.ActivationFunctionType
AX = mybir.AxisListType

P = 128
N = 6250
D = 96
HID = 192
HEADS, DH = 4, 24
E = 206250
NT = -(-N // P)
NP = NT * P
TAIL = N - (NT - 1) * P
EP, EC = 110, 1875
G = 8
NG = NP // G
GPB = P // G
K = 3
WIN = K * P
QG = 32 // G
RING = 16
AHEAD = 8
CODE = G * NT
GP = 98
GQ = NG // GP
SC = 7
NS = NT // SC
CW = 448
NC_ = NP // CW
CT = CW // 4
LN_EPS = 1e-5
CLIP = 10.0
EXP_HI = float(np.exp(10.0))
EXP_LO = float(np.exp(-10.0))
GTILES = E // P
GREST = E - GTILES * P
PAIRS = [[(0, 0), (0, 1), (1, 0), (1, 1), (0, 2)], [(2, 0), (1, 2), (2, 1), (2, 2)]]
ROWS = [len(p) * DH for p in PAIRS]


def build(nc, x, src, dst, attr, W1, b1, W2, b2, eps, qW, kW, vW, out):
    ctx = ExitStack()
    with ctx:
        def dram(name, shape, dt):
            return nc.dram_tensor(name, shape, dt).ap()

        count_d = dram("count_d", [(NP + 1) * NP, 1], F32)
        h_d = dram("h_d", [NP, D], F32)
        xp_d = dram("xp_d", [NP, D], F32)
        aggr_d = dram("aggr_d", [NP + P, D], F32)
        start_d = dram("start_d", [1, NG + 1], F32)
        rec_d = dram("rec_d", [E, 4], F32)
        xh_d = dram("xh_d", [NP, D], F32)
        parts_d = dram("parts_d", [2, D, 3, NP], BF16)
        qp_d = [dram(f"q{m}_d", [ROWS[m], HEADS, NP], BF16) for m in range(2)]

        flag_i = ctx.enter_context(nc.sbuf_tensor("flag_i", [1, 1], I32))
        start_i = ctx.enter_context(nc.sbuf_tensor("start_i", [1, NG], I32))
        ident = ctx.enter_context(nc.sbuf_tensor("ident", [P, P], F32))
        ones = ctx.enter_context(nc.sbuf_tensor("ones", [P, P], F32))

        ids_and_norm(nc, x, src, dst, xp_d, h_d, start_d, rec_d, aggr_d, flag_i, start_i, ident, ones)
        edges(nc, src, dst, attr, h_d, aggr_d, rec_d, count_d, flag_i, start_i, ident, ones)
        kb = [ctx.enter_context(nc.sbuf_tensor(f"kb{m}", [ROWS[m], HEADS, NP], BF16)) for m in range(2)]
        vb = ctx.enter_context(nc.sbuf_tensor("vb", [P, NT, HEADS, 32], F32))
        nodes(nc, xp_d, W1, b1, W2, b2, eps, qW, kW, vW, h_d, aggr_d, xh_d, parts_d, kb, qp_d, vb, ident, ones)
        attention(nc, count_d, xh_d, kb, qp_d, vb, ident, out)


def tools(nc, ctx):
    def sb(name, shape, dt):
        return ctx.enter_context(nc.sbuf_tensor(name, shape, dt))

    def ps(name, shape, dt=F32):
        return ctx.enter_context(nc.psum_tensor(name, shape, dt))

    def sem(name):
        return ctx.enter_context(nc.semaphore(name))

    return sb, ps, sem


def linker(eng, done):
    n = [0]

    def link(ins):
        n[0] += 1
        ins.then_inc(done, 1)
        eng.wait_ge(done, n[0])

    return link


def ids_and_norm(nc, x, src, dst, xp_d, h_d, start_d, rec_d, aggr_d, flag_i, start_i, ident, ones):
    ctx = ExitStack()
    with ctx:
        sb, ps, sem = tools(nc, ctx)
        xn = sb("xn", [P, NT, D], F32)
        sq = sb("sq", [P, NT, D], F32)
        mean = sb("mean", [P, NT], F32)
        rstd = sb("rstd", [P, NT], F32)
        srct = sb("srct", [EP, EC], I32)
        dstt = sb("dstt", [EP, EC], I32)
        part = sb("part", [EP, EC], I32)
        rec = sb("rec", [EP, EC, 4], F32)
        nexti = sb("nexti", [EP, 1], I32)
        nextf = sb("nextf", [EP, 1], F32)
        lasti = sb("lasti", [1, EP], I32)
        lastf = sb("lastf", [1, EP], F32)
        bad = sb("bad", [EP, 2], F32)
        lastb = sb("lastb", [GP, EP], F32)
        less = sb("less", [GP, EC], F32)
        row = sb("row", [GP, GQ, EC], I32)
        thr_i = sb("thr_i", [GP, GQ], I32)
        thr = sb("thr", [GP, GQ], F32)
        cnt = sb("cnt", [GP, GQ], F32)
        at = sb("at", [GP, GQ], F32)
        at_i = sb("at_i", [GP, GQ], I32)
        start = sb("start", [GP, GQ], F32)
        srow = sb("srow", [1, NG + 1], F32)
        diff = sb("diff", [1, NG], F32)
        fl = sb("fl", [1, 4], F32)
        lastp = ps("lastp", [GP, EP])
        badp = ps("badp", [1, 2])
        x_out = sem("x_out")
        x_in, ids_in, small_in, bnd_in = sem("x_in"), sem("ids_in"), sem("small_in"), sem("bnd_in")
        memset_done, consts, pool_done = sem("memset_done"), sem("consts"), sem("pool_done")
        dve_done, sqrt_in, sqrt_out = sem("dve_done"), sem("sqrt_in"), sem("sqrt_out")
        lastf_ready, lastp_ready = sem("lastf_ready"), sem("lastp_ready")
        bad_ready, badp_ready = sem("bad_ready"), sem("badp_ready")
        at_ready, rows_in = sem("at_ready"), sem("rows_in")
        start_ready, start_out, srow_in = sem("start_ready"), sem("start_out"), sem("srow_in")
        h_ready, rec_ready, h_out, rec_out = sem("h_ready"), sem("rec_ready"), sem("h_out"), sem("rec_out")
        block = ctx.enter_context(nc.Block())

        @block.sync
        def _(sp):
            sp.dma_start(dstt[:], dst.rearrange("(p c) -> p c", c=EC)).then_inc(ids_in, 16)
            sp.dma_start(srct[:], src.rearrange("(p c) -> p c", c=EC)).then_inc(ids_in, 16)
            d2 = dst.rearrange("(p c) -> p c", c=EC)
            with nc.allow_non_contiguous_dma(reason="110 ids"):
                sp.dma_start(nexti[0:EP - 1, :], d2[1:EP, 0:1]).then_inc(small_in, 16)
            with nc.allow_non_contiguous_dma(reason="110 ids"):
                sp.dma_start(lasti[:, :], d2[:, EC - 1:EC].rearrange("p c -> c p")).then_inc(bnd_in, 16)
            sp.wait_ge(start_ready, 1)
            for q in range(GQ):
                with nc.allow_non_contiguous_dma(reason="98 numbers"):
                    sp.dma_start(start_d[0:1, q * GP:(q + 1) * GP].rearrange("a p -> p a"),
                                 start[:, q:q + 1]).then_inc(start_out, 16)
            sp.wait_ge(start_out, 16 * GQ)
            sp.dma_start(srow[:, 0:NG], start_d[:, 0:NG]).then_inc(srow_in, 16)
            sp.wait_ge(rec_ready, 1)
            sp.dma_start(rec_d.rearrange("(p c) k -> p c k", c=EC), rec[:, :, :]).then_inc(rec_out, 16)
            sp.wait_ge(rec_out, 16)

        @block.scalar
        def _(act):
            act.wait_ge(memset_done, 1)
            act.dma_start(xn[:, 0:NT - 1, :],
                          x[0:(NT - 1) * P, :].rearrange("(t p) f -> p t f", p=P)).then_inc(x_in, 16)
            act.dma_start(xn[0:TAIL, NT - 1, :], x[(NT - 1) * P:N, :]).then_inc(x_in, 16)
            act.wait_ge(x_in, 32)
            act.dma_start(xp_d.rearrange("(t p) f -> p t f", p=P), xn[:, :, :]).then_inc(x_out, 16)
            act.wait_ge(sqrt_in, 1)
            act.activation(rstd[:, :], rstd[:, :], ACT.Sqrt).then_inc(sqrt_out, 1)
            act.wait_ge(h_ready, 1)
            act.dma_start(h_d.rearrange("(t p) f -> p t f", p=P), xn[:, :, :]).then_inc(h_out, 16)
            act.wait_ge(h_out, 16)

        @block.gpsimd
        def _(pool):
            pool.memset(ident[:], 0.0).then_inc(pool_done, 1)
            pool.memset(ones[:], 1.0).then_inc(consts, 1)
            pool.iota(thr_i[:], pattern=[[GP * G, GQ]], base=0, channel_multiplier=G).then_inc(consts, 1)
            pool.wait_ge(pool_done, 1)
            pool.affine_select(out=ident[:], in_=ident[:], compare_op=ALU.not_equal, fill=1.0, base=0,
                               pattern=[[-1, P]], channel_multiplier=1).then_inc(consts, 1)
            pool.wait_ge(at_ready, 1)
            for q in range(GQ):
                pool.indirect_dma_start(
                    out=row[:, q, :], out_offset=None, in_=dst.rearrange("(p c) -> p c", c=EC),
                    in_offset=bass.IndirectOffsetOnAxis(ap=at_i[:, q:q + 1], axis=0),
                ).then_inc(rows_in, 16)
            pool.wait_ge(rows_in, 16 * GQ)

        @block.tensor
        def _(pe):
            pe.wait_ge(consts, 3)
            pe.wait_ge(lastf_ready, 1)
            pe.matmul(lastp[:, :], ones[0:1, 0:GP], lastf[:, :], start=True, stop=True).then_inc(lastp_ready, 1)
            pe.wait_ge(bad_ready, 1)
            pe.matmul(badp[:, 0:1], ones[0:EP, 0:1], bad[:, 0:1], start=True, stop=True).then_inc(badp_ready, 1)

        @block.vector
        def _(dve):
            link = linker(dve, dve_done)
            dve.memset(xn[:, NT - 1, :], 0.0).then_inc(memset_done, 1)
            dve.memset(nextf[:, :], float(NP))
            link(dve.memset(srow[:, NG:NG + 1], float(E)))
            dve.wait_ge(consts, 3)
            link(dve.tensor_copy(thr[:, :], thr_i[:, :]))
            dve.wait_ge(bnd_in, 16)
            dve.tensor_copy(lastf[:, :], lasti[:, :]).then_inc(lastf_ready, 1)
            dve.wait_ge(lastp_ready, 1)
            link(dve.tensor_copy(lastb[:, :], lastp[:, :]))
            for q in range(GQ):
                link(dve.tensor_scalar(less[:, 0:EP], lastb[:, :], thr[:, q:q + 1], None, ALU.is_lt))
                link(dve.tensor_reduce(at[:, q:q + 1], less[:, 0:EP], axis=AX.X, op=ALU.add))
            link(dve.tensor_scalar(at[:, :], at[:, :], float(EP - 1), None, ALU.min))
            dve.tensor_copy(at_i[:, :], at[:, :]).then_inc(at_ready, 1)
            dve.wait_ge(ids_in, 32)
            link(dve.tensor_copy(rec[:, :, 1], dstt[:, :]))
            link(dve.tensor_scalar(part[:, :], srct[:, :], 7, None, ALU.logical_shift_right))
            link(dve.scalar_tensor_tensor(out=rec[:, :, 0], in0=rec[:, :, 1], scalar=float(NT), in1=part[:, :],
                                          op0=ALU.mult, op1=ALU.add))
            link(dve.tensor_scalar(part[:, :], srct[:, :], P - 1, None, ALU.bitwise_and))
            link(dve.tensor_copy(rec[:, :, 3], part[:, :]))
            link(dve.tensor_copy(rec[:, :, 2], srct[:, :]))
            dve.tensor_copy(bad[:, 1:2], rec[:, 0, 3:4]).then_inc(rec_ready, 1)
            dve.wait_ge(small_in, 16)
            link(dve.tensor_copy(nextf[0:EP - 1, :], nexti[0:EP - 1, :]))
            lt = sq[0:EP, :, :].rearrange("p a b -> p (a b)")[:, 0:EC]
            link(dve.tensor_tensor(lt[:, 0:EC - 1], rec[:, 0:EC - 1, 1], rec[:, 1:EC, 1], ALU.is_gt))
            link(dve.tensor_tensor(lt[:, EC - 1:EC], rec[:, EC - 1, 1:2], nextf[:, :], ALU.is_gt))
            dve.tensor_reduce(bad[:, 0:1], lt, axis=AX.X, op=ALU.add).then_inc(bad_ready, 1)
            dve.wait_ge(rows_in, 16 * GQ)
            for q in range(GQ):
                link(dve.tensor_scalar(less[:, :], row[:, q, :], thr[:, q:q + 1], None, ALU.is_lt))
                link(dve.tensor_reduce(cnt[:, q:q + 1], less[:, :], axis=AX.X, op=ALU.add))
            dve.scalar_tensor_tensor(out=start[:, :], in0=at[:, :], scalar=float(EC), in1=cnt[:, :],
                                     op0=ALU.mult, op1=ALU.add).then_inc(start_ready, 1)
            dve.wait_ge(srow_in, 16)
            link(dve.tensor_tensor(diff[:, :], srow[:, 1:NG + 1], srow[:, 0:NG], ALU.subtract))
            link(dve.tensor_reduce(fl[:, 0:1], diff[:, :], axis=AX.X, op=ALU.max))
            link(dve.tensor_scalar(fl[:, 1:2], fl[:, 0:1], float(WIN), None, ALU.is_le))
            dve.wait_ge(badp_ready, 1)
            link(dve.tensor_scalar(fl[:, 2:3], badp[:, 0:1], 0.0, None, ALU.is_equal))
            link(dve.tensor_tensor(fl[:, 3:4], fl[:, 1:2], fl[:, 2:3], ALU.mult))
            link(dve.tensor_copy(flag_i[:, :], fl[:, 3:4]))
            link(dve.tensor_scalar(srow[:, :], srow[:, :], float(E - WIN), None, ALU.min))
            link(dve.tensor_copy(start_i[:, :], srow[:, 0:NG]))
            dve.wait_ge(x_in, 32)
            link(dve.tensor_reduce(mean[:, :], xn[:, :, :], axis=AX.X, op=ALU.add))
            dve.wait_ge(x_out, 16)
            link(dve.tensor_scalar(mean[:, :], mean[:, :], 1.0 / D, None, ALU.mult))
            link(dve.tensor_tensor(xn[:, :, :], xn[:, :, :], mean[:, :].unsqueeze(2).to_broadcast([P, NT, D]),
                                   ALU.subtract))
            link(dve.tensor_tensor(sq[:, :, :], xn[:, :, :], xn[:, :, :], ALU.mult))
            link(dve.tensor_reduce(rstd[:, :], sq[:, :, :], axis=AX.X, op=ALU.add))
            dve.tensor_scalar(rstd[:, :], rstd[:, :], 1.0 / D, LN_EPS, ALU.mult, ALU.add).then_inc(sqrt_in, 1)
            dve.wait_ge(sqrt_out, 1)
            link(dve.reciprocal(rstd[:, :], rstd[:, :]))
            link(dve.tensor_tensor(xn[:, :, :], xn[:, :, :], rstd[:, :].unsqueeze(2).to_broadcast([P, NT, D]),
                                   ALU.mult))
            dve.tensor_scalar(xn[:, :, :], xn[:, :, :], 0.0, None, ALU.max).then_inc(h_ready, 1)


def edges(nc, src, dst, attr, h_d, aggr_d, rec_d, count_d, flag_i, start_i, ident, ones):
    count_rows = count_d[0:NP * NP, :].rearrange("(r c) o -> r (c o)", c=NP)
    ctx = ExitStack()
    with ctx:
        sb, ps, sem = tools(nc, ctx)
        hf = sb("hf", [P, NT, D], F32)
        hpart = sb("hpart", [P, NT, 3, D], F16)
        slab = sb("slab", [P, 2, NT, P], F16)
        rowsT = sb("rowsT", [P, 2, NP], F32)
        sums = sb("sums", [P, 2, 4, D], F32)
        aggr = sb("aggr", [P, D], F32)
        attr_w = sb("attr_w", [P, RING, K, D], F32)
        rec_w = sb("rec_w", [P, RING, K, 4], F32)
        rel = sb("rel", [P, RING, K, 2], F32)
        base_i = sb("base_i", [P, NG, 2], I32)
        base = sb("base", [P, NG, 2], F32)
        iota_i = sb("iota_i", [P, CODE], I32)
        iota = sb("iota", [P, CODE], F16)
        iota_g = sb("iota_g", [P, QG, QG * G], F32)
        code_oh = sb("code_oh", [P, 2, K, CODE], F16)
        lane_oh = sb("lane_oh", [P, 2, K, P], F16)
        dst_oh = sb("dst_oh", [P, 2, K, QG * G], F32)
        ident16 = sb("ident16", [P, P], F16)
        lane_i = sb("lane_i", [P, 1], I32)
        lane = sb("lane", [P, 1], F32)
        g_rec = sb("g_rec", [P, 4], F32)
        g_src = sb("g_src", [P, 1], I32)
        g_attr = sb("g_attr", [P, D], F32)
        g_h = sb("g_h", [P, D], F32)
        g_rest = sb("g_rest", [P, 2], F32)
        g_keys = sb("g_keys", [P, 2, P], F32)
        g_eq = sb("g_eq", [P, 3, P], F32)
        g_low = sb("g_low", [P, P], F32)
        g_first = sb("g_first", [P, 2, P], F32)
        g_dup = sb("g_dup", [P, 2], F32)
        g_cnt = sb("g_cnt", [P, 1], F32)
        g_tmp = sb("g_tmp", [P, 4], F32)
        g_idx = sb("g_idx", [P, 4], I32)
        g_sum = sb("g_sum", [P, D], F32)
        carrier = sb("carrier", [P, 4], F32)
        grp = ps("grp", [P, 4, 512])
        acc = ps("acc", [P, 2, 512])
        tp = ps("tp", [P, 2, 512])
        h_in, base_ready, set_done, consts = sem("h_in"), sem("base_ready"), sem("set_done"), sem("consts2")
        rec_in = [sem(f"rec_in{s}") for s in range(RING)]
        attr_in = [sem(f"attr_in{s}") for s in range(RING)]
        summed, sum_step, aggr_out = sem("summed"), sem("sum_step"), sem("aggr_out")
        rel_ready, oh_ready, group_done, slab_part = sem("rel_ready"), sem("oh_ready"), sem("group_done"), sem("slab_part")
        grp_ready, set_iota = sem("grp_ready"), sem("set_iota")
        tp_ready, tp_used, rows_ready = sem("tp_ready"), sem("tp_used"), sem("rows_ready")
        rows_out = [sem("rows_out0"), sem("rows_out1")]
        g_zero_out, g_in, g_dve, g_pe, g_idx_ready = sem("g_zero_out"), sem("g_in"), sem("g_dve"), sem("g_pe"), sem("g_idx_ready")
        g_h_in, g_keys_in, g_keysT, g_m_ready, g_summed = sem("g_h_in"), sem("g_keys_in"), sem("g_keysT"), sem("g_m_ready"), sem("g_summed")
        g_padded, g_out, g_zeroed, g_low_ready = sem("g_padded"), sem("g_out"), sem("g_zeroed"), sem("g_low_ready")
        g_carrier = sem("g_carrier")
        block = ctx.enter_context(nc.Block())

        SLICES = [range(13 * gi // GPB, 13 * (gi + 1) // GPB) for gi in range(GPB)]

        def on_pool(gi):
            return gi % 8 in (0, 2, 3, 5, 6)
        FIRST_SLICE = next(gi for gi in range(GPB) if SLICES[gi])

        def tiles_of(batch):
            return range(4 * batch, min(4 * batch + 4, NT))

        def all_blocks(eng, body, last_stage):
            body(0, 0, False)
            with eng.Fori(0, (NT - 1) // 2) as i:
                body(2 * i + 1, 1, True)
                body(2 * i + 2, 0, True)
            last_stage(NT - 1)

        @block.sync
        def _(sp):
            fast = sp.value_load(flag_i[0:1, 0:1], min_val=0, max_val=1)
            with sp.If(fast == 1):
                def windows(b, par, has_stage):
                    for gi in range(GPB):
                        g, slot = b * GPB + gi, gi % RING
                        first = sp.value_load(start_i[0:1, bass.ds(g, 1)], min_val=0, max_val=E - WIN)
                        sp.wait_ge(group_done, g + 1)
                        if not on_pool(gi):
                            sp.dma_start(rec_w[:, slot, :, :].rearrange("p k c -> p (k c)"),
                                         rec_d[bass.ds(first, WIN), :].rearrange("(p k) c -> p (k c)", k=K)
                                         ).then_inc(rec_in[slot], 16)
                        sp.dma_start(attr_w[:, slot, :, :].rearrange("p k c -> p (k c)"),
                                     attr[bass.ds(first, WIN), :].rearrange("(p k) c -> p (k c)", k=K)
                                     ).then_inc(attr_in[slot], 16)
                all_blocks(sp, windows, lambda b: None)
            with sp.Else():
                sp.wait_ge(g_zeroed, 1)
                with sp.Fori(0, NT) as j:
                    sp.dma_start(count_rows[bass.ds(j * P, P), :], rowsT[:, 0, :]).then_inc(g_zero_out, 16)
                    sp.dma_start(aggr_d[bass.ds(j * P, P), :], rowsT[:, 0, 0:D]).then_inc(g_zero_out, 16)
                sp.dma_start(count_d[NP * NP:NP * NP + NP, :].rearrange("(p c) o -> p (c o)", c=NT),
                             rowsT[:, 0, 0:NT]).then_inc(g_zero_out, 16)
                sp.dma_start(aggr_d[NP:NP + P, :], rowsT[:, 0, 0:D]).then_inc(g_zero_out, 16)
                sp.wait_ge(g_zero_out, 16 * (2 * NT + 2))

                def load(t, rows, at):
                    if not isinstance(t, int):
                        sp.wait_ge(g_out, t * 32)
                    sp.dma_start(g_rec[0:rows, :], rec_d[bass.ds(at, rows), :]).then_inc(g_in, 16)
                    sp.dma_start(g_attr[0:rows, :], attr[bass.ds(at, rows), :]).then_inc(g_in, 16)
                load(0, P, 0)
                with sp.Fori(1, GTILES) as t:
                    load(t, P, t * P)
                sp.wait_ge(g_out, GTILES * 32)
                sp.wait_ge(g_padded, 1)
                sp.dma_start(g_rec[0:GREST, :], rec_d[GTILES * P:E, :]).then_inc(g_in, 16)
                sp.dma_start(g_attr[0:GREST, :], attr[GTILES * P:E, :]).then_inc(g_in, 16)

        @block.gpsimd
        def _(pool):
            fast = pool.value_load(flag_i[0:1, 0:1], min_val=0, max_val=1)
            pool.iota(base_i[:, :, 0], pattern=[[CODE, NG]], base=0, channel_multiplier=0).then_inc(base_ready, 1)
            pool.iota(base_i[:, :, 1], pattern=[[G, NG]], base=0, channel_multiplier=0).then_inc(base_ready, 1)
            pool.iota(iota_i[:, :], pattern=[[1, CODE]], base=0, channel_multiplier=0).then_inc(base_ready, 1)
            pool.iota(lane_i[:, :], pattern=[[0, 1]], base=0, channel_multiplier=1).then_inc(base_ready, 1)
            with pool.If(fast == 1):
                pool.nop().then_inc(summed, 2)

                def load(g, slot):
                    first = pool.value_load(start_i[0:1, bass.ds(g, 1)], min_val=0, max_val=E - WIN)
                    pool.wait_ge(group_done, g + 1)
                    pool.dma_start(rec_w[:, slot, :, :].rearrange("p k c -> p (k c)"),
                                   rec_d[bass.ds(first, WIN), :].rearrange("(p k) c -> p (k c)", k=K)
                                   ).then_inc(rec_in[slot], 16)

                def relative(b, par, has_store):
                    for gi in range(GPB):
                        g, slot = b * GPB + gi, gi % RING
                        if on_pool((gi + AHEAD) % GPB) and not (isinstance(b, int) and g + AHEAD >= NG):
                            load(g + AHEAD, (gi + AHEAD) % RING)
                        pool.wait_ge(rec_in[slot], 16 * (GPB // RING * b + gi // RING + 1))
                        pool.tensor_tensor(rel[:, slot, :, :], rec_w[:, slot, :, 0:2],
                                           base[:, bass.ds(g, 1), :].to_broadcast([P, K, 2]),
                                           ALU.subtract).then_inc(rel_ready, 1)
                        if has_store and gi == 6:
                            store(b - 2, par)
                        if has_store and gi == 10:
                            pool.wait_ge(aggr_out, 16 * (b - 1))

                def store(st, par):
                    pool.wait_ge(rows_ready, st + 2)
                    pool.tensor_tensor(aggr[:, :], sums[:, par, 0, :], sums[:, par, 1, :], ALU.add).then_inc(sum_step, 1)
                    pool.wait_ge(sum_step, 2 * st + 1)
                    pool.tensor_tensor(aggr[:, :], aggr[:, :], sums[:, par, 2, :], ALU.add).then_inc(sum_step, 1)
                    pool.wait_ge(sum_step, 2 * st + 2)
                    pool.tensor_tensor(aggr[:, :], aggr[:, :], sums[:, par, 3, :], ALU.add).then_inc(summed, 1)
                    pool.wait_ge(summed, st + 3)
                    pool.dma_start(aggr_d[bass.ds(st * P, P), :], aggr[:, :]).then_inc(aggr_out, 16)
                pool.wait_ge(set_done, 1)
                for g in range(AHEAD):
                    if on_pool(g):
                        load(g, g)
                relative(0, 0, False)
                relative(1, 1, False)
                with pool.Fori(1, (NT - 1) // 2) as i:
                    relative(2 * i, 0, True)
                    relative(2 * i + 1, 1, True)
                relative(NT - 1, 0, True)
                store(NT - 2, 1)
                pool.wait_ge(aggr_out, 16 * (NT - 1))
                store(NT - 1, 0)
                pool.wait_ge(aggr_out, 16 * NT)
            with pool.Else():
                pool.wait_ge(g_low_ready, 1)
                pool.affine_select(out=g_low[:, :], in_=g_low[:, :], compare_op=ALU.is_gt, fill=0.0, base=0,
                                   pattern=[[-1, P]], channel_multiplier=1).then_inc(g_low_ready, 1)

                pool.memset(carrier[:, :], 0.0).then_inc(g_carrier, 1)
                pool.wait_ge(g_carrier, 1)

                def add(t):
                    pool.wait_ge(g_idx_ready, 2 * t + 1)
                    pool.tensor_tensor(carrier[:, 1:2], carrier[:, 0:1], carrier[:, 0:1], ALU.add
                                       ).then_inc(g_carrier, 1)
                    pool.indirect_dma_start(out=g_h[:, :], out_offset=None, in_=h_d,
                                            in_offset=bass.IndirectOffsetOnAxis(ap=g_idx[:, 0:1], axis=0),
                                            ).then_inc(g_h_in, 16)
                    pool.wait_ge(g_idx_ready, 2 * t + 2)
                    pool.tensor_tensor(carrier[:, 2:3], carrier[:, 0:1], carrier[:, 0:1], ALU.add
                                       ).then_inc(g_carrier, 1)
                    pool.indirect_dma_start(out=aggr_d, out_offset=bass.IndirectOffsetOnAxis(ap=g_idx[:, 1:2], axis=0),
                                            in_=g_sum[:, :], in_offset=None, compute_op=ALU.add).then_inc(g_out, 16)
                    pool.indirect_dma_start(out=count_d, out_offset=bass.IndirectOffsetOnAxis(ap=g_idx[:, 2:3], axis=0),
                                            in_=g_cnt[:, :], in_offset=None, compute_op=ALU.add).then_inc(g_out, 16)
                    pool.wait_ge(g_carrier, 2 * t + 3)
                    pool.wait_ge(g_out, (t + 1) * 32)
                with pool.Fori(0, GTILES) as t:
                    add(t)
                add(GTILES)

        @block.vector
        def _(dve):
            link = linker(dve, set_done)
            fast = dve.value_load(flag_i[0:1, 0:1], min_val=0, max_val=1)
            dve.wait_ge(base_ready, 4)
            dve.tensor_copy(base[:, :, :], base_i[:, :, :])
            dve.tensor_copy(iota[:, :], iota_i[:, :])
            dve.memset(iota_g[:, :, :], -1e6).then_inc(set_iota, 1)
            dve.wait_ge(set_iota, 1)
            for q in range(QG):
                dve.tensor_copy(iota_g[:, q, q * G:(q + 1) * G], iota_i[:, 0:G]).then_inc(set_iota, 1)
            dve.tensor_copy(lane[:, :], lane_i[:, :])
            link(dve.tensor_copy(ident16[:, :], ident[:, :]))
            dve.wait_ge(set_iota, QG + 1)
            with dve.If(fast == 1):
                dve.wait_ge(h_in, 16)
                for part in range(2):
                    link(dve.tensor_copy(hpart[:, :, part, :], hf[:, :, :]))
                    link(dve.tensor_tensor(hf[:, :, :], hf[:, :, :], hpart[:, :, part, :], ALU.subtract))
                dve.tensor_copy(hpart[:, :, 2, :], hf[:, :, :]).then_inc(consts, 1)

                def one_hots(b, par, has_stage):
                    for gi in range(GPB):
                        g, slot, s = b * GPB + gi, gi % RING, gi % 2
                        dve.wait_ge(rel_ready, g + 1)
                        dve.wait_ge(group_done, g - 1 + RING)
                        for k in range(K):
                            dve.tensor_scalar(code_oh[:, s, k, :], iota[:, :], rel[:, slot, k, 0:1], None, ALU.is_equal)
                            dve.tensor_scalar(lane_oh[:, s, k, :], iota[:, 0:P], rec_w[:, slot, k, 3:4], None, ALU.is_equal)
                        dve.tensor_tensor(dst_oh[:, s, :, :],
                                          iota_g[:, gi % QG, :].unsqueeze(1).to_broadcast([P, K, QG * G]),
                                          rel[:, slot, :, 1:2].to_broadcast([P, K, QG * G]),
                                          ALU.is_equal).then_inc(oh_ready, 1)
                all_blocks(dve, one_hots, lambda b: None)
            with dve.Else():
                dve.memset(g_low[:, :], 1.0).then_inc(g_low_ready, 1)
                dve.memset(g_rec[:, :], 0.0)
                dve.memset(g_attr[:, :], 0.0)
                dve.memset(rowsT[:, 0, :], 0.0).then_inc(g_zeroed, 1)
                dve.wait_ge(g_zeroed, 1)
                dve.wait_ge(g_low_ready, 2)

                def work(t):
                    steps = [0]

                    def step(ins):
                        steps[0] += 1
                        ins.then_inc(g_dve, 1)
                        dve.wait_ge(g_dve, t * 19 + steps[0])
                    dve.wait_ge(g_in, (t + 1) * 32)
                    step(dve.tensor_copy(g_keys[:, 0, :], g_rec[:, 1:2].to_broadcast([P, P])))
                    dve.tensor_copy(g_keys[:, 1, :], g_rec[:, 2:3].to_broadcast([P, P])).then_inc(g_keys_in, 1)
                    dve.tensor_copy(g_idx[:, 0:1], g_rec[:, 2:3]).then_inc(g_idx_ready, 1)
                    dve.wait_ge(g_keysT, t + 1)
                    step(dve.tensor_scalar(g_eq[:, 0, :], grp[:, 0, 0:P], g_rec[:, 1:2], None, ALU.is_equal))
                    step(dve.tensor_scalar(g_eq[:, 1, :], grp[:, 0, P:2 * P], g_rec[:, 2:3], None, ALU.is_equal))
                    step(dve.tensor_tensor(g_eq[:, 2, :], g_eq[:, 0, :], g_eq[:, 1, :], ALU.mult))
                    step(dve.tensor_reduce(g_cnt[:, :], g_eq[:, 2, :], axis=AX.X, op=ALU.add))
                    step(dve.tensor_tensor(g_first[:, 0, :], g_eq[:, 0, :], g_low[:, :], ALU.mult))
                    step(dve.tensor_tensor(g_first[:, 1, :], g_eq[:, 2, :], g_low[:, :], ALU.mult))
                    step(dve.tensor_reduce(g_dup[:, :], g_first[:, :, :], axis=AX.X, op=ALU.max))
                    step(dve.tensor_scalar(g_tmp[:, 0:1], lane[:, :], float(NP), g_rec[:, 1:2], ALU.add, ALU.subtract))
                    step(dve.tensor_tensor(g_tmp[:, 1:2], g_tmp[:, 0:1], g_dup[:, 0:1], ALU.mult))
                    step(dve.tensor_tensor(g_idx[:, 1:2], g_tmp[:, 1:2], g_rec[:, 1:2], ALU.add))
                    step(dve.tensor_scalar(g_tmp[:, 0:1], g_rec[:, 0:1], -1.0, float(NP * NT), ALU.mult, ALU.add))
                    step(dve.scalar_tensor_tensor(out=g_idx[:, 2:3], in0=g_tmp[:, 0:1], scalar=g_dup[:, 1:2],
                                                  in1=g_rec[:, 0:1], op0=ALU.mult, op1=ALU.add))
                    step(dve.tensor_tensor(g_tmp[:, 2:3], lane[:, :], g_rec[:, 3:4], ALU.subtract))
                    step(dve.scalar_tensor_tensor(out=g_idx[:, 3:4], in0=g_tmp[:, 2:3], scalar=g_dup[:, 1:2],
                                                  in1=g_rec[:, 3:4], op0=ALU.mult, op1=ALU.add))
                    step(dve.tensor_scalar(g_idx[:, 2:3], g_idx[:, 2:3], 7, None, ALU.logical_shift_left))
                    step(dve.tensor_tensor(g_idx[:, 2:3], g_idx[:, 2:3], g_idx[:, 3:4], ALU.bitwise_or))
                    dve.wait_ge(g_h_in, (t + 1) * 16)
                    step(dve.tensor_tensor(g_attr[:, :], g_attr[:, :], g_h[:, :], ALU.add))
                    dve.nop().then_inc(g_m_ready, 1)
                    dve.wait_ge(g_summed, t + 1)
                    step(dve.tensor_copy(g_sum[:, :], acc[:, 0, 0:D]))
                    assert steps[0] == 19
                    dve.nop().then_inc(g_idx_ready, 1)

                def padding(t):
                    dve.wait_ge(g_out, t * 32)
                    dve.memset(g_attr[:, :], 0.0)
                    dve.memset(g_rec[:, 0:1], float(NP * NT - 1))
                    dve.memset(g_rec[:, 1:3], float(NP - 1))
                    dve.memset(g_rec[:, 3:4], float(P - 1)).then_inc(g_padded, 1)

                with dve.Fori(0, GTILES) as t:
                    work(t)
                padding(GTILES)
                work(GTILES)

        @block.scalar
        def _(act):
            fast = act.value_load(flag_i[0:1, 0:1], min_val=0, max_val=1)
            with act.If(fast == 1):
                act.nop().then_inc(tp_used, 2)
                act.nop().then_inc(rows_ready, 1)
                for stored in rows_out:
                    act.nop().then_inc(stored, 16)
                act.dma_start(hf[:, :, :], h_d.rearrange("(t p) f -> p t f", p=P)).then_inc(h_in, 16)

                def store(st, par, batch):
                    if batch % 2 == 0 and batch < 12:
                        return
                    first = batch - batch % 2
                    cols = slice(4 * first * P, (4 * batch + len(tiles_of(batch))) * P)
                    act.wait_ge(tp_used, st * 13 + batch + 3)
                    act.dma_start(count_rows[bass.ds(st * P, P), cols], rowsT[:, par, cols]
                                  ).then_inc(rows_out[par], 16)

                def rows(st, par, batch):
                    tiles = tiles_of(batch)
                    n = st * 13 + batch
                    act.wait_ge(tp_ready, n + 1)
                    act.activation(rowsT[:, par, 4 * batch * P:(4 * batch + len(tiles)) * P],
                                   tp[:, batch % 2 if par == 0 else (batch + 1) % 2, 0:len(tiles) * P],
                                   ACT.Copy).then_inc(tp_used, 1)

                def finish(st, par):
                    act.wait_ge(tp_ready, (st + 1) * 13)
                    act.wait_ge(summed, st + 1)
                    act.activation(sums[:, par, :, :].rearrange("p a f -> p (a f)"), acc[:, par, 0:4 * D],
                                   ACT.Copy).then_inc(rows_ready, 1)

                def copies(b, par, has_stage):
                    for gi in range(GPB):
                        g = b * GPB + gi
                        act.wait_ge(grp_ready, g + 1)
                        act.activation(slab[:, par, :, gi * G:(gi + 1) * G].rearrange("p t d -> p d t"),
                                       grp[:, gi % 4, 0:CODE].rearrange("p (d t) -> p d t", t=NT),
                                       ACT.Copy).then_inc(slab_part, 1)
                        if has_stage:
                            if gi == 0:
                                act.wait_ge(rows_out[1 - par], 8 * 7 * (b - 1 - (1 - par)) + 16)
                            for batch in SLICES[gi]:
                                rows(b - 1, 1 - par, batch)
                                store(b - 1, 1 - par, batch)
                    if has_stage:
                        finish(b - 1, 1 - par)

                def last(st):
                    act.wait_ge(rows_out[0], 16 * 7 * (st // 2) + 16)
                    for batch in range(13):
                        rows(st, 0, batch)
                        store(st, 0, batch)
                    finish(st, 0)
                all_blocks(act, copies, last)
                act.wait_ge(rows_out[0], 16 * 7 * ((NT + 1) // 2) + 16)
                act.wait_ge(rows_out[1], 16 * 7 * ((NT - 1) // 2) + 16)
            with act.Else():
                act.nop()

        @block.tensor
        def _(pe):
            fast = pe.value_load(flag_i[0:1, 0:1], min_val=0, max_val=1)
            pe.wait_ge(set_done, 1)
            with pe.If(fast == 1):
                pe.nop().then_inc(group_done, RING)
                pe.wait_ge(consts, 1)

                def turn(st, par, batch):
                    n = st * 13 + batch
                    pe.wait_ge(tp_used, n + 1)
                    tiles = tiles_of(batch)
                    bank = batch % 2 if par == 0 else (batch + 1) % 2
                    for j, t in enumerate(tiles):
                        pe.matmul(acc[:, par, 0:3 * D], slab[:, par, t, :],
                                  hpart[:, t, :, :].rearrange("p a f -> p (a f)"),
                                  start=(t == 0), stop=(t == NT - 1), skip_group_check=True)
                        last = pe.matmul(tp[:, bank, j * P:(j + 1) * P], slab[:, par, t, :], ident16[:, :],
                                         start=True, stop=True)
                    last.then_inc(tp_ready, 1)

                def products(b, par, has_stage):
                    for gi in range(GPB):
                        g, slot, s = b * GPB + gi, gi % RING, gi % 2
                        pe.wait_ge(oh_ready, g + 1)
                        if gi >= 4 or has_stage:
                            pe.wait_ge(slab_part, g - 3)
                        for k in range(K):
                            last = pe.matmul(grp[:, gi % 4, 0:CODE], lane_oh[:, s, k, :], code_oh[:, s, k, :],
                                             start=(k == 0), stop=(k == K - 1))
                        last.then_inc(grp_ready, 1)
                        if gi == 0 and has_stage:
                            pe.wait_ge(rows_ready, b)
                        pe.wait_ge(attr_in[slot], 16 * (GPB // RING * b + gi // RING + 1))
                        rows32 = slice(gi // QG * 32, gi // QG * 32 + 32)
                        for k in range(K):
                            last = pe.matmul(acc[rows32, par, 3 * D:4 * D], dst_oh[:, s, k, :], attr_w[:, slot, k, :],
                                             start=(gi % QG == 0 and k == 0), stop=(gi % QG == QG - 1 and k == K - 1),
                                             skip_group_check=True)
                        last.then_inc(group_done, 1)
                        if has_stage:
                            if gi == FIRST_SLICE:
                                pe.wait_ge(slab_part, b * GPB)
                            for batch in SLICES[gi]:
                                turn(b - 1, 1 - par, batch)

                def last_stage(st):
                    pe.wait_ge(slab_part, NG)
                    for batch in range(13):
                        turn(st, 0, batch)
                all_blocks(pe, products, last_stage)
            with pe.Else():
                def match(t):
                    pe.wait_ge(g_keys_in, t + 1)
                    for c in range(2):
                        last = pe.matmul(grp[:, 0, c * P:(c + 1) * P], g_keys[:, c, :], ident[:, :],
                                         start=True, stop=True)
                    last.then_inc(g_keysT, 1)
                    pe.wait_ge(g_m_ready, t + 1)
                    pe.matmul(acc[:, 0, 0:D], g_eq[:, 0, :], g_attr[:, :], start=True, stop=True).then_inc(g_summed, 1)
                with pe.Fori(0, GTILES) as t:
                    match(t)
                match(GTILES)


def nodes(nc, xp_d, W1, b1, W2, b2, eps, qW, kW, vW, h_d, aggr_d, xh_d, parts_d, kb, qp_d, vb, ident, ones):
    ctx = ExitStack()
    W = SC * P
    with ctx:
        sb, ps, sem = tools(nc, ctx)
        w1 = sb("w1", [D, HID], F32)
        w2 = sb("w2", [D, 2, D], F32)
        b1c = sb("b1c", [D, 2], F32)
        b2r = sb("b2r", [1, D], F32)
        qkv = sb("qkv", [D, 3, D], F32)
        eps1 = sb("eps1", [P, 1], F32)
        xt = sb("xt", [P, SC, D], F32)
        ht = sb("ht", [P, SC, D], F32)
        at = sb("at2", [P, SC, D], F32)
        aT = sb("aT", [D, W], F32)
        hid = sb("hid", [D, 2, W], F32)
        x1 = sb("x1", [P, SC, D], F32)
        cen = sb("cen", [P, SC, D], F32)
        sq = sb("sq2", [P, SC, D], F32)
        xh = sb("xh", [P, SC, D], F32)
        mean = sb("mean2", [P, SC], F32)
        rstd = sb("rstd2", [P, SC], F32)
        h2T = sb("h2T", [D, W], F32)
        parts = sb("parts", [D, 2, 3, W], BF16)
        qk = sb("qk", [D, 2, W], F32)
        pa = ps("pa", [D, 2, 512])
        pb = ps("pb", [D, 2, 512])
        pm = ps("pm", [P, 2, 4, P])
        pt = ps("pt", [D, 2, 512])
        w_in, in_s = sem("w_in"), sem("in_s")
        hid_p, hid_s, mlp_p, var_s, std_s = sem("hid_p"), sem("hid_s"), sem("mlp_p"), sem("var_s"), sem("std_s")
        h2_s, h2T_p, h2T_s, q_p, k_p, v_p = sem("h2_s"), sem("h2T_p"), sem("h2T_s"), sem("q_p"), sem("k_p"), sem("v_p")
        v_s, parts_s, xh_s, step_s = sem("v_s"), sem("parts_s"), sem("xh_s"), sem("step_s")
        sp_out, pool_out, vb_set = sem("sp_out"), sem("pool_out"), sem("vb_set")
        qk_s = sem("qk_s")
        x1_s, aT_p, aT_s, packed = sem("x1_s"), sem("aT_p"), sem("aT_s"), [sem("q_packed"), sem("k_packed")]
        NSP, NPOOL = 1, 2
        block = ctx.enter_context(nc.Block())
        halves = ((0, 4), (4, 3))

        def pack(eng, s, which):
            cols = bass.ds((s - 1) * W if isinstance(s, int) else eng.snap((s - 1) * W), W)
            eng.wait_ge(pool_out, 16 * NPOOL * s)
            for m in range(2):
                for slot, pair in enumerate(PAIRS[m]):
                    part = pair[1 - which]
                    eng.dma_start((qp_d, kb)[which][m][slot * DH:(slot + 1) * DH, :, cols],
                                  parts_d[which, :, part, cols].rearrange("(h r) n -> r h n", h=HEADS)
                                  ).then_inc(packed[which], 16)

        @block.sync
        def _(sp):
            sp.dma_start(w1[:, :], W1).then_inc(w_in, 16)
            sp.dma_start(w2[:, :, :], W2.rearrange("(a p) n -> p a n", a=2)).then_inc(w_in, 16)
            with nc.allow_non_contiguous_dma(reason="192 numbers"):
                sp.dma_start(b1c[:, :], b1.rearrange("(a p) -> p a", a=2)).then_inc(w_in, 16)
            sp.dma_start(b2r[:, :], b2.rearrange("(a n) -> a n", a=1)).then_inc(w_in, 16)
            for n, w in enumerate((qW, kW, vW)):
                sp.dma_start(qkv[:, n, :], w).then_inc(w_in, 16)
            sp.dma_start(eps1[:, :], eps.rearrange("(a n) -> a n", a=1).to_broadcast([P, 1])).then_inc(w_in, 16)

            def load(s):
                rows = bass.ds(s * W if isinstance(s, int) else sp.snap(s * W), W)
                if not isinstance(s, int):
                    sp.wait_ge(x1_s, s)
                sp.dma_start(xt[:, :, :], xp_d[rows, :].rearrange("(t p) f -> p t f", p=P)).then_inc(in_s, 16)
                sp.dma_start(ht[:, :, :], h_d[rows, :].rearrange("(t p) f -> p t f", p=P)).then_inc(in_s, 16)
                sp.dma_start(at[:, :, :], aggr_d[rows, :].rearrange("(t p) f -> p t f", p=P)).then_inc(in_s, 16)
            load(0)
            with sp.Fori(1, NS) as s:
                load(s)
                pack(sp, s, 0)
            pack(sp, NS, 0)
            sp.wait_ge(packed[0], 16 * 9 * NS)

        @block.gpsimd
        def _(pool):
            pool.memset(vb[:, :, :, :], 0.0).then_inc(vb_set, 1)
            pool.wait_ge(vb_set, 1)
            pool.memset(vb[:, :, :, DH:DH + 1], 1.0).then_inc(vb_set, 1)

            def store(s):
                rows = bass.ds(s * W if isinstance(s, int) else pool.snap(s * W), W)
                pool.wait_ge(xh_s, s + 1)
                pool.dma_start(xh_d[rows, :].rearrange("(t p) f -> p t f", p=P), xh[:, :, :]).then_inc(sp_out, 16)
                for i in range(2):
                    pool.wait_ge(parts_s, 2 * s + i + 3)
                    pool.dma_start(parts_d[i, :, :, rows], parts[:, i, :, :]).then_inc(pool_out, 16)
            store(0)
            with pool.Fori(1, NS) as s:
                pack(pool, s, 1)
                store(s)
            pack(pool, NS, 1)
            pool.wait_ge(sp_out, 16 * NSP * NS)
            pool.wait_ge(packed[1], 16 * 9 * NS)

        @block.tensor
        def _(pe):
            pe.wait_ge(w_in, 128)
            with pe.Fori(0, NS) as s:
                pe.wait_ge(in_s, 48 * (s + 1))
                for c, (first, n) in enumerate(halves):
                    for j in range(n):
                        last = pe.transpose(pt[:, c, j * P:(j + 1) * P], at[:, first + j, :], ident[:, :])
                    last.then_inc(aT_p, 1)
                pe.wait_ge(qk_s, 2 * s + 2)
                pe.wait_ge(aT_s, 2 * (s + 1))
                for a, bank in enumerate((pa, pb)):
                    for c in range(2):
                        pe.matmul(bank[:, c, 0:CW], w1[:, a * D:(a + 1) * D], aT[:, c * CW:(c + 1) * CW],
                                  start=True, stop=True).then_inc(hid_p, 1)
                pe.wait_ge(hid_s, 4 * (s + 1))
                pe.wait_ge(v_s, 2 * s + 2)
                for c, (first, n) in enumerate(halves):
                    for j in range(n):
                        o, t = pm[:, c, j, 0:D], first + j
                        pe.matmul(o, ones[0:1, :], b2r[:, :], start=True, stop=False)
                        pe.matmul(o, hid[:, 0, t * P:(t + 1) * P], w2[:, 0, :], start=False, stop=False)
                        last = pe.matmul(o, hid[:, 1, t * P:(t + 1) * P], w2[:, 1, :], start=False, stop=True)
                    last.then_inc(mlp_p, 1)
                pe.wait_ge(h2_s, s + 1)
                for c, (first, n) in enumerate(halves):
                    for j in range(n):
                        last = pe.transpose(pt[:, c, j * P:(j + 1) * P], cen[:, first + j, :], ident[:, :])
                    last.then_inc(h2T_p, 1)
                pe.wait_ge(h2T_s, 2 * (s + 1))
                for n, (bank, done) in enumerate(((pa, q_p), (pb, k_p))):
                    for c in range(2):
                        last = pe.matmul(bank[:, c, 0:CW], qkv[:, n, :], h2T[:, c * CW:(c + 1) * CW],
                                         start=True, stop=True)
                    last.then_inc(done, 1)
                for c, (first, n) in enumerate(halves):
                    for j in range(n):
                        last = pe.matmul(pm[:, c, j, 0:D], h2T[:, (first + j) * P:(first + j + 1) * P],
                                         qkv[:, 2, :], start=True, stop=True)
                    last.then_inc(v_p, 1)

        @block.scalar
        def _(act):
            act.nop().then_inc(v_s, 2)
            act.nop().then_inc(qk_s, 2)
            act.wait_ge(w_in, 128)
            act.wait_ge(vb_set, 2)
            with act.Fori(0, NS) as s:
                for c, (first, n) in enumerate(halves):
                    act.wait_ge(aT_p, 2 * s + c + 1)
                    act.activation(aT[:, first * P:(first + n) * P], pt[:, c, 0:n * P], ACT.Copy).then_inc(aT_s, 1)
                for a, bank in enumerate((pa, pb)):
                    for c in range(2):
                        act.wait_ge(hid_p, 4 * s + 2 * a + c + 1)
                        act.activation(hid[:, a, c * CW:(c + 1) * CW], bank[:, c, 0:CW], ACT.Relu,
                                       bias=b1c[:, a:a + 1]).then_inc(hid_s, 1)
                act.wait_ge(var_s, s + 1)
                act.activation(rstd[:, :], rstd[:, :], ACT.Sqrt).then_inc(std_s, 1)
                for c, (first, n) in enumerate(halves):
                    act.wait_ge(h2T_p, 2 * s + c + 1)
                    act.activation(h2T[:, first * P:(first + n) * P], pt[:, c, 0:n * P], ACT.Copy).then_inc(h2T_s, 1)
                act.wait_ge(parts_s, 2 * s + 2)
                for i, (bank, done) in enumerate(((pa, q_p), (pb, k_p))):
                    act.wait_ge(done, s + 1)
                    act.activation(qk[:, i, :].rearrange("p (c n) -> p c n", c=2), bank[:, :, 0:CW],
                                   ACT.Copy).then_inc(qk_s, 1)
                for c, (first, n) in enumerate(halves):
                    act.wait_ge(v_p, 2 * s + c + 1)
                    act.activation(vb[:, bass.ds(s * SC + first, n), :, 0:DH],
                                   pm[:, c, 0:n, 0:D].rearrange("p t (h d) -> p t h d", h=HEADS),
                                   ACT.Copy).then_inc(v_s, 1)

        @block.vector
        def _(dve):
            dve.wait_ge(w_in, 128)
            dve.tensor_scalar(eps1[:, :], eps1[:, :], 1.0, None, ALU.add).then_inc(step_s, 1)
            dve.nop().then_inc(parts_s, 2)
            dve.wait_ge(step_s, 1)

            def superchunk(s):
                STEPS = 17
                n = [0]

                def step(ins):
                    n[0] += 1
                    ins.then_inc(step_s, 1)
                    dve.wait_ge(step_s, STEPS * s + n[0] + 1)
                dve.wait_ge(in_s, 48 * (s + 1))
                dve.wait_ge(mlp_p, 2 * (s + 1))
                for c, (first, m) in enumerate(halves):
                    step(dve.scalar_tensor_tensor(out=x1[:, first:first + m, :], in0=ht[:, first:first + m, :],
                                                  scalar=eps1[:, 0:1], in1=pm[:, c, 0:m, 0:D],
                                                  op0=ALU.mult, op1=ALU.add))
                dve.tensor_tensor(x1[:, :, :], x1[:, :, :], xt[:, :, :], ALU.add).then_inc(x1_s, 1)
                dve.wait_ge(x1_s, s + 1)
                step(dve.tensor_reduce(mean[:, :], x1[:, :, :], axis=AX.X, op=ALU.add))
                step(dve.tensor_scalar(mean[:, :], mean[:, :], 1.0 / D, None, ALU.mult))
                step(dve.tensor_tensor(cen[:, :, :], x1[:, :, :], mean[:, :].unsqueeze(2).to_broadcast([P, SC, D]),
                                       ALU.subtract))
                step(dve.tensor_tensor(sq[:, :, :], cen[:, :, :], cen[:, :, :], ALU.mult))
                step(dve.tensor_reduce(rstd[:, :], sq[:, :, :], axis=AX.X, op=ALU.add))
                dve.tensor_scalar(rstd[:, :], rstd[:, :], 1.0 / D, LN_EPS, ALU.mult, ALU.add).then_inc(var_s, 1)
                dve.wait_ge(std_s, s + 1)
                step(dve.reciprocal(rstd[:, :], rstd[:, :]))
                step(dve.tensor_tensor(cen[:, :, :], cen[:, :, :],
                                       rstd[:, :].unsqueeze(2).to_broadcast([P, SC, D]), ALU.mult))
                dve.tensor_scalar(cen[:, :, :], cen[:, :, :], 0.0, None, ALU.max).then_inc(h2_s, 1)
                dve.wait_ge(h2_s, s + 1)
                if not isinstance(s, int):
                    dve.wait_ge(sp_out, 16 * NSP * s)
                    dve.wait_ge(pool_out, 16 * NPOOL * s)
                dve.tensor_tensor(xh[:, :, :], x1[:, :, :], cen[:, :, :], ALU.add).then_inc(xh_s, 1)
                for i in range(2):
                    dve.wait_ge(qk_s, 2 * s + i + 3)
                    for part in range(2):
                        step(dve.tensor_copy(parts[:, i, part, :], qk[:, i, :]))
                        step(dve.tensor_tensor(qk[:, i, :], qk[:, i, :], parts[:, i, part, :], ALU.subtract))
                    dve.tensor_copy(parts[:, i, 2, :], qk[:, i, :]).then_inc(parts_s, 1)
                assert n[0] == STEPS, n
            superchunk(0)
            with dve.Fori(1, NS) as s:
                superchunk(s)


def attention(nc, count_d, xh_d, kb, qp_d, vb, ident, out):
    ctx = ExitStack()
    LAG = 3
    C = 7
    assert NT % C == 0
    R = 4
    assert NT % R == 1
    CREDIT = R
    with ctx:
        sb, ps, sem = tools(nc, ctx)
        cnt = sb("counts", [P, C, CW], F32)
        qb = [sb(f"qb{m}", [ROWS[m], 2, HEADS, CW], BF16) for m in range(2)]
        wa = sb("wa", [P, R + 1, 2, CW], F32)
        wb = sb("wb", [P, R + 1, 2, CW], F32)
        ten = sb("ten", [P, 1], F32)
        accs = sb("accs", [P, CW], F32)
        xh = sb("xh3", [CT, 4, D], F32)
        den = sb("den", [CT, 4, HEADS, 1], F32)
        res = sb("res", [CT, 4, HEADS, DH], F32)
        sc = ps("sc", [P, 3, 2, 512])
        acc = ps("acc3", [P, 2, 512])
        q_in, xh_in = sem("q_in"), sem("xh_in")
        t_in = [sem(f"t_in{s}") for s in range(C)]
        sc_a, sc_b, clip_a = sem("sc_a"), sem("sc_b"), sem("clip_a")
        clip_b, clip_v = sem("clip_b"), sem("clip_v")
        exp_a, exp_b, w_a, w_b, pv_done = sem("exp_a"), sem("exp_b"), sem("w_a"), sem("w_b"), sem("pv_done")
        ten_set, acc_out, tq_ready, den_s, o_ready, o_out = (sem(n) for n in (
            "ten_set", "acc_out", "tq_ready", "den_s", "o_ready", "o_out"))
        rows = count_d[0:NP * NP, :].rearrange("(r c) o -> r (c o)", c=NP)
        block = ctx.enter_context(nc.Block())

        def vector_clips(t):
            return t % 3 == 2

        def clipped_b(eng, c, t):
            in_chunk = [u for u in range(NT) if vector_clips(u) == vector_clips(t)]
            eng.wait_ge(clip_v if vector_clips(t) else clip_b, c * len(in_chunk) + in_chunk.index(t) + 1)

        def ring(t):
            return R if t == NT - 1 else t % R

        def counted(eng, c, t):
            eng.wait_ge(t_in[t % C], 16 * (NT // C) * c + 16 * (t // C + 1))

        def all_chunks(eng, chunk, end):
            chunk(0, 0, False)
            with eng.Fori(0, NC_ // 2 - 1) as i:
                chunk(2 * i + 1, 1, True)
                chunk(2 * i + 2, 0, True)
            chunk(NC_ - 1, 1, True)
            end(NC_ - 1, 1)

        @block.sync
        def _(sp):
            def chunk(c, par, after):
                cols = bass.ds(c * CW if isinstance(c, int) else sp.snap(c * CW), CW)
                if after:
                    sp.wait_ge(sc_a, (c - 1) * NT)
                    sp.wait_ge(sc_b, (c - 1) * NT)
                for m in range(2):
                    sp.dma_start(qb[m][:, par, :, :], qp_d[m][:, :, cols]).then_inc(q_in, 16)
                for t in [1, 0] + list(range(2, NT)):
                    n = c * NT + t
                    if t >= C or after and t > 0:
                        sp.wait_ge(w_a, n - C + 1)
                        sp.wait_ge(w_b, n - C + 1)
                    sp.dma_start(cnt[:, t % C, :], rows[t * P:(t + 1) * P, cols]).then_inc(t_in[t % C], 16)
                    if t == 3 * C:
                        if after:
                            store(c - 1, CT)
                        sp.dma_start(xh[:, :, :], xh_d[cols, :].rearrange("(t p) f -> p t f", p=CT)
                                     ).then_inc(xh_in, 16)

            def store(c, last):
                sp.wait_ge(o_ready, c + 1)
                res3 = res[:, :, :, :].rearrange("p t h d -> p t (h d)")
                if last == CT:
                    sp.dma_start(out[bass.ds(c * CW, CW), :].rearrange("(t p) f -> p t f", p=CT),
                                 res3).then_inc(o_out, 16)
                    sp.wait_ge(o_out, 16 * (c + 1))
                else:
                    sp.dma_start(out[c * CW:c * CW + 3 * CT, :].rearrange("(t p) f -> p t f", p=CT),
                                 res3[:, 0:3, :]).then_inc(o_out, 16)
                    sp.dma_start(out[c * CW + 3 * CT:N, :], res3[0:last, 3, :]).then_inc(o_out, 16)
                    sp.wait_ge(o_out, 16 * (c + 2))
            all_chunks(sp, chunk, lambda c, par: store(c, N - c * CW - 3 * CT))

        @block.tensor
        def _(pe):
            pe.nop().then_inc(pv_done, CREDIT)
            pe.nop().then_inc(tq_ready, 1)

            def scores(t, par, pair, done):
                for h in range(2):
                    for m in range(2):
                        last = pe.matmul(sc[:, (2 * t + pair) % 3, h, 0:CW],
                                         kb[m][:, 2 * pair + h, t * P:(t + 1) * P],
                                         qb[m][:, par, 2 * pair + h, :], start=(m == 0), stop=(m == 1))
                last.then_inc(done, 1)

            def weigh(c, par, t):
                for pair, w, ready in ((1, wb, w_b), (0, wa, w_a)):
                    pe.wait_ge(ready, c * NT + t + 1)
                    for h in range(2):
                        q = 2 * pair + h
                        last = pe.matmul(acc[32 * q:32 * q + 32, par, 0:CW], vb[:, t, q, :],
                                         w[:, ring(t), h, :], start=(t == 0), stop=(t == NT - 1))
                last.then_inc(pv_done, 1)

            def turn(c, par):
                pe.wait_ge(acc_out, c + 1)
                for i in range(4):
                    last = pe.transpose(acc[0:CT, par, i * P:(i + 1) * P], accs[:, i * CT:(i + 1) * CT],
                                        ident[:, :])
                last.then_inc(tq_ready, 1)

            def chunk(c, par, after):
                pe.wait_ge(q_in, 32 * (c + 1))
                for t in range(NT):
                    n = c * NT + t
                    if t == 0 and after:
                        pe.wait_ge(clip_a, n)
                    if t >= 2:
                        clipped_b(pe, c, t - 2)
                    elif t == 1 and after:
                        clipped_b(pe, c - 1, NT - 2)
                    scores(t, par, 0, sc_a)
                    if t == 0 and after:
                        clipped_b(pe, c - 1, NT - 1)
                    if t >= 1:
                        pe.wait_ge(clip_a, n)
                    scores(t, par, 1, sc_b)
                    if t >= LAG:
                        if t == LAG and after:
                            pe.wait_ge(den_s, 3 * c)
                        weigh(c, par, t - LAG)
                    elif after:
                        weigh(c - 1, 1 - par, NT - LAG + t)
                    if t == LAG + 2 and after:
                        turn(c - 1, 1 - par)

            def end(c, par):
                for t in range(NT - LAG, NT):
                    weigh(c, par, t)
                turn(c, par)
            all_chunks(pe, chunk, end)

        @block.scalar
        def _(act):
            act.wait_ge(ten_set, 1)

            def chunk(c, par, after):
                for t in range(NT):
                    n, r = c * NT + t, ring(t)
                    if not vector_clips(t):
                        act.wait_ge(sc_b, n + 1)
                        act.wait_ge(pv_done, n - R + 1 + CREDIT)
                        act.activation(wb[:, r, :, :], sc[:, (2 * t + 1) % 3, :, 0:CW], ACT.Relu,
                                       bias=ten[:, 0:1], scale=-1.0).then_inc(clip_b, 1)
                        clipped_b(act, c, t)
                        act.activation(wb[:, r, :, :], wb[:, r, :, :], ACT.Exp,
                                       bias=ten[:, 0:1], scale=-1.0).then_inc(exp_b, 1)
                    act.wait_ge(clip_a, n + 1)
                    act.activation(wa[:, r, :, :], wa[:, r, :, :], ACT.Exp).then_inc(exp_a, 1)
                    if vector_clips(t):
                        clipped_b(act, c, t)
                        act.activation(wb[:, r, :, :], wb[:, r, :, :], ACT.Exp).then_inc(exp_b, 1)
            all_chunks(act, chunk, lambda c, par: None)

        @block.gpsimd
        def _(pool):
            pool.memset(ten[:, :], CLIP).then_inc(ten_set, 1)

            def add(c):
                pool.wait_ge(den_s, 3 * c + 6)
                pool.wait_ge(xh_in, 16 * (c + 1))
                pool.tensor_tensor(res[:, :, :, :], res[:, :, :, :],
                                   xh[:, :, :].rearrange("p t (h d) -> p t h d", h=HEADS), ALU.add).then_inc(o_ready, 1)

            def chunk(c, par, after):
                for t in range(NT):
                    n, r = c * NT + t, ring(t)
                    counted(pool, c, t)
                    pool.wait_ge(exp_a, n + 1)
                    pool.tensor_tensor(wa[:, r, :, :], wa[:, r, :, :],
                                       cnt[:, t % C, :].unsqueeze(1).to_broadcast([P, 2, CW]),
                                       ALU.mult).then_inc(w_a, 1)
                    if t == LAG + 7 and after:
                        add(c - 1)
            all_chunks(pool, chunk, lambda c, par: add(c))

        @block.vector
        def _(dve):
            dve.nop().then_inc(den_s, 3)

            def weights(c, t):
                counted(dve, c, t)
                dve.wait_ge(exp_b, c * NT + t + 1)
                dve.scalar_tensor_tensor(out=wb[:, ring(t), :, :], in0=wb[:, ring(t), :, :], scalar=EXP_LO,
                                         in1=cnt[:, t % C, :].unsqueeze(1).to_broadcast([P, 2, CW]),
                                         op0=ALU.max, op1=ALU.mult).then_inc(w_b, 1)

            def take(c, par):
                dve.wait_ge(pv_done, (c + 1) * NT + CREDIT)
                dve.wait_ge(tq_ready, c + 1)
                dve.tensor_copy(accs[:, :], acc[:, par, 0:CW]).then_inc(acc_out, 1)

            def divide(c, par):
                dve.wait_ge(tq_ready, c + 2)
                num = acc[0:CT, par, :].rearrange("p (t h d) -> p t h d", t=4, h=HEADS)
                dve.tensor_scalar(den[:, :, :, :], num[:, :, :, DH:DH + 1], 1e-8, None, ALU.add).then_inc(den_s, 1)
                dve.wait_ge(den_s, 3 * c + 4)
                dve.reciprocal(den[:, :, :, :], den[:, :, :, :]).then_inc(den_s, 1)
                dve.wait_ge(den_s, 3 * c + 5)
                dve.wait_ge(xh_in, 16 * (c + 1))
                dve.tensor_tensor(res[:, :, :, :], num[:, :, :, 0:DH],
                                  den[:, :, :, :].to_broadcast([CT, 4, HEADS, DH]), ALU.mult).then_inc(den_s, 1)

            def chunk(c, par, after):
                for t in range(NT):
                    n, r = c * NT + t, ring(t)
                    dve.wait_ge(sc_a, n + 1)
                    dve.wait_ge(pv_done, n - R + 1 + CREDIT)
                    dve.tensor_scalar(wa[:, r, :, :], sc[:, (2 * t) % 3, :, 0:CW], CLIP, -CLIP,
                                      ALU.min, ALU.max).then_inc(clip_a, 1)
                    if vector_clips(t):
                        dve.wait_ge(sc_b, n + 1)
                        dve.tensor_scalar(wb[:, r, :, :], sc[:, (2 * t + 1) % 3, :, 0:CW], CLIP, -CLIP,
                                          ALU.min, ALU.max).then_inc(clip_v, 1)
                    if t >= 1:
                        weights(c, t - 1)
                    elif after:
                        weights(c - 1, NT - 1)
                    if after and t == LAG:
                        take(c - 1, 1 - par)
                    if after and t == LAG + 4:
                        divide(c - 1, 1 - par)

            def end(c, par):
                weights(c, NT - 1)
                take(c, par)
                divide(c, par)
            all_chunks(dve, chunk, end)


_INS = ["x", "src", "dst", "edge_attr_96", "L0_gnn_W1", "L0_gnn_b1", "L0_gnn_W2", "L0_gnn_b2", "L0_gnn_eps",
        "L1_gnn_qW", "L1_gnn_kW", "L1_gnn_vW"]


def kernel(**inputs):
    import numpy as _np
    import concourse.bacc as _bacc
    from concourse import mybir as _mybir
    from concourse.bass_utils import run_bass_kernel_spmd as _run

    nc = _bacc.Bacc("TRN2", target_bir_lowering=False, num_devices=1)
    arrays, args = {}, []
    for name in _INS:
        a = _np.ascontiguousarray(inputs[name])
        arrays[f"in_{name}"] = a
        args.append(nc.dram_tensor(f"in_{name}", a.shape, _mybir.dt.from_np(a.dtype), kind="ExternalInput").ap())
    args.append(nc.dram_tensor("out_x", (N, D), _mybir.dt.float32, kind="ExternalOutput").ap())
    build(nc, *args)
    r = _run(nc, [arrays], core_ids=[0])
    return r.results[0]["out_x"]
```
